# Optimizing a Trainium2 kernel written in Bass

```python
import numpy as np
import jax
import jax.numpy as jnp

def _softmax(x, axis=-1):
    return jax.nn.softmax(x, axis=axis)

def _gelu(x):
    return jax.nn.gelu(x, approximate=True)

def _silu(x):
    return jax.nn.silu(x)

def _sigmoid(x):
    return jax.nn.sigmoid(x)

def _layernorm(x, axis=-1, eps=1e-05):
    m = jnp.mean(x, axis=axis, keepdims=True)
    v = jnp.var(x, axis=axis, keepdims=True)
    return (x - m) / jnp.sqrt(v + eps)

def _scatter_add(tgt, idx, src, axis=0):
    return tgt.at[idx].add(src)

def _segment_sum(src, seg, n):
    return jax.ops.segment_sum(src, seg, n)
kernel_name = 'mk_flamingo_gated_d1_seqx_r4_15d10f'

def setup_inputs(seed: int=0):
    np.random.seed(seed)
    _w = jnp.asarray

    def _rec_inputs():
        import jax
        import jax.numpy as jnp
        _rk = jax.random.key(seed)
        x = -0.0005207 + 1.001 * jax.random.normal(jax.random.fold_in(_rk, 1), (8, 100, 1024), jnp.float32)
        _lenS = 100 - jax.random.randint(jax.random.fold_in(_rk, 7), (8,), 0, max(1, 100 // 4) + 1, jnp.int32)
        _lenS2 = 361 - jax.random.randint(jax.random.fold_in(_rk, 8), (8,), 0, max(1, 361 // 4) + 1, jnp.int32)
        _ctx_4096P = jax.random.normal(jax.random.fold_in(_rk, 11), (8, 16, 1024), jnp.float32)
        _ctx_4096c = jax.random.dirichlet(jax.random.fold_in(_rk, 511), 0.3 * jnp.ones((16,), jnp.float32), (8, 361))
        _ctx_4096t = jnp.einsum('bsk,bkd->bsd', _ctx_4096c, _ctx_4096P)
        _ctx_4096t = _ctx_4096t * jax.lax.rsqrt(jnp.mean(jnp.square(_ctx_4096t)) + 1e-12) * 0.953939
        ctx_4096 = -0.00010331 + 0.999899 * (_ctx_4096t + 0.3 * jax.random.normal(jax.random.fold_in(_rk, 611), (8, 361, 1024), jnp.float32))
        _g = jax.random.normal(jax.random.fold_in(_rk, 9001), (2, 1), jnp.float32)
        _g = jnp.sign(_g) * jnp.maximum(jnp.abs(_g), 1.0) + (_g == 0) * 1.0
        g_xattn = _g[0]
        g_ffn = _g[1]
        return (x, ctx_4096, g_xattn, g_ffn)
    x, ctx_4096, g_xattn, g_ffn = _rec_inputs()

    def _L0_xattn_setup():
        import jax, jax.numpy as jnp
        import numpy as np
        HEADS = 32
        KV_HEADS = 8
        HEAD_DIM = 128
        EPS = 1e-06

        def rms_norm(x, w):
            var = jnp.mean(jnp.square(x.astype(jnp.float32)), axis=-1, keepdims=True)
            return (x.astype(jnp.float32) * jax.lax.rsqrt(var + EPS)).astype(x.dtype) * w
        key = jax.random.key(seed)
        ks = jax.random.split(key, 6)
        bsz, n_lat, seq, hidden = (8, 64, 1024, 1024)
        return {'latents': jax.random.normal(ks[0], (bsz, n_lat, hidden), jnp.float32), 'context': jax.random.normal(ks[1], (bsz, seq, hidden), jnp.float32), 'Wq': jax.random.normal(ks[2], (hidden, HEADS * HEAD_DIM), jnp.float32) * 0.02, 'Wk': jax.random.normal(ks[3], (hidden, KV_HEADS * HEAD_DIM), jnp.float32) * 0.02, 'Wv': jax.random.normal(ks[4], (hidden, KV_HEADS * HEAD_DIM), jnp.float32) * 0.02, 'Wo': jax.random.normal(ks[5], (HEADS * HEAD_DIM, hidden), jnp.float32) * 0.02, 'q_norm_w': jnp.ones((HEAD_DIM,), jnp.float32), 'k_norm_w': jnp.ones((HEAD_DIM,), jnp.float32)}
    _L0_xattn_all = _L0_xattn_setup()
    _L0_xattn_in = {k: v for k, v in _L0_xattn_all.items() if k in ('Wq', 'Wk', 'Wv', 'Wo', 'q_norm_w', 'k_norm_w')}
    del _L0_xattn_all

    def _L0_ffn_setup():
        import jax, jax.numpy as jnp
        import numpy as np
        B_, S, D = (4, 1024, 1024)
        E, R, O = (8, 16, 1024)
        TOP_K = 2
        SCALING = 8.0 / R
        key = jax.random.key(seed)
        ks = jax.random.split(key, 5)
        x = jax.random.normal(ks[0], (B_, S, D), dtype=jnp.float32)
        router_w = jax.random.normal(ks[1], (E, D), dtype=jnp.float32) * (1.0 / np.sqrt(D))
        router_b = jax.random.normal(ks[2], (E,), dtype=jnp.float32) * 0.01
        A = jax.random.normal(ks[3], (E, R, D), dtype=jnp.float32) * (1.0 / np.sqrt(D))
        Bm = jax.random.normal(ks[4], (E, O, R), dtype=jnp.float32) * 0.02
        return {'x': x, 'router_w': router_w, 'router_b': router_b, 'A': A, 'Bm': Bm}
    _L0_ffn_all = _L0_ffn_setup()
    _L0_ffn_in = {k: v for k, v in _L0_ffn_all.items() if k in ('router_w', 'router_b', 'A', 'Bm')}
    del _L0_ffn_all
    return {'x': x, 'ctx_4096': ctx_4096, 'g_xattn': g_xattn, 'g_ffn': g_ffn, 'L0_xattn_Wq': _L0_xattn_in['Wq'], 'L0_xattn_Wk': _L0_xattn_in['Wk'], 'L0_xattn_Wv': _L0_xattn_in['Wv'], 'L0_xattn_Wo': _L0_xattn_in['Wo'], 'L0_xattn_q_norm_w': _L0_xattn_in['q_norm_w'], 'L0_xattn_k_norm_w': _L0_xattn_in['k_norm_w'], 'L0_ffn_router_w': _L0_ffn_in['router_w'], 'L0_ffn_router_b': _L0_ffn_in['router_b'], 'L0_ffn_A': _L0_ffn_in['A'], 'L0_ffn_Bm': _L0_ffn_in['Bm']}

def reference(x, ctx_4096, g_xattn, g_ffn, L0_xattn_Wq, L0_xattn_Wk, L0_xattn_Wv, L0_xattn_Wo, L0_xattn_q_norm_w, L0_xattn_k_norm_w, L0_ffn_router_w, L0_ffn_router_b, L0_ffn_A, L0_ffn_Bm):
    import jax
    import jax.numpy as jnp

    def _L0_xattn_ref(latents, context, Wq, Wk, Wv, Wo, q_norm_w, k_norm_w):
        import jax, jax.numpy as jnp
        import numpy as np
        HEADS = 32
        KV_HEADS = 8
        HEAD_DIM = 128
        EPS = 1e-06

        def rms_norm(x, w):
            var = jnp.mean(jnp.square(x.astype(jnp.float32)), axis=-1, keepdims=True)
            return (x.astype(jnp.float32) * jax.lax.rsqrt(var + EPS)).astype(x.dtype) * w
        bsz, q_len, hidden = latents.shape
        kv = jnp.concatenate([context, latents], axis=1)
        kv_len = kv.shape[1]
        groups = HEADS // KV_HEADS
        q = (latents @ Wq).reshape(bsz, q_len, HEADS, HEAD_DIM).transpose(0, 2, 1, 3)
        k = (kv @ Wk).reshape(bsz, kv_len, KV_HEADS, HEAD_DIM).transpose(0, 2, 1, 3)
        v = (kv @ Wv).reshape(bsz, kv_len, KV_HEADS, HEAD_DIM).transpose(0, 2, 1, 3)
        q = rms_norm(q, q_norm_w)
        k = rms_norm(k, k_norm_w)
        qg = q.reshape(bsz, KV_HEADS, groups, q_len, HEAD_DIM)
        scale = 1.0 / np.sqrt(HEAD_DIM)
        scores = jnp.einsum('bhgqd,bhkd->bhgqk', qg, k) * scale
        probs = jax.nn.softmax(scores.astype(jnp.float32), axis=-1).astype(q.dtype)
        out = jnp.einsum('bhgqk,bhkd->bhgqd', probs, v)
        out = out.reshape(bsz, HEADS, q_len, HEAD_DIM).transpose(0, 2, 1, 3)
        out = out.reshape(bsz, q_len, HEADS * HEAD_DIM)
        return out @ Wo

    def _L0_ffn_ref(x, router_w, router_b, A, Bm):
        import jax, jax.numpy as jnp
        import numpy as np
        B_, S, D = (4, 1024, 1024)
        E, R, O = (8, 16, 1024)
        TOP_K = 2
        SCALING = 8.0 / R
        flat = x.reshape(-1, x.shape[-1])
        N = flat.shape[0]
        logits = flat @ router_w.T + router_b
        probs = jax.nn.softmax(logits, axis=-1)
        topv, topi = jax.lax.top_k(probs, TOP_K)
        gates = topv / jnp.sum(topv, axis=-1, keepdims=True)
        w = jnp.zeros((N, E), dtype=flat.dtype).at[jnp.arange(N)[:, None], topi].add(gates)
        h = jnp.einsum('nd,erd->ner', flat, A)
        hw = h * w[:, :, None]
        out = jnp.einsum('ner,eor->no', hw, Bm) * SCALING
        return out.reshape(*x.shape[:-1], O)
    x = x + jnp.tanh(g_xattn[0]) * _L0_xattn_ref(_layernorm(x, axis=-1), ctx_4096, L0_xattn_Wq, L0_xattn_Wk, L0_xattn_Wv, L0_xattn_Wo, L0_xattn_q_norm_w, L0_xattn_k_norm_w)
    x = x + jnp.tanh(g_ffn[0]) * _L0_ffn_ref(_layernorm(x, axis=-1), L0_ffn_router_w, L0_ffn_router_b, L0_ffn_A, L0_ffn_Bm)
    return x

_drawn_inputs = setup_inputs


def setup_inputs(seed=0):
    import zlib

    import numpy as np

    out = dict(_drawn_inputs(seed))
    spreads = {'L0_xattn_q_norm_w': (1.0, 0.6), 'L0_xattn_k_norm_w': (1.0, 0.6)}
    factors = {'L0_ffn_router_b': 8.0}
    for name, (base, spread) in spreads.items():
        noise = np.random.default_rng([zlib.crc32(name.encode()), seed]).standard_normal(out[name].shape)
        drawn = base * np.exp(spread * noise) if base else spread * noise
        out[name] = jnp.asarray(drawn.astype(out[name].dtype))
    for name, factor in factors.items():
        out[name] = (out[name] * factor).astype(out[name].dtype)
    return out
```

```python
from contextlib import ExitStack

import numpy as np

import concourse.bass as bass
from concourse import mybir

F32 = mybir.dt.float32
F32R = mybir.dt.float32r
U32 = mybir.dt.uint32
ACT = mybir.ActivationFunctionType
ALU = mybir.AluOpType
AX = mybir.AxisListType

P = 128
B = 8
NQ = 100
NC = 361
NK = NC + NQ
NKE = NK + NK % 2
D = 1024
C = D // P
HD = 128
H = 32
G = 8
R = H // G
HALVES = 2
GH = G // HALVES
KT = 4
ROWS = [121, 120, 120, NQ]
OFF = [0, 121, 241, NC]
RMAX = max(ROWS)
QW = R * NQ
KW = GH * HD
STAGES = HALVES * B
TH = 2
TB = B // TH
TW = TB * NQ
E = 8
ER = 128
AE = ER + E
RMS_EPS = 1e-6
LN_EPS = 1e-5
SCALING = 8.0 / 16


def build(nc, x, ctxT, Wq, Wkv, Wo, AR, BmT, vecs, rows, out):
    with ExitStack() as ctx:
        def sem(name):
            return ctx.enter_context(nc.semaphore(name))

        def sb(stack, name, shape, dt=F32):
            return stack.enter_context(nc.sbuf_tensor(name, shape, dt))

        xnT_d = nc.dram_tensor("xnT_d", [B, P, C, NQ], F32).ap()
        q_d = nc.dram_tensor("q_d", [G, P, B, QW], F32).ap()
        at_d = nc.dram_tensor("at_d", [STAGES, GH, P, QW], F32).ap()

        ident = sb(ctx, "ident", [P, P])
        ones = sb(ctx, "ones", [P, 1])
        mhalf = sb(ctx, "mhalf", [P, E])
        qkw = sb(ctx, "qkw", [P, 2])
        wqk = sb(ctx, "wqk", [P, 1])
        rowc = sb(ctx, "rowc", [P, 2 + 2 * E])
        gates_t = sb(ctx, "gates_t", [P, 2])
        cffn = sb(ctx, "cffn", [P, 1])
        rq = sb(ctx, "rq", [P, H, B])
        bn6 = sb(ctx, "bn6", [P, 2, 2, 6])
        mv = sb(ctx, "mv", [P, B, 2])
        mv2 = sb(ctx, "mv2", [P, B, 2])
        rstd = sb(ctx, "rstd", [P, B, 2])
        ms = sb(ctx, "ms", [P, R, B])
        rqt = sb(ctx, "rqt", [P, R, B])
        epst = sb(ctx, "epst", [P, GH])
        ssk = sb(ctx, "ssk", [P, KT, GH])
        msk = sb(ctx, "msk", [P, KT, GH])
        rk = sb(ctx, "rk", [P, 2, KT, GH])
        mx = sb(ctx, "mx", [P, R])
        nm = sb(ctx, "nm", [P, R])
        rqs = sb(ctx, "rqs", [P, R])
        nrq = sb(ctx, "nrq", [P, R])
        rs = sb(ctx, "rs", [P, R])
        rr = sb(ctx, "rr", [P, R])

        with ExitStack() as a1:
            xa = sb(a1, "xa", [P, B, D])
            xT_raw = sb(a1, "xT_raw", [P, B, C, NQ])
        bst = ExitStack()
        w_hi = sb(bst, "w_hi", [P, C, 2 * KW], F32R)
        w_lo = sb(bst, "w_lo", [P, C, 2 * KW], F32R)
        kv_raw = sb(bst, "kv_raw", [P, KT, C * RMAX])
        kv_hi = sb(bst, "kv_hi", [P, KT, C, P], F32R)
        kv_lo = sb(bst, "kv_lo", [P, KT, C, P], F32R)
        with ExitStack() as a2:
            xT_hi = sb(a2, "xT_hi", [P, C, B * NQ], F32R)
            xT_lo = sb(a2, "xT_lo", [P, C, B * NQ], F32R)
            wq_raw = sb(a2, "wq_raw", [P, 2, C, HD])
            wq_hi = sb(a2, "wq_hi", [P, 2, C, HD], F32R)
            wq_lo = sb(a2, "wq_lo", [P, 2, C, HD], F32R)
            qo = sb(a2, "qo", [P, B, R, NQ])
            sq = sb(a2, "sq", [P, TH, TW])
        with ExitStack() as b2:
            k_raw = sb(b2, "k_raw", [P, 2, KT, KW])
            v_raw = sb(b2, "v_raw", [P, 2, KT, KW])
            ksq = sb(b2, "ksq", [P, KW])
            w_raw = sb(b2, "w_raw", [P, 2, 2 * KW])
            q_raw = sb(b2, "q_raw", [P, QW])
            q_hi = sb(b2, "q_hi", [P, QW], F32R)
            q_lo = sb(b2, "q_lo", [P, QW], F32R)
            k_n = sb(b2, "k_n", [P, KT, HD])
            kT_hi = sb(b2, "kT_hi", [P, NKE], F32R)
            kT_lo = sb(b2, "kT_lo", [P, NKE], F32R)
            v_hi = sb(b2, "v_hi", [P, KT, HD], F32R)
            v_lo = sb(b2, "v_lo", [P, KT, HD], F32R)
            pr = sb(b2, "pr", [P, 2, R, NK])
            pT_hi = sb(b2, "pT_hi", [P, KT, QW], F32R)
            pT_lo = sb(b2, "pT_lo", [P, KT, QW], F32R)
            ao = sb(b2, "ao", [P, 2, QW])
        with ExitStack() as c2:
            oT = sb(c2, "oT", [P, C, TW])
            ar = sb(c2, "ar", [P, C, AE])
            bm = sb(c2, "bm", [P, D])
            xr = sb(c2, "xr", [P, 2, D])
            x1 = sb(c2, "x1", [P, 3, D])
            y = sb(c2, "y", [P, 2, D])
            yT = sb(c2, "yT", [P, 2, C, NQ])
            lg = sb(c2, "lg", [P, E])
            top = sb(c2, "top", [P, E])
            topi = sb(c2, "topi", [P, E], U32)
            topf = sb(c2, "topf", [P, 2])
            ntop = sb(c2, "ntop", [P, 1])
            ex = sb(c2, "ex", [P, 2])
            exs = sb(c2, "exs", [P, 1])
            exr = sb(c2, "exr", [P, 1])
            gt = sb(c2, "gt", [P, 2])
            wa = sb(c2, "wa", [P, E])
            wb = sb(c2, "wb", [P, E])
            we = sb(c2, "we", [P, E])
            hw = sb(c2, "hw", [P, ER])
            hwT = sb(c2, "hwT", [P, NQ])
            x2 = sb(c2, "x2", [P, 2, D])
        bst.close()
        c1 = ctx.enter_context(ExitStack())
        wo_raw = sb(c1, "wo_raw", [P, 2, R, 512])
        at_raw = sb(c1, "at_raw", [P, 2, TB, QW])
        wo_hi = sb(c1, "wo_hi", [P, 2, R, 512], F32R)
        wo_lo = sb(c1, "wo_lo", [P, 2, R, 512], F32R)
        at_hi = sb(c1, "at_hi", [P, 2, TB, QW], F32R)
        at_lo = sb(c1, "at_lo", [P, 2, TB, QW], F32R)

        ps = [ctx.enter_context(nc.psum_tensor(f"bank{i}", [P, 512], F32)) for i in range(8)]
        BK, BV, BS, BPT, BPV, BKT = 0, 1, (2, 3), (4, 5), 6, 7

        def sbank(i, last):
            return (BS + (BK, BV))[i] if last else BS[i % 2]

        consts_in = sem("consts_in")
        pool_consts = sem("pool_consts")
        wqk_done = sem("wqk_done")
        tanh_done = sem("tanh_done")
        cffn_done = sem("cffn_done")
        x_in = [sem(f"x_in{b}") for b in range(B)]
        stats_done = sem("stats_done")
        aggr_done = sem("aggr_done")
        var_done = sem("var_done")
        rstd_done = sem("rstd_done")
        xn_done = sem("xn_done")
        xt_done = sem("xt_done")
        xt_raw_done = sem("xt_raw_done")
        xt_hi_done = sem("xt_hi_done")
        xt_lo_done = sem("xt_lo_done")
        xnT_stored = sem("xnT_stored")
        wq_in = [sem("wq_in0"), sem("wq_in1")]
        wq_hi_done = sem("wq_hi_done")
        wq_lo_done = sem("wq_lo_done")
        q_done = sem("q_done")
        sq_done = sem("sq_done")
        qo_done = sem("qo_done")
        qo_stored = sem("qo_stored")
        ss_done = sem("ss_done")
        ms_done = sem("ms_done")
        rqt_done = sem("rqt_done")
        rq_done = sem("rq_done")
        pad_done = sem("pad_done")
        w_in = [sem("w_in0"), sem("w_in1")]
        w_hi_done = sem("w_hi_done")
        w_lo_done = sem("w_lo_done")
        kv_in = [sem(f"kv_in{t}") for t in range(KT)]
        kv_hi_done = sem("kv_hi_done")
        kv_lo_done = sem("kv_lo_done")
        k_proj_done = sem("k_proj_done")
        v_proj_done = sem("v_proj_done")
        k_raw_done = sem("k_raw_done")
        ksq_done = sem("ksq_done")
        v_raw_done = sem("v_raw_done")
        ssk_done = sem("ssk_done")
        msk_done = sem("msk_done")
        rk_done = sem("rk_done")
        kn_done = sem("kn_done")
        kt_done = sem("kt_done")
        kT_hi_done = sem("kT_hi_done")
        kT_lo_done = sem("kT_lo_done")
        q_in = sem("q_in")
        q_hi_done = sem("q_hi_done")
        q_lo_done = sem("q_lo_done")
        v_hi_done = sem("v_hi_done")
        v_lo_done = sem("v_lo_done")
        s_done = sem("s_done")
        rqs_done = sem("rqs_done")
        nrq_done = sem("nrq_done")
        mx_done = sem("mx_done")
        nm_done = sem("nm_done")
        exp_done = sem("exp_done")
        rr_done = sem("rr_done")
        p_done = sem("p_done")
        pt_done = sem("pt_done")
        pT_hi_done = sem("pT_hi_done")
        pT_lo_done = sem("pT_lo_done")
        pv_done = sem("pv_done")
        ao_done = sem("ao_done")
        ao_stored = [sem("ao_stored0"), sem("ao_stored1")]
        wo_in = [sem("wo_in0"), sem("wo_in1")]
        wo_hi_done = sem("wo_hi_done")
        wo_lo_done = sem("wo_lo_done")
        wo_used = sem("wo_used")
        o_done = sem("o_done")
        oT_act = sem("oT_act")
        oT_dve = sem("oT_dve")
        ffn_in = sem("ffn_in")
        xr_in = [sem("xr_in0"), sem("xr_in1")]
        t1_done = sem("t1_done")
        x1_done = sem("x1_done")
        st2_done = sem("st2_done")
        ag2_done = sem("ag2_done")
        va2_done = sem("va2_done")
        rs2_done = sem("rs2_done")
        y_done = sem("y_done")
        t2_done = sem("t2_done")
        yT_done = sem("yT_done")
        ae_done = sem("ae_done")
        lg_done = sem("lg_done")
        top_done = sem("top_done")
        topi_done = sem("topi_done")
        topf_done = sem("topf_done")
        ex_done = sem("ex_done")
        gate_step = sem("gate_step")
        wsum_done = sem("wsum_done")
        hw_done = sem("hw_done")
        t3_done = sem("t3_done")
        hwT_done = sem("hwT_done")
        y2_done = sem("y2_done")
        x2_done = sem("x2_done")
        x2_stored = [sem("x2_stored0"), sem("x2_stored1")]

        block = ctx.enter_context(nc.Block())

        def later(n, k):
            return not isinstance(n, int) or n >= k

        def stages(eng, stage):
            stage(0, 0, 0)
            with eng.Fori(1, 6, 2) as s:
                stage(s, 1, 0)
                stage(s + 1, 0, 0)
            stage(7, 1, 0)
            with eng.Fori(8, 13, 2) as s:
                stage(s, 0, 1)
                stage(s + 1, 1, 1)
            stage(14, 0, 1)
            stage(15, 1, 1)

        def projects(s):
            return not isinstance(s, int) or s + 1 < STAGES

        def splits(s, j):
            return not isinstance(s, int) or 4 * s + j + 7 < 4 * STAGES

        def wstage(c):
            flat = kv_raw[:].rearrange("p t k -> p (t k)")
            return flat[:, (c % 2) * 2 * KW:(c % 2 + 1) * 2 * KW]

        def raw_tile(t):
            return kv_raw[:, t, 0:C * ROWS[t]].rearrange("p (c k) -> p c k", c=C)

        @block.sync
        def _(sp):
            sp.dma_start(qkw[:], vecs).then_inc(consts_in, 16)
            sp.dma_start(rowc[:], rows).then_inc(consts_in, 16)
            for b in range(B):
                sp.dma_start(xa[0:NQ, b, :], x[b]).then_inc(x_in[b], 16)
                if b < 2:
                    sp.dma_start(wq_raw[:, b], Wq[b]).then_inc(wq_in[b], 16)
            for b in range(B):
                sp.wait_ge(xt_raw_done, b + 1)
                sp.dma_start(xnT_d[b], xT_raw[:, b]).then_inc(xnT_stored, 16)

            def queries(g):
                for i in range(R):
                    h = 4 * g + i
                    if isinstance(h, int) and h < H - 2 or not isinstance(h, int):
                        sp.wait_ge(wq_lo_done, h + 1)
                        sp.dma_start(wq_raw[:, i % 2], Wq[h + 2] if isinstance(h, int) else
                                     Wq[bass.ds(h + 2, 1)].rearrange("o p c n -> p (o c) n")).then_inc(wq_in[i % 2], 16)
                    if isinstance(g, int) and g == 0:
                        for c in (2 * i, 2 * i + 1):
                            if c >= 2:
                                sp.wait_ge(w_lo_done, c - 1)
                            sp.dma_start(wstage(c), Wkv[0, :, c]).then_inc(w_in[c % 2], 16)
                sp.wait_ge(qo_done, 8 * g + 8)
                if isinstance(g, int):
                    sp.dma_start(q_d[g], qo[:].rearrange("p b i q -> p b (i q)")).then_inc(qo_stored, 16)
                else:
                    sp.dma_start(q_d[bass.ds(g, 1)].rearrange("o p b q -> p (o b) q"),
                                 qo[:].rearrange("p b i q -> p b (i q)")).then_inc(qo_stored, 16)

            queries(0)

            def load_kv(n, t):
                if later(n, 1):
                    sp.wait_ge(kv_lo_done, 4 * (n - 1) + t + 1)
                dst = kv_raw[:, t, 0:C * ROWS[t]]
                if t < KT - 1:
                    cols = slice(C * OFF[t], C * (OFF[t] + ROWS[t]))
                    src = ctxT[n % B, :, cols] if isinstance(n, int) else \
                        ctxT[bass.ds(n % B, 1), :, cols].rearrange("o p k -> p (o k)")
                else:
                    src = xnT_d[n % B].rearrange("p c k -> p (c k)") if isinstance(n, int) else \
                        xnT_d[bass.ds(n % B, 1)].rearrange("o p c k -> p (o c k)")
                sp.dma_start(dst, src).then_inc(kv_in[t], 16)

            sp.wait_ge(w_lo_done, C)
            sp.wait_ge(xnT_stored, 16 * B)
            for t in range(KT):
                load_kv(0, t)
            with sp.Fori(1, G - 1) as g:
                queries(g)
            queries(G - 1)

            def load_q(s, j, half):
                u = 4 * s + j
                if later(u, 1):
                    sp.wait_ge(q_lo_done, u)
                else:
                    sp.wait_ge(qo_stored, 16 * G)
                if isinstance(s, int):
                    src = q_d[half * GH + j, :, s % B]
                else:
                    src = q_d[half * GH + j, :, bass.ds(s - B * half, 1)].rearrange("p o q -> p (o q)")
                sp.dma_start(q_raw[:], src).then_inc(q_in, 16)

            def store_attn(s, j):
                u = 4 * s + j
                sp.wait_ge(ao_done, u + 1)
                dst = at_d[s, j] if isinstance(s, int) else at_d[bass.ds(s, 1), j].rearrange("o p q -> p (o q)")
                sp.dma_start(dst, ao[:, j % 2]).then_inc(ao_stored[j % 2], 16)

            load_q(0, 0, 0)
            for t in range(KT):
                load_kv(1, t)

            at_g = at_d.rearrange("(h b) g p q -> h b g p q", h=HALVES)

            def chunk(th, nh, gp, k):
                m = 16 * th + 8 * nh + 2 * gp + k
                if later(m, 2):
                    sp.wait_ge(wo_lo_done, 2 * m - 2)
                if isinstance(gp, int):
                    g = 2 * gp + k
                    wsrc = Wo[nh, g]
                    asrc = at_g[g // GH, TB * th:TB * th + TB, g % GH].rearrange("b p q -> p b q")
                else:
                    wsrc = Wo[nh, bass.ds(2 * gp + k, 1)].rearrange("o p i n -> p (o i) n")
                    asrc = at_g[bass.ds(gp // 2, 1), TB * th:TB * th + TB, bass.ds(gp % 2 * 2 + k, 1)]\
                        .rearrange("h b o p q -> p (h b o) q")
                sp.dma_start(wo_raw[:, k], wsrc).then_inc(wo_in[k], 16)
                sp.dma_start(at_raw[:, k], asrc).then_inc(wo_in[k], 16)

            def combo(th, nh, first=0):
                if not first:
                    chunk(th, nh, 0, 0)
                    chunk(th, nh, 0, 1)
                with sp.Fori(1, G // 2) as gp:
                    chunk(th, nh, gp, 0)
                    chunk(th, nh, gp, 1)

            def stage(s, par, half):
                for j in range(GH):
                    if j == 0 and isinstance(s, int) and s == B - 1:
                        for c in range(C):
                            if c >= 2:
                                sp.wait_ge(w_lo_done, C + c - 1)
                            sp.dma_start(w_raw[:, c % 2], Wkv[1, :, c]).then_inc(w_in[c % 2], 16)
                    if splits(s, 1):
                        load_kv(s + 2, j)
                    if isinstance(s, int) and s == STAGES - 1 and j == 0:
                        sp.wait_ge(v_proj_done, 4 * STAGES)
                        sp.wait_ge(ao_stored[0], 32 * (B + TB))
                        sp.wait_ge(ao_stored[1], 32 * (B + TB))
                        chunk(0, 0, 0, 0)
                        chunk(0, 0, 0, 1)
                    if j + 1 < GH:
                        load_q(s, j + 1, half)
                    elif projects(s):
                        last_of_half = isinstance(s, int) and s == B - 1
                        load_q(s + 1, 0, 1 if last_of_half else half)
                    if j >= 1:
                        store_attn(s, j - 1)
                    elif later(s, 1):
                        store_attn(s - 1, GH - 1)

            stages(sp, stage)

            sp.wait_ge(ao_done, 4 * STAGES)
            sp.dma_start(at_d[STAGES - 1, GH - 1], ao[:, 1]).then_inc(ao_stored[1], 16)

            def load_x(t):
                sp.dma_start(xr[0:NQ, t % 2], x[t]).then_inc(xr_in[t % 2], 16)

            def store(t):
                sp.wait_ge(x2_done, 2 * t + 2)
                sp.dma_start(out[t], x2[0:NQ, t % 2]).then_inc(x2_stored[t % 2], 16)

            sp.wait_ge(ao_stored[0], 16 * 2 * STAGES)
            sp.wait_ge(ao_stored[1], 16 * 2 * STAGES)
            sp.dma_start(ar[:], AR).then_inc(ffn_in, 16)
            sp.dma_start(bm[:], BmT).then_inc(ffn_in, 16)
            load_x(0)
            load_x(1)
            combo(0, 0, first=1)
            combo(0, 1)
            for t in range(TB):
                sp.wait_ge(x1_done, 2 * t + 2)
                load_x(t + 2)
                store(t)
            combo(1, 0)
            combo(1, 1)
            for t in range(TB, B):
                sp.wait_ge(x1_done, 2 * t + 2)
                if t + 2 < B:
                    load_x(t + 2)
                store(t)
            sp.wait_ge(x2_stored[0], 16 * B // 2)
            sp.wait_ge(x2_stored[1], 16 * B // 2)

        @block.gpsimd
        def _(pool):
            pool.memset(ident[:], 0.0).then_inc(pool_consts, 1)
            pool.memset(ones[:], 1.0).then_inc(pool_consts, 1)
            pool.memset(mhalf[:], -0.5).then_inc(pool_consts, 1)
            pool.memset(epst[:], RMS_EPS).then_inc(pool_consts, 1)
            pool.wait_ge(pool_consts, 4)
            pool.affine_select(out=ident[:], in_=ident[:], compare_op=ALU.not_equal, fill=1.0, base=0,
                               pattern=[[-1, P]], channel_multiplier=1).then_inc(pool_consts, 1)
            for b in range(B):
                pool.wait_ge(aggr_done, b + 1)
                pool.tensor_scalar(rstd[0:NQ, b, 0:1], mv[0:NQ, b, 1:2], 1.0, LN_EPS, ALU.mult, ALU.add).then_inc(var_done, 1)
                pool.wait_ge(var_done, b + 1)
                pool.tensor_tensor(rstd[0:NQ, b, 1:2], rstd[0:NQ, b, 0:1], mhalf[0:NQ, 0:1], ALU.pow).then_inc(rstd_done, 1)

            def head_rms(g):
                for i in range(R):
                    if later(g, 1):
                        pool.wait_ge(rq_done, 4 * g + i - 3)
                    pool.wait_ge(ms_done, 4 * g + i + 1)
                    pool.tensor_tensor(rqt[0:NQ, i, :], ms[0:NQ, i, :], mhalf[0:NQ, 0:B], ALU.pow).then_inc(rqt_done, 1)

            head_rms(0)
            with pool.Fori(1, G) as g:
                head_rms(g)

            def key_rms(n, par):
                for t in range(KT):
                    v = 4 * n + t
                    pool.wait_ge(ssk_done, v + 1)
                    pool.tensor_tensor(msk[:, t, :], ssk[:, t, :], epst[:], ALU.add).then_inc(msk_done, 1)
                    if t == 0 and later(n, 2):
                        pool.wait_ge(kn_done, 4 * (n - 1))
                    pool.wait_ge(msk_done, v + 1)
                    pool.tensor_tensor(rk[:, par, t, :], msk[:, t, :], mhalf[:, 0:GH], ALU.pow).then_inc(rk_done, 1)

            key_rms(0, 0)
            key_rms(1, 1)
            with pool.Fori(2, STAGES - 1, 2) as n:
                key_rms(n, 0)
                key_rms(n + 1, 1)
            for t in range(B):
                pool.wait_ge(ag2_done, t + 1)
                pool.tensor_scalar(mv2[0:NQ, t, 0:1], mv[0:NQ, t, 1:2], 1.0, LN_EPS, ALU.mult, ALU.add).then_inc(va2_done, 1)
                pool.wait_ge(va2_done, t + 1)
                pool.tensor_tensor(mv2[0:NQ, t, 1:2], mv2[0:NQ, t, 0:1], mhalf[0:NQ, 0:1], ALU.pow).then_inc(rs2_done, 1)

        @block.tensor
        def _(pe):
            def three(o, lh, ll, rh, rl, start, stop):
                pe.matmul(o, lh, rh, start=start, stop=False)
                pe.matmul(o, lh, rl, start=False, stop=False)
                return pe.matmul(o, ll, rh, start=False, stop=stop)

            pe.wait_ge(pool_consts, 5)
            for b in range(B):
                pe.wait_ge(xn_done, b + 1)
                if b >= 2:
                    pe.wait_ge(xt_raw_done, b - 1)
                for c in range(C):
                    bank = ps[4 + 2 * (b % 2) + c // 4]
                    mm = pe.transpose(bank[:, (c % 4) * NQ:(c % 4 + 1) * NQ], xa[0:NQ, b, c * P:(c + 1) * P],
                                      ident[0:NQ, 0:NQ])
                mm.then_inc(xt_done, 1)

            def squares(h, th, i):
                pe.wait_ge(sq_done, 2 * h + th + 1)
                if th == 0 and later(h, 2):
                    pe.wait_ge(ms_done, h - 1)
                for b in range(TB):
                    mm = pe.matmul(ps[4 + i % 2][0:NQ, TB * th + b:TB * th + b + 1],
                                   sq[:, th, b * NQ:(b + 1) * NQ], ones[:], start=True, stop=True)
                mm.then_inc(ss_done, 1)

            def queries(g):
                for i in range(R):
                    h = 4 * g + i
                    pe.wait_ge(wq_lo_done, h + 1)
                    for th in range(TH):
                        if isinstance(g, int) and g == 0 and i == 0:
                            pe.wait_ge(xt_lo_done, TB * (th + 1))
                        if later(h, 2):
                            pe.wait_ge(qo_done, 2 * (h - 2) + th + 1)
                        o = ps[2 * (i % 2) + th][:, 0:TW]
                        for c in range(C):
                            mm = three(o, wq_hi[:, i % 2, c], wq_lo[:, i % 2, c],
                                       xT_hi[:, c, th * TW:(th + 1) * TW], xT_lo[:, c, th * TW:(th + 1) * TW],
                                       c == 0, c == C - 1)
                        mm.then_inc(q_done, 1)
                        if th == 0 and later(h, 1):
                            squares(h - 1, 1, i + 1)
                        if th == 1:
                            squares(h, 0, i)

            queries(0)
            with pe.Fori(1, G) as g:
                queries(g)
            squares(H - 1, 1, R - 1)

            def proj_chunk(s, j, half, n):
                v = 4 * s + 4 + j
                isv, cc = n // 4, 2 * (n % 4)
                if n == 0:
                    pe.wait_ge(kv_lo_done, v + 1)
                    if later(v, 1):
                        pe.wait_ge(ksq_done, v)
                if n == 4 and later(v, 1):
                    pe.wait_ge(v_raw_done, v)
                for c in (cc, cc + 1):
                    if j == 0 and isv == 0:
                        pe.wait_ge(w_lo_done, C * half + c + 1)
                    mm = three(ps[BV if isv else BK][:, 0:KW], kv_hi[:, j, c], kv_lo[:, j, c],
                               w_hi[:, c, isv * KW:(isv + 1) * KW], w_lo[:, c, isv * KW:(isv + 1) * KW],
                               c == 0, c == C - 1)
                if n == 3:
                    mm.then_inc(k_proj_done, 1)
                if n == 7:
                    mm.then_inc(v_proj_done, 1)

            def turn_keys(u):
                pe.wait_ge(kn_done, u + 1)
                if later(u, 1):
                    pe.wait_ge(kT_lo_done, u)
                for t in range(KT):
                    r = ROWS[t] + (NKE - NK if t == KT - 1 else 0)
                    mm = pe.transpose(ps[BKT][:, OFF[t]:OFF[t] + r], k_n[0:r, t, :], ident[0:r, 0:r])
                mm.then_inc(kt_done, 1)

            def scores(u, i, last=False):
                if i == 0:
                    pe.wait_ge(kT_lo_done, u + 1)
                    pe.wait_ge(q_lo_done, u + 1)
                a = 4 * u + i
                if last and u > 4 * (STAGES - 1):
                    pe.wait_ge(exp_done, a - 3)
                elif last and i >= 2:
                    pe.wait_ge(v_raw_done, u)
                    pe.wait_ge(ksq_done, u)
                elif later(a, 2):
                    pe.wait_ge(exp_done, a - 1)
                three(ps[sbank(i, last)][0:NQ, 0:NKE], q_hi[:, i * NQ:(i + 1) * NQ], q_lo[:, i * NQ:(i + 1) * NQ],
                      kT_hi[:], kT_lo[:], True, True).then_inc(s_done, 1)

            def turn_probs(u, par, t):
                if t == 0:
                    pe.wait_ge(p_done, 4 * u + 4)
                a = 4 * u + t
                if later(a, 2):
                    pe.wait_ge(pT_lo_done, a - 1)
                for i in range(R):
                    mm = pe.transpose(ps[BPT[t % 2]][0:ROWS[t], i * NQ:(i + 1) * NQ],
                                      pr[0:NQ, par, i, OFF[t]:OFF[t] + ROWS[t]], ident[0:NQ, 0:NQ])
                mm.then_inc(pt_done, 1)

            def values(u, t):
                pe.wait_ge(pT_lo_done, 4 * u + t + 1)
                if t == 0:
                    pe.wait_ge(v_lo_done, u + 1)
                    if later(u, 1):
                        pe.wait_ge(ao_done, u)
                r = ROWS[t]
                mm = three(ps[BPV][:, 0:QW], v_hi[0:r, t], v_lo[0:r, t], pT_hi[0:r, t], pT_lo[0:r, t],
                           t == 0, t == KT - 1)
                if t == KT - 1:
                    mm.then_inc(pv_done, 1)

            def slot(s, j, half, attend, project):
                u = 4 * s + j
                prev = attend and later(u, 1)
                par = (j + 1) % 2
                nhalf = 1 if isinstance(s, int) and s == B - 1 else half

                def c_(n):
                    if project:
                        proj_chunk(s, j, nhalf, n)
                if attend and not project:
                    turn_keys(u)
                    for i in range(R):
                        scores(u, i, last=True)
                    for t in range(KT + 1):
                        if t < KT:
                            turn_probs(u - 1, par, t)
                        if t:
                            values(u - 1, t - 1)
                    return
                new_weights = isinstance(s, int) and s == B - 1 and j == 0
                if not new_weights:
                    c_(0)
                if attend:
                    turn_keys(u)
                if prev:
                    turn_probs(u - 1, par, 0)
                if new_weights:
                    turn_probs(u - 1, par, 1)
                    c_(0)
                c_(1)
                if prev and not new_weights:
                    turn_probs(u - 1, par, 1)
                c_(2)
                if attend:
                    scores(u, 0)
                if prev:
                    values(u - 1, 0)
                    turn_probs(u - 1, par, 2)
                c_(3)
                if attend:
                    scores(u, 1)
                if prev:
                    values(u - 1, 1)
                    turn_probs(u - 1, par, 3)
                c_(4)
                if attend:
                    scores(u, 2)
                if prev:
                    values(u - 1, 2)
                c_(5)
                if attend:
                    scores(u, 3)
                if prev:
                    values(u - 1, 3)
                c_(6)
                c_(7)

            pe.wait_ge(qo_done, 2 * H)
            for j in range(KT):
                slot(-1, j, 0, False, True)
            pe.wait_ge(rq_done, H)
            stages(pe, lambda s, par, half: [slot(s, j, half, True, projects(s)) for j in range(GH)])
            last = 4 * STAGES - 1
            for t in range(KT):
                turn_probs(last, 1, t)
                if t:
                    values(last, t - 1)
            values(last, KT - 1)

            def chunk(th, nh, gp, k, first=False, last=False):
                m = 16 * th + 8 * nh + 2 * gp + k
                pe.wait_ge(wo_lo_done, 2 * m + 2)
                for i in range(R):
                    for n in range(4):
                        mm = three(ps[n][:, 0:TW].rearrange("p (b q) -> p b q", b=TB),
                                   wo_hi[:, k, i, n * P:(n + 1) * P], wo_lo[:, k, i, n * P:(n + 1) * P],
                                   at_hi[:, k, :, i * NQ:(i + 1) * NQ], at_lo[:, k, :, i * NQ:(i + 1) * NQ],
                                   first and i == 0, last and i == R - 1)
                return mm

            def combo(th, nh):
                if th or nh:
                    m = 2 * (2 * th + nh)
                    pe.wait_ge(oT_dve, m)
                    pe.wait_ge(oT_act, m)
                for k in range(2):
                    chunk(th, nh, 0, k, first=k == 0).then_inc(wo_used, 1)
                with pe.Fori(1, G // 2 - 1) as gp:
                    for k in range(2):
                        chunk(th, nh, gp, k).then_inc(wo_used, 1)
                for k in range(2):
                    chunk(th, nh, G // 2 - 1, k, last=k == 1).then_inc(wo_used, 1)

            def turn_out(t):
                m = 4 if t < TB else 8
                if t % TB == 0:
                    pe.wait_ge(oT_dve, m)
                    pe.wait_ge(oT_act, m)
                if t >= 1:
                    pe.wait_ge(x1_done, 2 * t)
                for c in range(C):
                    mm = pe.transpose(ps[4 + c // 4][0:NQ, (c % 4) * P:(c % 4 + 1) * P],
                                      oT[:, c, (t % TB) * NQ:(t % TB + 1) * NQ], ident[:])
                mm.then_inc(t1_done, 1)

            def turn_y(t):
                pe.wait_ge(y_done, t + 1)
                if t >= 1:
                    pe.wait_ge(yT_done, 2 * t)
                for c in range(C):
                    mm = pe.transpose(ps[6 + c // 4][:, (c % 4) * NQ:(c % 4 + 1) * NQ],
                                      y[0:NQ, t % 2, c * P:(c + 1) * P], ident[0:NQ, 0:NQ])
                mm.then_inc(t2_done, 1)

            def low_rank(t):
                pe.wait_ge(yT_done, 2 * t + 2)
                if t == 0:
                    pe.wait_ge(ffn_in, 32)
                if t >= 1:
                    pe.wait_ge(hw_done, t)
                for c in range(C):
                    mm = pe.matmul(ps[0][0:NQ, 0:AE], yT[:, t % 2, c], ar[:, c], start=(c == 0), stop=(c == C - 1))
                mm.then_inc(ae_done, 1)

            def turn_h(t):
                pe.wait_ge(hw_done, t + 1)
                if t >= 1:
                    pe.wait_ge(hwT_done, t)
                pe.transpose(ps[1][:, 0:NQ], hw[0:NQ], ident[0:NQ, 0:NQ]).then_inc(t3_done, 1)

            def up(t):
                pe.wait_ge(hwT_done, t + 1)
                if t >= 1:
                    pe.wait_ge(x2_done, 2 * t)
                pe.matmul(ps[2][0:NQ, :], hwT[:], bm[:, 0:512], start=True, stop=True)
                pe.matmul(ps[3][0:NQ, :], hwT[:], bm[:, 512:1024], start=True, stop=True).then_inc(y2_done, 1)

            def experts(t0):
                for k in range(TB + 2):
                    if k < TB:
                        turn_out(t0 + k)
                    if 1 <= k <= TB:
                        turn_y(t0 + k - 1)
                    if k >= 2:
                        turn_h(t0 + k - 2)
                        up(t0 + k - 2)
                    if 1 <= k <= TB:
                        low_rank(t0 + k - 1)

            combo(0, 0)
            combo(0, 1)
            experts(0)
            pe.wait_ge(x2_done, 2 * TB)
            combo(1, 0)
            combo(1, 1)
            experts(TB)

        @block.scalar
        def _(act):
            act.wait_ge(consts_in, 32)
            act.activation(gates_t[:], rowc[:, 0:2], ACT.Tanh).then_inc(tanh_done, 1)

            def wq_split(g, i):
                k, h = i % 2, 4 * g + i
                act.wait_ge(wq_in[k], 16 * (2 * g + i // 2 + 1))
                if later(h, 2):
                    act.wait_ge(q_done, 2 * (h - 2) + 2)
                act.activation(wq_hi[:, k], wq_raw[:, k], ACT.Copy).then_inc(wq_hi_done, 1)

            wq_split(0, 0)
            wq_split(0, 1)
            for b in range(B):
                act.wait_ge(xt_done, b + 1)
                for n in range(2):
                    ins = act.activation(xT_raw[:, b, 4 * n:4 * n + 4].rearrange("p c q -> p (c q)"),
                                         ps[4 + 2 * (b % 2) + n][:, 0:4 * NQ], ACT.Copy)
                ins.then_inc(xt_raw_done, 1)
                act.wait_ge(xt_raw_done, b + 1)
                act.activation(xT_hi[:, :, b * NQ:(b + 1) * NQ], xT_raw[:, b], ACT.Copy).then_inc(xt_hi_done, 1)

            def w_split(c, half):
                act.wait_ge(w_in[c % 2], 16 * (C // 2 * half + c // 2 + 1))
                if half == 0:
                    if c == 0:
                        act.wait_ge(xt_lo_done, B)
                        act.wait_ge(xnT_stored, 16 * B)
                elif c == 0:
                    act.wait_ge(v_proj_done, 4 * B)
                act.activation(w_hi[:, c], wstage(c) if half == 0 else w_raw[:, c % 2], ACT.Copy).then_inc(w_hi_done, 1)

            def queries(g):
                for i in range(R):
                    h = 4 * g + i
                    for th in range(TH):
                        act.wait_ge(q_done, 2 * h + th + 1)
                        if later(h, 1):
                            act.wait_ge(ss_done, 2 * (h - 1) + th + 1)
                        act.activation(sq[:, th], ps[2 * (i % 2) + th][:, 0:TW], ACT.Square).then_inc(sq_done, 1)
                    if not isinstance(g, int) or h + 2 < H:
                        wq_split(g, i + 2)
                    if isinstance(g, int) and g == 0:
                        w_split(2 * i, 0)
                        w_split(2 * i + 1, 0)

            queries(0)
            with act.Fori(1, G - 1) as g:
                queries(g)
            queries(G - 1)

            def kv_split(n, t):
                w = 4 * n + t
                act.wait_ge(kv_in[t], 16 * (n + 1))
                if later(w, 4):
                    act.wait_ge(v_proj_done, w - 3)
                act.activation(kv_hi[:, t, :, 0:ROWS[t]], raw_tile(t), ACT.Copy).then_inc(kv_hi_done, 1)

            act.wait_ge(pad_done, 1)
            for t in range(3):
                kv_split(0, t)

            def q_split(u):
                act.wait_ge(q_in, 16 * (u + 1))
                if later(u, 1):
                    act.wait_ge(s_done, 4 * u)
                act.activation(q_hi[:], q_raw[:], ACT.Copy).then_inc(q_hi_done, 1)

            def slot(s, j, par, half, attend, project):
                u, v = 4 * s + j, 4 * s + 4 + j
                prev = attend and later(u, 1)

                def p_split(t):
                    act.wait_ge(pt_done, 4 * (u - 1) + t + 1)
                    act.activation(pT_hi[0:ROWS[t], t], ps[BPT[t % 2]][0:ROWS[t], 0:QW], ACT.Copy).then_inc(pT_hi_done, 1)

                def exps(i):
                    a = 4 * u + i
                    act.wait_ge(nm_done, a + 1)
                    if i == 0 and later(u, 2):
                        act.wait_ge(pt_done, 4 * (u - 1))
                    act.activation(pr[0:NQ, j % 2, i], ps[sbank(i, not project)][0:NQ, 0:NK], ACT.Exp, bias=nm[0:NQ, i:i + 1],
                                   scale=rqs[0:NQ, i:i + 1], accum_out=rs[0:NQ, i:i + 1]).then_inc(exp_done, 1)

                if attend:
                    act.wait_ge(kt_done, u + 1)
                    act.activation(kT_hi[:], ps[BKT][:, 0:NKE], ACT.Copy).then_inc(kT_hi_done, 1)
                if isinstance(s, int) and s == B - 1 and j == 0:
                    for c in range(C):
                        w_split(c, 1)
                if attend and not project:
                    exps(0)
                    exps(1)
                    exps(2)
                    p_split(0)
                    exps(3)
                    p_split(1)
                    p_split(2)
                    p_split(3)
                if attend and project:
                    if prev:
                        p_split(0)
                        p_split(1)
                    exps(0)
                    if prev:
                        p_split(2)
                if project:
                    act.wait_ge(k_proj_done, v + 1)
                    if j == 0 and later(s, 1):
                        act.wait_ge(kn_done, 4 * s)
                    act.activation(k_raw[:, 1 - par, j], ps[BK][:, 0:KW], ACT.Copy).then_inc(k_raw_done, 1)
                    if later(v, 1):
                        act.wait_ge(ssk_done, v)
                    act.activation(ksq[:], ps[BK][:, 0:KW], ACT.Square, scale=float(HD) ** -0.5).then_inc(ksq_done, 1)
                if attend and project:
                    exps(1)
                    if prev:
                        p_split(3)
                    exps(2)
                    exps(3)
                if prev:
                    act.wait_ge(pv_done, u)
                    if later(u, 3):
                        act.wait_ge(ao_stored[1 - j % 2], 16 * (2 * s + (-1, 0, 0, 1)[j]))
                    act.activation(ao[:, 1 - j % 2], ps[BPV][:, 0:QW], ACT.Copy).then_inc(ao_done, 1)
                if splits(s, j):
                    kv_split(s + 1 if j == 0 else s + 2, (j + 3) % 4)
                if attend:
                    act.wait_ge(v_raw_done, 4 * s + 4)
                    if prev:
                        act.wait_ge(pv_done, u)
                    act.activation(v_hi[:], v_raw[:, par, :, j * HD:(j + 1) * HD], ACT.Copy).then_inc(v_hi_done, 1)
                    if j + 1 < GH or projects(s):
                        q_split(u + 1)
                if project:
                    act.wait_ge(v_proj_done, v + 1)
                    if j == 0 and later(s, 1):
                        act.wait_ge(v_lo_done, 4 * s)
                    act.activation(v_raw[:, 1 - par, j], ps[BV][:, 0:KW], ACT.Copy).then_inc(v_raw_done, 1)

            for j in range(KT):
                slot(-1, j, 1, 0, False, True)
            q_split(0)
            stages(act, lambda s, par, half: [slot(s, j, par, half, True, projects(s)) for j in range(GH)])
            last = 4 * STAGES - 1
            for t in range(KT):
                act.wait_ge(pt_done, 4 * last + t + 1)
                act.activation(pT_hi[0:ROWS[t], t], ps[BPT[t % 2]][0:ROWS[t], 0:QW], ACT.Copy).then_inc(pT_hi_done, 1)
            act.wait_ge(pv_done, last + 1)
            act.wait_ge(ao_stored[1], 16 * (2 * STAGES - 1))
            act.activation(ao[:, 1], ps[BPV][:, 0:QW], ACT.Copy).then_inc(ao_done, 1)

            def chunk(th, nh, gp, k):
                m = 16 * th + 8 * nh + 2 * gp + k
                act.wait_ge(wo_in[k], 32 * (8 * th + 4 * nh + gp + 1))
                if later(m, 2):
                    act.wait_ge(wo_used, m - 1)
                act.activation(wo_hi[:, k], wo_raw[:, k], ACT.Copy).then_inc(wo_hi_done, 1)
                act.activation(at_hi[:, k], at_raw[:, k], ACT.Copy).then_inc(wo_hi_done, 1)

            def combo(th, nh):
                chunk(th, nh, 0, 0)
                chunk(th, nh, 0, 1)
                with act.Fori(1, G // 2) as gp:
                    chunk(th, nh, gp, 0)
                    chunk(th, nh, gp, 1)

            def accumulators(th, nh):
                act.wait_ge(wo_used, 16 * th + 8 * nh + 8)
                for n in (2, 3):
                    act.activation(oT[:, 4 * nh + n], ps[n][:, 0:TW], ACT.Copy).then_inc(oT_act, 1)

            def turned_y(t):
                act.wait_ge(t2_done, t + 1)
                if t >= 2:
                    act.wait_ge(ae_done, t - 1)
                for n in range(2):
                    act.activation(yT[:, t % 2, 4 * n:4 * n + 4].rearrange("p c q -> p (c q)"), ps[6 + n][:, 0:4 * NQ],
                                   ACT.Copy).then_inc(yT_done, 1)

            def exps2(t):
                act.wait_ge(top_done, 2 * t + 2)
                if t >= 1:
                    act.wait_ge(gate_step, 5 * t)
                act.activation(ex[0:NQ], top[0:NQ, 0:2], ACT.Exp, bias=ntop[0:NQ]).then_inc(ex_done, 1)

            def turned_h(t):
                act.wait_ge(t3_done, t + 1)
                if t >= 1:
                    act.wait_ge(y2_done, t)
                act.activation(hwT[:], ps[1][:, 0:NQ], ACT.Copy).then_inc(hwT_done, 1)

            def experts(t0):
                for k in range(TB + 2):
                    if 1 <= k <= TB:
                        turned_y(t0 + k - 1)
                    if k >= 2:
                        turned_h(t0 + k - 2)
                    if 1 <= k <= TB:
                        exps2(t0 + k - 1)

            combo(0, 0)
            accumulators(0, 0)
            combo(0, 1)
            accumulators(0, 1)
            experts(0)
            combo(1, 0)
            accumulators(1, 0)
            combo(1, 1)
            accumulators(1, 1)
            experts(TB)

        @block.vector
        def _(dve):
            dve.wait_ge(consts_in, 32)
            dve.scalar_tensor_tensor(out=wqk[:], in0=qkw[:, 0:1], scalar=float(HD) ** -0.5, in1=qkw[:, 1:2],
                                     op0=ALU.mult, op1=ALU.mult).then_inc(wqk_done, 1)
            dve.wait_ge(tanh_done, 1)
            dve.tensor_scalar(cffn[:], gates_t[:, 1:2], SCALING, None, ALU.mult).then_inc(cffn_done, 1)

            def wq_split(k, h):
                dve.wait_ge(wq_hi_done, h + 1)
                dve.tensor_tensor(wq_lo[:, k], wq_raw[:, k], wq_hi[:, k], ALU.subtract).then_inc(wq_lo_done, 1)

            def stats(b):
                dve.wait_ge(x_in[b], 16)
                for n in range(2):
                    dve.bn_stats(bn6[0:NQ, b % 2, n], xa[0:NQ, b, n * 512:(n + 1) * 512]).then_inc(stats_done, 1)
                dve.wait_ge(stats_done, 2 * b + 2)
                dve.bn_aggr(mv[0:NQ, b], bn6[0:NQ, b % 2]).then_inc(aggr_done, 1)

            for t in range(KT):
                dve.memset(kv_hi[:, t, :, ROWS[t]:P].bitcast(U32), 0)
                ins = dve.memset(kv_lo[:, t, :, ROWS[t]:P].bitcast(U32), 0)
            ins.then_inc(pad_done, 1)

            def latent_split(b):
                dve.wait_ge(xt_hi_done, b + 1)
                dve.tensor_tensor(xT_lo[:, :, b * NQ:(b + 1) * NQ], xT_raw[:, b], xT_hi[:, :, b * NQ:(b + 1) * NQ],
                                  ALU.subtract).then_inc(xt_lo_done, 1)

            stats(0)
            for b in range(B):
                if b + 1 < B:
                    stats(b + 1)
                dve.wait_ge(aggr_done, b + 1)
                dve.wait_ge(rstd_done, b + 1)
                dve.tensor_scalar(xa[0:NQ, b], xa[0:NQ, b], mv[0:NQ, b, 0:1], rstd[0:NQ, b, 1:2],
                                  ALU.subtract, ALU.mult).then_inc(xn_done, 1)
                if b == 1:
                    wq_split(0, 0)
                    wq_split(1, 1)
                if b >= 1:
                    latent_split(b - 1)
            latent_split(B - 1)

            def w_split(c, half):
                dve.wait_ge(w_hi_done, C * half + c + 1)
                src = wstage(c) if half == 0 else w_raw[:, c % 2]
                dve.tensor_tensor(w_lo[:, c], src, w_hi[:, c], ALU.subtract).then_inc(w_lo_done, 1)

            def mean_squares(h, i):
                dve.wait_ge(ss_done, 2 * h + 2)
                if later(h, 4):
                    dve.wait_ge(rqt_done, h - 3)
                dve.tensor_scalar(ms[0:NQ, i % R], ps[4 + i % 2][0:NQ, 0:B], 1.0 / HD, RMS_EPS,
                                  ALU.mult, ALU.add).then_inc(ms_done, 1)

            def keep_rms(h, i):
                dve.wait_ge(rqt_done, h + 1)
                dst = rq[0:NQ, h] if isinstance(h, int) else rq[0:NQ, bass.ds(h, 1)].rearrange("p o b -> p (o b)")
                dve.tensor_scalar(dst, rqt[0:NQ, i % R], 1.0, None, ALU.mult).then_inc(rq_done, 1)

            def queries(g):
                for i in range(R):
                    h = 4 * g + i
                    for th in range(TH):
                        dve.wait_ge(sq_done, 2 * h + th + 1)
                        if not later(h, 1) and th == 0:
                            dve.wait_ge(wqk_done, 1)
                        if i == 0 and th == 0 and later(g, 1):
                            dve.wait_ge(qo_stored, 16 * g)
                        dve.tensor_scalar(qo[:, TB * th:TB * th + TB, i],
                                          ps[2 * (i % 2) + th][:, 0:TW].rearrange("p (b q) -> p b q", b=TB),
                                          wqk[:], None, ALU.mult).then_inc(qo_done, 1)
                        if th == 0 and later(h, 1):
                            mean_squares(h - 1, i + 3)
                        if th == 1 and later(h, 2):
                            keep_rms(h - 2, i + 2)
                    if not isinstance(g, int) or h + 2 < H:
                        wq_split(i % 2, h + 2)
                    if isinstance(g, int) and g == 0:
                        w_split(2 * i, 0)
                        w_split(2 * i + 1, 0)

            queries(0)
            with dve.Fori(1, G - 1) as g:
                queries(g)
            queries(G - 1)
            mean_squares(H - 1, R - 1)
            keep_rms(H - 2, R - 2)

            def kv_split(w, t):
                dve.wait_ge(kv_hi_done, w + 1)
                dve.tensor_tensor(kv_lo[:, t, :, 0:ROWS[t]], raw_tile(t), kv_hi[:, t, :, 0:ROWS[t]],
                                  ALU.subtract).then_inc(kv_lo_done, 1)

            for t in range(3):
                kv_split(t, t)
            keep_rms(H - 1, R - 1)

            def normalise_keys(s, j, par):
                u = 4 * s + j
                dve.wait_ge(rk_done, 4 * s + 4)
                dve.wait_ge(k_raw_done, 4 * s + 4)
                if later(u, 1):
                    dve.wait_ge(kt_done, u)
                dve.tensor_tensor(k_n[:], k_raw[:, par, :, j * HD:(j + 1) * HD],
                                  rk[:, par, :, j:j + 1].to_broadcast([P, KT, HD]), ALU.mult).then_inc(kn_done, 1)

            def q_split(u):
                dve.wait_ge(q_hi_done, u + 1)
                dve.tensor_tensor(q_lo[:], q_raw[:], q_hi[:], ALU.subtract).then_inc(q_lo_done, 1)

            def query_scales(s, j, half):
                u = 4 * s + j
                if later(u, 1):
                    dve.wait_ge(exp_done, 4 * u)
                elif isinstance(u, int):
                    dve.wait_ge(rq_done, H)
                h0 = R * (half * GH + j)
                if isinstance(s, int):
                    src = rq[0:NQ, h0:h0 + R, s % B]
                else:
                    src = rq[0:NQ, h0:h0 + R, bass.ds(s - B * half, 1)].rearrange("p h o -> p (h o)")
                dve.tensor_scalar(rqs[0:NQ], src, 1.0, None, ALU.mult).then_inc(rqs_done, 1)
                dve.tensor_scalar(nrq[0:NQ], src, -1.0, None, ALU.mult).then_inc(nrq_done, 1)

            def slot(s, j, par, half, attend, project):
                u, v, w = 4 * s + j, 4 * s + 4 + j, 4 * s + 7 + j
                prev = attend and later(u, 1)

                def p_split(t):
                    dve.wait_ge(pT_hi_done, 4 * (u - 1) + t + 1)
                    dve.tensor_tensor(pT_lo[0:ROWS[t], t], ps[BPT[t % 2]][0:ROWS[t], 0:QW], pT_hi[0:ROWS[t], t],
                                      ALU.subtract).then_inc(pT_lo_done, 1)

                def maxima(i):
                    a = 4 * u + i
                    dve.wait_ge(s_done, a + 1)
                    dve.tensor_reduce(mx[0:NQ, i:i + 1], ps[sbank(i, not project)][0:NQ, 0:NK], AX.X, ALU.max).then_inc(mx_done, 1)
                    if i == 0:
                        dve.wait_ge(nrq_done, u + 1)
                        dve.wait_ge(rqs_done, u + 1)
                    dve.wait_ge(mx_done, a + 1)
                    dve.tensor_tensor(nm[0:NQ, i:i + 1], mx[0:NQ, i:i + 1], nrq[0:NQ, i:i + 1], ALU.mult).then_inc(nm_done, 1)

                def scale(i):
                    a = 4 * u + i
                    dve.wait_ge(exp_done, a + 1)
                    dve.reciprocal(rr[0:NQ, i:i + 1], rs[0:NQ, i:i + 1]).then_inc(rr_done, 1)
                    dve.wait_ge(rr_done, a + 1)
                    dve.tensor_scalar(pr[0:NQ, j % 2, i], pr[0:NQ, j % 2, i], rr[0:NQ, i:i + 1], None,
                                      ALU.mult).then_inc(p_done, 1)

                if attend:
                    query_scales(s, j, half)
                    dve.wait_ge(kT_hi_done, u + 1)
                    dve.tensor_tensor(kT_lo[:], ps[BKT][:, 0:NKE], kT_hi[:], ALU.subtract).then_inc(kT_lo_done, 1)
                if isinstance(s, int) and s == B - 1 and j == 0:
                    for c in range(C):
                        w_split(c, 1)
                if attend and not project:
                    for i in range(R):
                        maxima(i)
                    if j + 1 < GH:
                        normalise_keys(s, j + 1, par)
                    for t in range(KT):
                        p_split(t)
                    for i in range(R):
                        scale(i)
                if attend and project:
                    if prev:
                        p_split(0)
                    if j + 1 < GH:
                        normalise_keys(s, j + 1, par)
                    if prev:
                        p_split(1)
                    maxima(0)
                    if prev:
                        p_split(2)
                    maxima(1)
                    scale(0)
                    if prev:
                        p_split(3)
                if project:
                    dve.wait_ge(ksq_done, v + 1)
                    if later(v, 4):
                        dve.wait_ge(msk_done, v - 3)
                    dve.tensor_reduce(ssk[:, j], ksq[:].rearrange("p (g d) -> p g d", g=GH), AX.X, ALU.add).then_inc(ssk_done, 1)
                if attend and project:
                    maxima(2)
                    scale(1)
                    maxima(3)
                    if j + 1 == GH:
                        normalise_keys(s + 1, 0, 1 - par)
                    scale(2)
                    scale(3)
                if splits(s, j):
                    kv_split(w, (j + 3) % 4)
                if attend:
                    dve.wait_ge(v_hi_done, u + 1)
                    dve.tensor_tensor(v_lo[:], v_raw[:, par, :, j * HD:(j + 1) * HD], v_hi[:], ALU.subtract).then_inc(v_lo_done, 1)
                    if j + 1 < GH or projects(s):
                        q_split(u + 1)

            for j in range(KT):
                slot(-1, j, 1, 0, False, True)
            q_split(0)
            normalise_keys(0, 0, 0)
            stages(dve, lambda s, par, half: [slot(s, j, par, half, True, projects(s)) for j in range(GH)])
            last = 4 * STAGES - 1
            for t in range(KT):
                dve.wait_ge(pT_hi_done, 4 * last + t + 1)
                dve.tensor_tensor(pT_lo[0:ROWS[t], t], ps[BPT[t % 2]][0:ROWS[t], 0:QW], pT_hi[0:ROWS[t], t],
                                  ALU.subtract).then_inc(pT_lo_done, 1)

            def chunk(th, nh, gp, k):
                m = 16 * th + 8 * nh + 2 * gp + k
                dve.wait_ge(wo_hi_done, 2 * m + 1)
                dve.tensor_tensor(wo_lo[:, k], wo_raw[:, k], wo_hi[:, k], ALU.subtract).then_inc(wo_lo_done, 1)
                dve.wait_ge(wo_hi_done, 2 * m + 2)
                dve.tensor_tensor(at_lo[:, k], at_raw[:, k], at_hi[:, k], ALU.subtract).then_inc(wo_lo_done, 1)

            def combo(th, nh):
                with dve.Fori(0, G // 2) as gp:
                    chunk(th, nh, gp, 0)
                    chunk(th, nh, gp, 1)

            def accumulators(th, nh):
                dve.wait_ge(wo_used, 16 * th + 8 * nh + 8)
                for n in (0, 1):
                    dve.tensor_copy(oT[:, 4 * nh + n], ps[n][:, 0:TW]).then_inc(oT_dve, 1)

            def residual(t):
                dve.wait_ge(t1_done, t + 1)
                dve.wait_ge(xr_in[t % 2], 16 * (t // 2 + 1))
                for n in range(2):
                    dve.scalar_tensor_tensor(out=x1[0:NQ, t % 3, n * 512:(n + 1) * 512], in0=ps[4 + n][0:NQ, :],
                                             scalar=gates_t[0:NQ, 0:1], in1=xr[0:NQ, t % 2, n * 512:(n + 1) * 512],
                                             op0=ALU.mult, op1=ALU.add).then_inc(x1_done, 1)
                for n in range(2):
                    dve.wait_ge(x1_done, 2 * t + n + 1)
                    dve.bn_stats(bn6[0:NQ, t % 2, n], x1[0:NQ, t % 3, n * 512:(n + 1) * 512]).then_inc(st2_done, 1)
                dve.wait_ge(st2_done, 2 * t + 2)
                dve.bn_aggr(mv[0:NQ, t], bn6[0:NQ, t % 2]).then_inc(ag2_done, 1)

            def norm(t):
                dve.wait_ge(rs2_done, t + 1)
                dve.wait_ge(ag2_done, t + 1)
                if t >= 2:
                    dve.wait_ge(t2_done, t - 1)
                dve.tensor_scalar(y[0:NQ, t % 2], x1[0:NQ, t % 3], mv[0:NQ, t, 0:1], mv2[0:NQ, t, 1:2],
                                  ALU.subtract, ALU.mult).then_inc(y_done, 1)

            def route(t):
                dve.wait_ge(ae_done, t + 1)
                dve.tensor_tensor(lg[0:NQ], ps[0][0:NQ, ER:AE], rowc[0:NQ, 2:2 + E], ALU.add).then_inc(lg_done, 1)
                dve.wait_ge(lg_done, t + 1)
                dve.max(top[0:NQ], lg[0:NQ]).then_inc(top_done, 1)
                dve.wait_ge(top_done, 2 * t + 1)
                dve.max_index(topi[0:NQ], top[0:NQ], lg[0:NQ]).then_inc(topi_done, 1)
                dve.tensor_scalar(ntop[0:NQ], top[0:NQ, 0:1], -1.0, None, ALU.mult).then_inc(top_done, 1)
                dve.wait_ge(topi_done, t + 1)
                dve.tensor_copy(topf[0:NQ], topi[0:NQ, 0:2]).then_inc(topf_done, 1)
                dve.wait_ge(ex_done, t + 1)
                dve.tensor_reduce(exs[0:NQ], ex[0:NQ], AX.X, ALU.add).then_inc(gate_step, 1)
                dve.wait_ge(gate_step, 5 * t + 1)
                dve.reciprocal(exr[0:NQ], exs[0:NQ]).then_inc(gate_step, 1)
                dve.wait_ge(gate_step, 5 * t + 2)
                dve.tensor_scalar(gt[0:NQ], ex[0:NQ], exr[0:NQ], None, ALU.mult).then_inc(gate_step, 1)
                dve.wait_ge(gate_step, 5 * t + 3)
                dve.wait_ge(topf_done, t + 1)
                dve.tensor_scalar(wa[0:NQ], rowc[0:NQ, 2 + E:2 + 2 * E], topf[0:NQ, 0:1], gt[0:NQ, 0:1],
                                  ALU.is_equal, ALU.mult).then_inc(gate_step, 1)
                dve.tensor_scalar(wb[0:NQ], rowc[0:NQ, 2 + E:2 + 2 * E], topf[0:NQ, 1:2], gt[0:NQ, 1:2],
                                  ALU.is_equal, ALU.mult).then_inc(gate_step, 1)
                dve.wait_ge(gate_step, 5 * t + 5)
                dve.tensor_tensor(we[0:NQ], wa[0:NQ], wb[0:NQ], ALU.add).then_inc(wsum_done, 1)
                dve.wait_ge(wsum_done, t + 1)
                if t >= 1:
                    dve.wait_ge(t3_done, t)
                dve.tensor_tensor(hw[0:NQ].rearrange("p (e r) -> p e r", e=E),
                                  ps[0][0:NQ, 0:ER].rearrange("p (e r) -> p e r", e=E),
                                  we[0:NQ].rearrange("p (e o) -> p e o", o=1).to_broadcast([NQ, E, ER // E]),
                                  ALU.mult).then_inc(hw_done, 1)

            def final(t):
                dve.wait_ge(y2_done, t + 1)
                if t == 0:
                    dve.wait_ge(cffn_done, 1)
                if t >= 2:
                    dve.wait_ge(x2_stored[t % 2], 16 * (t // 2))
                for n in range(2):
                    dve.scalar_tensor_tensor(out=x2[0:NQ, t % 2, n * 512:(n + 1) * 512], in0=ps[2 + n][0:NQ, :],
                                             scalar=cffn[0:NQ], in1=x1[0:NQ, t % 3, n * 512:(n + 1) * 512],
                                             op0=ALU.mult, op1=ALU.add).then_inc(x2_done, 1)

            def experts(t0):
                for k in range(TB + 2):
                    if k < TB:
                        residual(t0 + k)
                        norm(t0 + k)
                    if k >= 2:
                        final(t0 + k - 2)
                    if 1 <= k <= TB:
                        route(t0 + k - 1)

            combo(0, 0)
            accumulators(0, 0)
            combo(0, 1)
            accumulators(0, 1)
            experts(0)
            combo(1, 0)
            accumulators(1, 0)
            combo(1, 1)
            accumulators(1, 1)
            experts(TB)


def kernel(x, ctx_4096, g_xattn, g_ffn, L0_xattn_Wq, L0_xattn_Wk, L0_xattn_Wv, L0_xattn_Wo,
           L0_xattn_q_norm_w, L0_xattn_k_norm_w, L0_ffn_router_w, L0_ffn_router_b, L0_ffn_A, L0_ffn_Bm):
    import concourse.bacc as bacc
    from concourse.bass_utils import run_bass_kernel_spmd

    a = np.asarray
    ctxT = a(ctx_4096).transpose(0, 2, 1).reshape(B, C, P, NC).transpose(0, 2, 1, 3)
    arrays = {
        "x": a(x),
        "ctxT": np.concatenate([ctxT[..., OFF[t]:OFF[t] + ROWS[t]].reshape(B, P, C * ROWS[t]) for t in range(KT - 1)],
                               axis=-1),
        "Wq": a(L0_xattn_Wq).reshape(C, P, H, HD).transpose(2, 1, 0, 3),
        "Wkv": np.concatenate([a(w).reshape(C, P, HALVES, KW).transpose(2, 1, 0, 3)
                               for w in (L0_xattn_Wk, L0_xattn_Wv)], axis=-1),
        "Wo": a(L0_xattn_Wo).reshape(G, R, HD, 2, 512).transpose(3, 0, 2, 1, 4),
        "AR": np.concatenate([a(L0_ffn_A).reshape(ER, D), a(L0_ffn_router_w)], axis=0)
                .T.reshape(C, P, AE).transpose(1, 0, 2),
        "BmT": a(L0_ffn_Bm).transpose(0, 2, 1).reshape(ER, D),
        "vecs": np.stack([a(L0_xattn_q_norm_w), a(L0_xattn_k_norm_w)], axis=1),
        "rows": np.broadcast_to(np.concatenate([a(g_xattn), a(g_ffn), a(L0_ffn_router_b),
                                                np.arange(E, dtype=np.float32)]), (P, 2 + 2 * E)),
    }
    arrays = {k: np.ascontiguousarray(v) for k, v in arrays.items()}
    nc = bacc.Bacc("TRN2", target_bir_lowering=False, num_devices=1)
    args = [nc.dram_tensor(k, v.shape, mybir.dt.from_np(v.dtype), kind="ExternalInput").ap() for k, v in arrays.items()]
    out = nc.dram_tensor("out", (B, NQ, D), F32, kind="ExternalOutput").ap()
    build(nc, *args, out)
    return run_bass_kernel_spmd(nc, [arrays], core_ids=[0]).results[0]["out"]
```

```python
from contextlib import ExitStack

import numpy as np

import concourse.bass as bass
from concourse import mybir

F32 = mybir.dt.float32
F32R = mybir.dt.float32r
U32 = mybir.dt.uint32
ACT = mybir.ActivationFunctionType
ALU = mybir.AluOpType
AX = mybir.AxisListType

P = 128
B = 8
NQ = 100
NC = 361
NK = NC + NQ
NKE = NK + NK % 2
D = 1024
C = D // P
HD = 128
H = 32
G = 8
R = H // G
HALVES = 2
GH = G // HALVES
KT = 4
ROWS = [121, 120, 120, NQ]
OFF = [0, 121, 241, NC]
RMAX = max(ROWS)
QW = R * NQ
KW = GH * HD
STAGES = HALVES * B
TH = 2
TB = B // TH
TW = TB * NQ
E = 8
ER = 128
AE = ER + E
RMS_EPS = 1e-6
LN_EPS = 1e-5
SCALING = 8.0 / 16


def build(nc, x, ctxT, Wq, Wkv, Wo, AR, BmT, vecs, rows, out):
    with ExitStack() as ctx:
        def sem(name):
            return ctx.enter_context(nc.semaphore(name))

        def sb(stack, name, shape, dt=F32):
            return stack.enter_context(nc.sbuf_tensor(name, shape, dt))

        xnT_d = nc.dram_tensor("xnT_d", [B, P, C, NQ], F32).ap()
        q_d = nc.dram_tensor("q_d", [G, P, B, QW], F32).ap()
        at_d = nc.dram_tensor("at_d", [STAGES, GH, P, QW], F32).ap()

        ident = sb(ctx, "ident", [P, P])
        ones = sb(ctx, "ones", [P, 1])
        mhalf = sb(ctx, "mhalf", [P, E])
        qkw = sb(ctx, "qkw", [P, 2])
        wqk = sb(ctx, "wqk", [P, 1])
        rowc = sb(ctx, "rowc", [P, 2 + 2 * E])
        gates_t = sb(ctx, "gates_t", [P, 2])
        cffn = sb(ctx, "cffn", [P, 1])
        rq = sb(ctx, "rq", [P, H, B])
        bn6 = sb(ctx, "bn6", [P, 2, 2, 6])
        mv = sb(ctx, "mv", [P, B, 2])
        mv2 = sb(ctx, "mv2", [P, B, 2])
        rstd = sb(ctx, "rstd", [P, B, 2])
        ms = sb(ctx, "ms", [P, R, B])
        rqt = sb(ctx, "rqt", [P, R, B])
        epst = sb(ctx, "epst", [P, GH])
        ssk = sb(ctx, "ssk", [P, KT, GH])
        msk = sb(ctx, "msk", [P, KT, GH])
        rk = sb(ctx, "rk", [P, 2, KT, GH])
        mx = sb(ctx, "mx", [P, R])
        nm = sb(ctx, "nm", [P, R])
        rqs = sb(ctx, "rqs", [P, R])
        nrq = sb(ctx, "nrq", [P, R])
        rs = sb(ctx, "rs", [P, R])
        rr = sb(ctx, "rr", [P, R])

        with ExitStack() as a1:
            xa = sb(a1, "xa", [P, B, D])
            xT_raw = sb(a1, "xT_raw", [P, B, C, NQ])
        bst = ExitStack()
        w_hi = sb(bst, "w_hi", [P, C, 2 * KW], F32R)
        w_lo = sb(bst, "w_lo", [P, C, 2 * KW], F32R)
        kv_raw = sb(bst, "kv_raw", [P, KT, C * RMAX])
        kv_hi = sb(bst, "kv_hi", [P, KT, C, P], F32R)
        kv_lo = sb(bst, "kv_lo", [P, KT, C, P], F32R)
        with ExitStack() as a2:
            xT_hi = sb(a2, "xT_hi", [P, C, B * NQ], F32R)
            xT_lo = sb(a2, "xT_lo", [P, C, B * NQ], F32R)
            wq_raw = sb(a2, "wq_raw", [P, 2, C, HD])
            wq_hi = sb(a2, "wq_hi", [P, 2, C, HD], F32R)
            wq_lo = sb(a2, "wq_lo", [P, 2, C, HD], F32R)
            qo = sb(a2, "qo", [P, B, R, NQ])
            sq = sb(a2, "sq", [P, TH, TW])
        with ExitStack() as b2:
            k_raw = sb(b2, "k_raw", [P, 2, KT, KW])
            v_raw = sb(b2, "v_raw", [P, 2, KT, KW])
            ksq = sb(b2, "ksq", [P, KW])
            w_raw = sb(b2, "w_raw", [P, 2, 2 * KW])
            q_raw = sb(b2, "q_raw", [P, QW])
            q_hi = sb(b2, "q_hi", [P, QW], F32R)
            q_lo = sb(b2, "q_lo", [P, QW], F32R)
            k_n = sb(b2, "k_n", [P, KT, HD])
            kT_hi = sb(b2, "kT_hi", [P, NKE], F32R)
            kT_lo = sb(b2, "kT_lo", [P, NKE], F32R)
            v_hi = sb(b2, "v_hi", [P, KT, HD], F32R)
            v_lo = sb(b2, "v_lo", [P, KT, HD], F32R)
            pr = sb(b2, "pr", [P, 2, R, NK])
            pT_hi = sb(b2, "pT_hi", [P, KT, QW], F32R)
            pT_lo = sb(b2, "pT_lo", [P, KT, QW], F32R)
            ao = sb(b2, "ao", [P, 2, QW])
        with ExitStack() as c2:
            oT0 = sb(c2, "oT0", [P, C, TW])
            ar = sb(c2, "ar", [P, C, AE])
            bm = sb(c2, "bm", [P, D])
            xr = sb(c2, "xr", [P, 2, D])
            x1 = sb(c2, "x1", [P, 3, D])
            y = sb(c2, "y", [P, 2, D])
            yT = sb(c2, "yT", [P, 2, C, NQ])
            lg = sb(c2, "lg", [P, E])
            top = sb(c2, "top", [P, E])
            topi = sb(c2, "topi", [P, E], U32)
            topf = sb(c2, "topf", [P, 2])
            ntop = sb(c2, "ntop", [P, 1])
            ex = sb(c2, "ex", [P, 2])
            exs = sb(c2, "exs", [P, 1])
            exr = sb(c2, "exr", [P, 1])
            gt = sb(c2, "gt", [P, 2])
            wa = sb(c2, "wa", [P, E])
            wb = sb(c2, "wb", [P, E])
            we = sb(c2, "we", [P, E])
            hw = sb(c2, "hw", [P, ER])
            hwT = sb(c2, "hwT", [P, NQ])
            x2 = sb(c2, "x2", [P, 2, D])
        bst.close()
        c1 = ctx.enter_context(ExitStack())
        wo_raw = sb(c1, "wo_raw", [P, 2, R, 512])
        at_raw = sb(c1, "at_raw", [P, 2, TB, QW])
        wo_hi = sb(c1, "wo_hi", [P, 2, R, 512], F32R)
        wo_lo = sb(c1, "wo_lo", [P, 2, R, 512], F32R)
        at_hi = sb(c1, "at_hi", [P, 2, TB, QW], F32R)
        at_lo = sb(c1, "at_lo", [P, 2, TB, QW], F32R)
        oT1 = sb(c1, "oT1", [P, C, TW])
        oT = (oT0, oT1)

        ps = [ctx.enter_context(nc.psum_tensor(f"bank{i}", [P, 512], F32)) for i in range(8)]
        BK, BV, BS, BPT, BPV, BKT = 0, 1, (2, 3), (4, 5), 6, 7

        def sbank(i, last):
            return (BS + (BK, BV))[i] if last else BS[i % 2]

        consts_in = sem("consts_in")
        pool_consts = sem("pool_consts")
        wqk_done = sem("wqk_done")
        tanh_done = sem("tanh_done")
        cffn_done = sem("cffn_done")
        x_in = [sem(f"x_in{b}") for b in range(B)]
        stats_done = sem("stats_done")
        aggr_done = sem("aggr_done")
        var_done = sem("var_done")
        rstd_done = sem("rstd_done")
        xn_done = sem("xn_done")
        xt_done = sem("xt_done")
        xt_raw_done = sem("xt_raw_done")
        xt_hi_done = sem("xt_hi_done")
        xt_lo_done = sem("xt_lo_done")
        xnT_stored = sem("xnT_stored")
        wq_in = [sem("wq_in0"), sem("wq_in1")]
        wq_hi_done = sem("wq_hi_done")
        wq_lo_done = sem("wq_lo_done")
        q_done = sem("q_done")
        sq_done = sem("sq_done")
        qo_done = sem("qo_done")
        qo_stored = sem("qo_stored")
        ss_done = sem("ss_done")
        ms_done = sem("ms_done")
        rqt_done = sem("rqt_done")
        rq_done = sem("rq_done")
        pad_done = sem("pad_done")
        w_in = [sem("w_in0"), sem("w_in1")]
        w_hi_done = sem("w_hi_done")
        w_lo_done = sem("w_lo_done")
        kv_in = [sem(f"kv_in{t}") for t in range(KT)]
        kv_hi_done = sem("kv_hi_done")
        kv_lo_done = sem("kv_lo_done")
        k_proj_done = sem("k_proj_done")
        v_proj_done = sem("v_proj_done")
        k_raw_done = sem("k_raw_done")
        ksq_done = sem("ksq_done")
        v_raw_done = sem("v_raw_done")
        ssk_done = sem("ssk_done")
        msk_done = sem("msk_done")
        rk_done = sem("rk_done")
        kn_done = sem("kn_done")
        kt_done = sem("kt_done")
        kT_hi_done = sem("kT_hi_done")
        kT_lo_done = sem("kT_lo_done")
        q_in = sem("q_in")
        q_hi_done = sem("q_hi_done")
        q_lo_done = sem("q_lo_done")
        v_hi_done = sem("v_hi_done")
        v_lo_done = sem("v_lo_done")
        s_done = sem("s_done")
        rqs_done = sem("rqs_done")
        nrq_done = sem("nrq_done")
        mx_done = sem("mx_done")
        nm_done = sem("nm_done")
        exp_done = sem("exp_done")
        rr_done = sem("rr_done")
        p_done = sem("p_done")
        pt_done = sem("pt_done")
        pT_hi_done = sem("pT_hi_done")
        pT_lo_done = sem("pT_lo_done")
        pv_done = sem("pv_done")
        ao_done = sem("ao_done")
        ao_stored = [sem("ao_stored0"), sem("ao_stored1")]
        wo_in = [sem("wo_in0"), sem("wo_in1")]
        wo_hi_done = sem("wo_hi_done")
        wo_lo_done = sem("wo_lo_done")
        wo_used = sem("wo_used")
        o_done = sem("o_done")
        oT_act = sem("oT_act")
        oT_dve = sem("oT_dve")
        ffn_in = sem("ffn_in")
        xr_in = [sem("xr_in0"), sem("xr_in1")]
        t1_done = sem("t1_done")
        x1_done = sem("x1_done")
        st2_done = sem("st2_done")
        ag2_done = sem("ag2_done")
        va2_done = sem("va2_done")
        rs2_done = sem("rs2_done")
        y_done = sem("y_done")
        t2_done = sem("t2_done")
        yT_done = sem("yT_done")
        ae_done = sem("ae_done")
        lg_done = sem("lg_done")
        top_done = sem("top_done")
        topi_done = sem("topi_done")
        topf_done = sem("topf_done")
        ex_done = sem("ex_done")
        gate_step = sem("gate_step")
        wsum_done = sem("wsum_done")
        hw_done = sem("hw_done")
        t3_done = sem("t3_done")
        hwT_done = sem("hwT_done")
        y2_done = sem("y2_done")
        x2_done = sem("x2_done")
        x2_stored = [sem("x2_stored0"), sem("x2_stored1")]

        block = ctx.enter_context(nc.Block())

        def later(n, k):
            return not isinstance(n, int) or n >= k

        def stages(eng, stage):
            stage(0, 0, 0)
            with eng.Fori(1, 6, 2) as s:
                stage(s, 1, 0)
                stage(s + 1, 0, 0)
            stage(7, 1, 0)
            with eng.Fori(8, 13, 2) as s:
                stage(s, 0, 1)
                stage(s + 1, 1, 1)
            stage(14, 0, 1)
            stage(15, 1, 1)

        def projects(s):
            return not isinstance(s, int) or s + 1 < STAGES

        def experts_bank(t):
            return 0 if t > TB and t % 2 else 4

        def bank_user(t):
            return t - 1 if t <= TB else t - 2 if t > TB + 1 else None

        def splits(s, j):
            return not isinstance(s, int) or 4 * s + j + 7 < 4 * STAGES

        def wstage(c):
            flat = kv_raw[:].rearrange("p t k -> p (t k)")
            return flat[:, (c % 2) * 2 * KW:(c % 2 + 1) * 2 * KW]

        def raw_tile(t):
            return kv_raw[:, t, 0:C * ROWS[t]].rearrange("p (c k) -> p c k", c=C)

        @block.sync
        def _(sp):
            sp.dma_start(qkw[:], vecs).then_inc(consts_in, 16)
            sp.dma_start(rowc[:], rows).then_inc(consts_in, 16)
            for b in range(B):
                sp.dma_start(xa[0:NQ, b, :], x[b]).then_inc(x_in[b], 16)
                if b < 2:
                    sp.dma_start(wq_raw[:, b], Wq[b]).then_inc(wq_in[b], 16)
            for b in range(B):
                sp.wait_ge(xt_raw_done, b + 1)
                sp.dma_start(xnT_d[b], xT_raw[:, b]).then_inc(xnT_stored, 16)

            def queries(g):
                for i in range(R):
                    h = 4 * g + i
                    if isinstance(h, int) and h < H - 2 or not isinstance(h, int):
                        sp.wait_ge(wq_lo_done, h + 1)
                        sp.dma_start(wq_raw[:, i % 2], Wq[h + 2] if isinstance(h, int) else
                                     Wq[bass.ds(h + 2, 1)].rearrange("o p c n -> p (o c) n")).then_inc(wq_in[i % 2], 16)
                    if isinstance(g, int) and g == 0:
                        for c in (2 * i, 2 * i + 1):
                            if c >= 2:
                                sp.wait_ge(w_lo_done, c - 1)
                            sp.dma_start(wstage(c), Wkv[0, :, c]).then_inc(w_in[c % 2], 16)
                sp.wait_ge(qo_done, 8 * g + 8)
                if isinstance(g, int):
                    sp.dma_start(q_d[g], qo[:].rearrange("p b i q -> p b (i q)")).then_inc(qo_stored, 16)
                else:
                    sp.dma_start(q_d[bass.ds(g, 1)].rearrange("o p b q -> p (o b) q"),
                                 qo[:].rearrange("p b i q -> p b (i q)")).then_inc(qo_stored, 16)

            queries(0)

            def load_kv(n, t):
                if later(n, 1):
                    sp.wait_ge(kv_lo_done, 4 * (n - 1) + t + 1)
                dst = kv_raw[:, t, 0:C * ROWS[t]]
                if t < KT - 1:
                    cols = slice(C * OFF[t], C * (OFF[t] + ROWS[t]))
                    src = ctxT[n % B, :, cols] if isinstance(n, int) else \
                        ctxT[bass.ds(n % B, 1), :, cols].rearrange("o p k -> p (o k)")
                else:
                    src = xnT_d[n % B].rearrange("p c k -> p (c k)") if isinstance(n, int) else \
                        xnT_d[bass.ds(n % B, 1)].rearrange("o p c k -> p (o c k)")
                sp.dma_start(dst, src).then_inc(kv_in[t], 16)

            sp.wait_ge(w_lo_done, C)
            sp.wait_ge(xnT_stored, 16 * B)
            for t in range(KT):
                load_kv(0, t)
            with sp.Fori(1, G - 1) as g:
                queries(g)
            queries(G - 1)

            def load_q(s, j, half):
                u = 4 * s + j
                if later(u, 1):
                    sp.wait_ge(q_lo_done, u)
                else:
                    sp.wait_ge(qo_stored, 16 * G)
                if isinstance(s, int):
                    src = q_d[half * GH + j, :, s % B]
                else:
                    src = q_d[half * GH + j, :, bass.ds(s - B * half, 1)].rearrange("p o q -> p (o q)")
                sp.dma_start(q_raw[:], src).then_inc(q_in, 16)

            def store_attn(s, j):
                u = 4 * s + j
                sp.wait_ge(ao_done, u + 1)
                dst = at_d[s, j] if isinstance(s, int) else at_d[bass.ds(s, 1), j].rearrange("o p q -> p (o q)")
                sp.dma_start(dst, ao[:, j % 2]).then_inc(ao_stored[j % 2], 16)

            load_q(0, 0, 0)
            for t in range(KT):
                load_kv(1, t)

            at_g = at_d.rearrange("(h b) g p q -> h b g p q", h=HALVES)

            def chunk(th, nh, gp, k):
                m = 16 * th + 8 * nh + 2 * gp + k
                if later(m, 2):
                    sp.wait_ge(wo_lo_done, 2 * m - 2)
                if isinstance(gp, int):
                    g = 2 * gp + k
                    wsrc = Wo[nh, g]
                    asrc = at_g[g // GH, TB * th:TB * th + TB, g % GH].rearrange("b p q -> p b q")
                else:
                    wsrc = Wo[nh, bass.ds(2 * gp + k, 1)].rearrange("o p i n -> p (o i) n")
                    asrc = at_g[bass.ds(gp // 2, 1), TB * th:TB * th + TB, bass.ds(gp % 2 * 2 + k, 1)]\
                        .rearrange("h b o p q -> p (h b o) q")
                sp.dma_start(wo_raw[:, k], wsrc).then_inc(wo_in[k], 16)
                sp.dma_start(at_raw[:, k], asrc).then_inc(wo_in[k], 16)

            def stage(s, par, half):
                for j in range(GH):
                    if j == 0 and isinstance(s, int) and s == B - 1:
                        for c in range(C):
                            if c >= 2:
                                sp.wait_ge(w_lo_done, C + c - 1)
                            sp.dma_start(w_raw[:, c % 2], Wkv[1, :, c]).then_inc(w_in[c % 2], 16)
                    if splits(s, 1):
                        load_kv(s + 2, j)
                    if isinstance(s, int) and s == STAGES - 1 and j == 0:
                        sp.wait_ge(v_proj_done, 4 * STAGES)
                        sp.wait_ge(ao_stored[0], 32 * (B + TB))
                        sp.wait_ge(ao_stored[1], 32 * (B + TB))
                        chunk(0, 0, 0, 0)
                        chunk(0, 0, 0, 1)
                    if j + 1 < GH:
                        load_q(s, j + 1, half)
                    elif projects(s):
                        last_of_half = isinstance(s, int) and s == B - 1
                        load_q(s + 1, 0, 1 if last_of_half else half)
                    if j >= 1:
                        store_attn(s, j - 1)
                    elif later(s, 1):
                        store_attn(s - 1, GH - 1)

            stages(sp, stage)

            chunk(0, 0, 1, 0)
            chunk(0, 0, 1, 1)
            sp.wait_ge(ao_done, 4 * STAGES)
            sp.dma_start(at_d[STAGES - 1, GH - 1], ao[:, 1]).then_inc(ao_stored[1], 16)

            def load_x(t):
                sp.dma_start(xr[0:NQ, t % 2], x[t]).then_inc(xr_in[t % 2], 16)

            def store(t):
                sp.wait_ge(x2_done, 2 * t + 2)
                sp.dma_start(out[t], x2[0:NQ, t % 2]).then_inc(x2_stored[t % 2], 16)

            with sp.Fori(2, G // 2) as gp:
                chunk(0, 0, gp, 0)
                chunk(0, 0, gp, 1)
            sp.wait_ge(ao_stored[0], 16 * 2 * STAGES)
            sp.wait_ge(ao_stored[1], 16 * 2 * STAGES)
            sp.dma_start(ar[:], AR).then_inc(ffn_in, 16)
            sp.dma_start(bm[:], BmT).then_inc(ffn_in, 16)
            load_x(0)
            load_x(1)
            with sp.Fori(0, G // 2) as gp:
                chunk(0, 1, gp, 0)
                chunk(0, 1, gp, 1)
            for c in range(2 * G):
                t = c // 4
                chunk(1, c // G, c % G // 2, c % 2)
                if c % 4 == 0 and t >= 1:
                    sp.wait_ge(x1_done, 2 * t)
                    load_x(t + 1)
                if c % 4 == 3 and t >= 1:
                    store(t - 1)
            for t in range(TB - 1, B):
                if t + 2 < B:
                    sp.wait_ge(x1_done, 2 * t + 2)
                    load_x(t + 2)
                if t != TB:
                    store(t if t < TB else t - 1)
            store(B - 1)
            sp.wait_ge(x2_stored[0], 16 * B // 2)
            sp.wait_ge(x2_stored[1], 16 * B // 2)

        @block.gpsimd
        def _(pool):
            pool.memset(ident[:], 0.0).then_inc(pool_consts, 1)
            pool.memset(ones[:], 1.0).then_inc(pool_consts, 1)
            pool.memset(mhalf[:], -0.5).then_inc(pool_consts, 1)
            pool.memset(epst[:], RMS_EPS).then_inc(pool_consts, 1)
            pool.wait_ge(pool_consts, 4)
            pool.affine_select(out=ident[:], in_=ident[:], compare_op=ALU.not_equal, fill=1.0, base=0,
                               pattern=[[-1, P]], channel_multiplier=1).then_inc(pool_consts, 1)
            for b in range(B):
                pool.wait_ge(aggr_done, b + 1)
                pool.tensor_scalar(rstd[0:NQ, b, 0:1], mv[0:NQ, b, 1:2], 1.0, LN_EPS, ALU.mult, ALU.add).then_inc(var_done, 1)
                pool.wait_ge(var_done, b + 1)
                pool.tensor_tensor(rstd[0:NQ, b, 1:2], rstd[0:NQ, b, 0:1], mhalf[0:NQ, 0:1], ALU.pow).then_inc(rstd_done, 1)

            def head_rms(g):
                for i in range(R):
                    if later(g, 1):
                        pool.wait_ge(rq_done, 4 * g + i - 3)
                    pool.wait_ge(ms_done, 4 * g + i + 1)
                    pool.tensor_tensor(rqt[0:NQ, i, :], ms[0:NQ, i, :], mhalf[0:NQ, 0:B], ALU.pow).then_inc(rqt_done, 1)

            head_rms(0)
            with pool.Fori(1, G) as g:
                head_rms(g)

            def key_rms(n, par):
                for t in range(KT):
                    v = 4 * n + t
                    pool.wait_ge(ssk_done, v + 1)
                    pool.tensor_tensor(msk[:, t, :], ssk[:, t, :], epst[:], ALU.add).then_inc(msk_done, 1)
                    if t == 0 and later(n, 2):
                        pool.wait_ge(kn_done, 4 * (n - 1))
                    pool.wait_ge(msk_done, v + 1)
                    pool.tensor_tensor(rk[:, par, t, :], msk[:, t, :], mhalf[:, 0:GH], ALU.pow).then_inc(rk_done, 1)

            key_rms(0, 0)
            key_rms(1, 1)
            with pool.Fori(2, STAGES - 1, 2) as n:
                key_rms(n, 0)
                key_rms(n + 1, 1)
            for t in range(B):
                pool.wait_ge(ag2_done, t + 1)
                pool.tensor_scalar(mv2[0:NQ, t, 0:1], mv[0:NQ, t, 1:2], 1.0, LN_EPS, ALU.mult, ALU.add).then_inc(va2_done, 1)
                pool.wait_ge(va2_done, t + 1)
                pool.tensor_tensor(mv2[0:NQ, t, 1:2], mv2[0:NQ, t, 0:1], mhalf[0:NQ, 0:1], ALU.pow).then_inc(rs2_done, 1)

        @block.tensor
        def _(pe):
            def three(o, lh, ll, rh, rl, start, stop):
                pe.matmul(o, lh, rh, start=start, stop=False)
                pe.matmul(o, lh, rl, start=False, stop=False)
                return pe.matmul(o, ll, rh, start=False, stop=stop)

            pe.wait_ge(pool_consts, 5)
            for b in range(B):
                pe.wait_ge(xn_done, b + 1)
                if b >= 2:
                    pe.wait_ge(xt_raw_done, b - 1)
                for c in range(C):
                    bank = ps[4 + 2 * (b % 2) + c // 4]
                    mm = pe.transpose(bank[:, (c % 4) * NQ:(c % 4 + 1) * NQ], xa[0:NQ, b, c * P:(c + 1) * P],
                                      ident[0:NQ, 0:NQ])
                mm.then_inc(xt_done, 1)

            def squares(h, th, i):
                pe.wait_ge(sq_done, 2 * h + th + 1)
                if th == 0 and later(h, 2):
                    pe.wait_ge(ms_done, h - 1)
                for b in range(TB):
                    mm = pe.matmul(ps[4 + i % 2][0:NQ, TB * th + b:TB * th + b + 1],
                                   sq[:, th, b * NQ:(b + 1) * NQ], ones[:], start=True, stop=True)
                mm.then_inc(ss_done, 1)

            def queries(g):
                for i in range(R):
                    h = 4 * g + i
                    pe.wait_ge(wq_lo_done, h + 1)
                    for th in range(TH):
                        if isinstance(g, int) and g == 0 and i == 0:
                            pe.wait_ge(xt_lo_done, TB * (th + 1))
                        if later(h, 2):
                            pe.wait_ge(qo_done, 2 * (h - 2) + th + 1)
                        o = ps[2 * (i % 2) + th][:, 0:TW]
                        for c in range(C):
                            mm = three(o, wq_hi[:, i % 2, c], wq_lo[:, i % 2, c],
                                       xT_hi[:, c, th * TW:(th + 1) * TW], xT_lo[:, c, th * TW:(th + 1) * TW],
                                       c == 0, c == C - 1)
                        mm.then_inc(q_done, 1)
                        if th == 0 and later(h, 1):
                            squares(h - 1, 1, i + 1)
                        if th == 1:
                            squares(h, 0, i)

            queries(0)
            with pe.Fori(1, G) as g:
                queries(g)
            squares(H - 1, 1, R - 1)

            def proj_chunk(s, j, half, n):
                v = 4 * s + 4 + j
                isv, cc = n // 4, 2 * (n % 4)
                if n == 0:
                    pe.wait_ge(kv_lo_done, v + 1)
                    if later(v, 1):
                        pe.wait_ge(ksq_done, v)
                if n == 4 and later(v, 1):
                    pe.wait_ge(v_raw_done, v)
                for c in (cc, cc + 1):
                    if j == 0 and isv == 0:
                        pe.wait_ge(w_lo_done, C * half + c + 1)
                    mm = three(ps[BV if isv else BK][:, 0:KW], kv_hi[:, j, c], kv_lo[:, j, c],
                               w_hi[:, c, isv * KW:(isv + 1) * KW], w_lo[:, c, isv * KW:(isv + 1) * KW],
                               c == 0, c == C - 1)
                if n == 3:
                    mm.then_inc(k_proj_done, 1)
                if n == 7:
                    mm.then_inc(v_proj_done, 1)

            def turn_keys(u):
                pe.wait_ge(kn_done, u + 1)
                if later(u, 1):
                    pe.wait_ge(kT_lo_done, u)
                for t in range(KT):
                    r = ROWS[t] + (NKE - NK if t == KT - 1 else 0)
                    mm = pe.transpose(ps[BKT][:, OFF[t]:OFF[t] + r], k_n[0:r, t, :], ident[0:r, 0:r])
                mm.then_inc(kt_done, 1)

            def scores(u, i, last=False):
                if i == 0:
                    pe.wait_ge(kT_lo_done, u + 1)
                    pe.wait_ge(q_lo_done, u + 1)
                a = 4 * u + i
                if last and u > 4 * (STAGES - 1):
                    pe.wait_ge(exp_done, a - 3)
                elif last and i >= 2:
                    pe.wait_ge(v_raw_done, u)
                    pe.wait_ge(ksq_done, u)
                elif later(a, 2):
                    pe.wait_ge(exp_done, a - 1)
                three(ps[sbank(i, last)][0:NQ, 0:NKE], q_hi[:, i * NQ:(i + 1) * NQ], q_lo[:, i * NQ:(i + 1) * NQ],
                      kT_hi[:], kT_lo[:], True, True).then_inc(s_done, 1)

            def turn_probs(u, par, t):
                if t == 0:
                    pe.wait_ge(p_done, 4 * u + 4)
                a = 4 * u + t
                if later(a, 2):
                    pe.wait_ge(pT_lo_done, a - 1)
                for i in range(R):
                    mm = pe.transpose(ps[BPT[t % 2]][0:ROWS[t], i * NQ:(i + 1) * NQ],
                                      pr[0:NQ, par, i, OFF[t]:OFF[t] + ROWS[t]], ident[0:NQ, 0:NQ])
                mm.then_inc(pt_done, 1)

            def values(u, t):
                pe.wait_ge(pT_lo_done, 4 * u + t + 1)
                if t == 0:
                    pe.wait_ge(v_lo_done, u + 1)
                    if later(u, 1):
                        pe.wait_ge(ao_done, u)
                r = ROWS[t]
                mm = three(ps[BPV][:, 0:QW], v_hi[0:r, t], v_lo[0:r, t], pT_hi[0:r, t], pT_lo[0:r, t],
                           t == 0, t == KT - 1)
                if t == KT - 1:
                    mm.then_inc(pv_done, 1)

            def slot(s, j, half, attend, project):
                u = 4 * s + j
                prev = attend and later(u, 1)
                par = (j + 1) % 2
                nhalf = 1 if isinstance(s, int) and s == B - 1 else half

                def c_(n):
                    if project:
                        proj_chunk(s, j, nhalf, n)
                if attend and not project:
                    turn_keys(u)
                    for i in range(R):
                        scores(u, i, last=True)
                    for t in range(KT + 1):
                        if t < KT:
                            turn_probs(u - 1, par, t)
                        if t:
                            values(u - 1, t - 1)
                    return
                new_weights = isinstance(s, int) and s == B - 1 and j == 0
                if not new_weights:
                    c_(0)
                if attend:
                    turn_keys(u)
                if prev:
                    turn_probs(u - 1, par, 0)
                if new_weights:
                    turn_probs(u - 1, par, 1)
                    c_(0)
                c_(1)
                if prev and not new_weights:
                    turn_probs(u - 1, par, 1)
                c_(2)
                if attend:
                    scores(u, 0)
                if prev:
                    values(u - 1, 0)
                    turn_probs(u - 1, par, 2)
                c_(3)
                if attend:
                    scores(u, 1)
                if prev:
                    values(u - 1, 1)
                    turn_probs(u - 1, par, 3)
                c_(4)
                if attend:
                    scores(u, 2)
                if prev:
                    values(u - 1, 2)
                c_(5)
                if attend:
                    scores(u, 3)
                if prev:
                    values(u - 1, 3)
                c_(6)
                c_(7)

            pe.wait_ge(qo_done, 2 * H)
            for j in range(KT):
                slot(-1, j, 0, False, True)
            pe.wait_ge(rq_done, H)
            stages(pe, lambda s, par, half: [slot(s, j, half, True, projects(s)) for j in range(GH)])
            last = 4 * STAGES - 1
            for t in range(KT):
                turn_probs(last, 1, t)
                if t:
                    values(last, t - 1)
            values(last, KT - 1)

            def chunk(th, nh, gp, k, first=False, last=False, between=None):
                m = 16 * th + 8 * nh + 2 * gp + k
                pe.wait_ge(wo_lo_done, 2 * m + 2)
                for i in range(R):
                    for n in range(4):
                        mm = three(ps[n][:, 0:TW].rearrange("p (b q) -> p b q", b=TB),
                                   wo_hi[:, k, i, n * P:(n + 1) * P], wo_lo[:, k, i, n * P:(n + 1) * P],
                                   at_hi[:, k, :, i * NQ:(i + 1) * NQ], at_lo[:, k, :, i * NQ:(i + 1) * NQ],
                                   first and i == 0, last and i == R - 1)
                    if between and i == R // 2 - 1:
                        between()
                mm.then_inc(wo_used, 1)

            def accumulators_free(th, nh):
                m = 2 * (2 * th + nh)
                pe.wait_ge(oT_dve, m)
                pe.wait_ge(oT_act, m)

            def turn_out(t):
                e, prev = experts_bank(t), bank_user(t)
                if t % TB == 0:
                    accumulators_free(t // TB + 1, 0)
                if t and prev is not None:
                    pe.wait_ge(hw_done, prev + 1)
                    pe.wait_ge(hwT_done, prev + 1)
                for c in range(C):
                    mm = pe.transpose(ps[e + c // 4][0:NQ, (c % 4) * P:(c % 4 + 1) * P],
                                      oT[t // TB][:, c, (t % TB) * NQ:(t % TB + 1) * NQ], ident[:])
                mm.then_inc(t1_done, 1)

            def turn_y(t):
                e, prev = experts_bank(t), bank_user(t)
                pe.wait_ge(y_done, t + 1)
                if t and prev is not None:
                    pe.wait_ge(x2_done, 2 * prev + 2)
                for c in range(C):
                    mm = pe.transpose(ps[e + 2 + c // 4][:, (c % 4) * NQ:(c % 4 + 1) * NQ],
                                      y[0:NQ, t % 2, c * P:(c + 1) * P], ident[0:NQ, 0:NQ])
                mm.then_inc(t2_done, 1)

            def low_rank(t):
                pe.wait_ge(yT_done, 2 * t + 2)
                if t == 0:
                    pe.wait_ge(ffn_in, 32)
                pe.wait_ge(x1_done, 2 * t + 2)
                for c in range(C):
                    mm = pe.matmul(ps[experts_bank(t)][0:NQ, 0:AE], yT[:, t % 2, c], ar[:, c],
                                   start=(c == 0), stop=(c == C - 1))
                mm.then_inc(ae_done, 1)

            def turn_h(t):
                pe.wait_ge(hw_done, t + 1)
                pe.transpose(ps[experts_bank(t) + 1][:, 0:NQ], hw[0:NQ], ident[0:NQ, 0:NQ]).then_inc(t3_done, 1)

            def up(t):
                pe.wait_ge(hwT_done, t + 1)
                e = experts_bank(t) + 2
                pe.matmul(ps[e][0:NQ, :], hwT[:], bm[:, 0:512], start=True, stop=True)
                pe.matmul(ps[e + 1][0:NQ, :], hwT[:], bm[:, 512:1024], start=True, stop=True).then_inc(y2_done, 1)

            for nh in range(2):
                if nh:
                    accumulators_free(0, nh)
                chunk(0, nh, 0, 0, first=True)
                chunk(0, nh, 0, 1)
                with pe.Fori(1, G // 2 - 1) as gp:
                    chunk(0, nh, gp, 0)
                    chunk(0, nh, gp, 1)
                chunk(0, nh, G // 2 - 1, 0)
                chunk(0, nh, G // 2 - 1, 1, last=True)
            for c in range(2 * G):
                t = c // 4
                if c % G == 0:
                    accumulators_free(1, c // G)
                chunk(1, c // G, c % G // 2, c % 2, first=c % G == 0, last=c % G == G - 1,
                      between=(lambda: up(t - 1)) if c % 4 == 0 and t else None)
                (turn_out, turn_y, low_rank, turn_h)[c % 4](t)
            up(TB - 1)
            a, b = TB, TB + 1
            turn_out(a)
            turn_out(b)
            turn_y(a)
            turn_y(b)
            low_rank(a)
            low_rank(b)
            turn_h(a)
            up(a)
            turn_out(a + 2)
            turn_h(b)
            up(b)
            turn_out(b + 2)
            turn_y(a + 2)
            turn_y(b + 2)
            low_rank(a + 2)
            low_rank(b + 2)
            turn_h(a + 2)
            up(a + 2)
            turn_h(b + 2)
            up(b + 2)

        @block.scalar
        def _(act):
            act.wait_ge(consts_in, 32)
            act.activation(gates_t[:], rowc[:, 0:2], ACT.Tanh).then_inc(tanh_done, 1)

            def wq_split(g, i):
                k, h = i % 2, 4 * g + i
                act.wait_ge(wq_in[k], 16 * (2 * g + i // 2 + 1))
                if later(h, 2):
                    act.wait_ge(q_done, 2 * (h - 2) + 2)
                act.activation(wq_hi[:, k], wq_raw[:, k], ACT.Copy).then_inc(wq_hi_done, 1)

            wq_split(0, 0)
            wq_split(0, 1)
            for b in range(B):
                act.wait_ge(xt_done, b + 1)
                for n in range(2):
                    ins = act.activation(xT_raw[:, b, 4 * n:4 * n + 4].rearrange("p c q -> p (c q)"),
                                         ps[4 + 2 * (b % 2) + n][:, 0:4 * NQ], ACT.Copy)
                ins.then_inc(xt_raw_done, 1)
                act.wait_ge(xt_raw_done, b + 1)
                act.activation(xT_hi[:, :, b * NQ:(b + 1) * NQ], xT_raw[:, b], ACT.Copy).then_inc(xt_hi_done, 1)

            def w_split(c, half):
                act.wait_ge(w_in[c % 2], 16 * (C // 2 * half + c // 2 + 1))
                if half == 0:
                    if c == 0:
                        act.wait_ge(xt_lo_done, B)
                        act.wait_ge(xnT_stored, 16 * B)
                elif c == 0:
                    act.wait_ge(v_proj_done, 4 * B)
                act.activation(w_hi[:, c], wstage(c) if half == 0 else w_raw[:, c % 2], ACT.Copy).then_inc(w_hi_done, 1)

            def queries(g):
                for i in range(R):
                    h = 4 * g + i
                    for th in range(TH):
                        act.wait_ge(q_done, 2 * h + th + 1)
                        if later(h, 1):
                            act.wait_ge(ss_done, 2 * (h - 1) + th + 1)
                        act.activation(sq[:, th], ps[2 * (i % 2) + th][:, 0:TW], ACT.Square).then_inc(sq_done, 1)
                    if not isinstance(g, int) or h + 2 < H:
                        wq_split(g, i + 2)
                    if isinstance(g, int) and g == 0:
                        w_split(2 * i, 0)
                        w_split(2 * i + 1, 0)

            queries(0)
            with act.Fori(1, G - 1) as g:
                queries(g)
            queries(G - 1)

            def kv_split(n, t):
                w = 4 * n + t
                act.wait_ge(kv_in[t], 16 * (n + 1))
                if later(w, 4):
                    act.wait_ge(v_proj_done, w - 3)
                act.activation(kv_hi[:, t, :, 0:ROWS[t]], raw_tile(t), ACT.Copy).then_inc(kv_hi_done, 1)

            act.wait_ge(pad_done, 1)
            for t in range(3):
                kv_split(0, t)

            def q_split(u):
                act.wait_ge(q_in, 16 * (u + 1))
                if later(u, 1):
                    act.wait_ge(s_done, 4 * u)
                act.activation(q_hi[:], q_raw[:], ACT.Copy).then_inc(q_hi_done, 1)

            def chunk_weights(th, nh, gp, k):
                m = 16 * th + 8 * nh + 2 * gp + k
                act.wait_ge(wo_in[k], 32 * (8 * th + 4 * nh + gp + 1))
                if later(m, 2):
                    act.wait_ge(wo_used, m - 1)
                act.activation(wo_hi[:, k], wo_raw[:, k], ACT.Copy).then_inc(wo_hi_done, 1)

            def chunk_heads(k):
                act.activation(at_hi[:, k], at_raw[:, k], ACT.Copy).then_inc(wo_hi_done, 1)

            def chunk(th, nh, gp, k):
                chunk_weights(th, nh, gp, k)
                chunk_heads(k)

            def slot(s, j, par, half, attend, project):
                u, v = 4 * s + j, 4 * s + 4 + j
                prev = attend and later(u, 1)

                def p_split(t):
                    act.wait_ge(pt_done, 4 * (u - 1) + t + 1)
                    act.activation(pT_hi[0:ROWS[t], t], ps[BPT[t % 2]][0:ROWS[t], 0:QW], ACT.Copy).then_inc(pT_hi_done, 1)

                def exps(i):
                    a = 4 * u + i
                    act.wait_ge(nm_done, a + 1)
                    if i == 0 and later(u, 2):
                        act.wait_ge(pt_done, 4 * (u - 1))
                    act.activation(pr[0:NQ, j % 2, i], ps[sbank(i, not project)][0:NQ, 0:NK], ACT.Exp, bias=nm[0:NQ, i:i + 1],
                                   scale=rqs[0:NQ, i:i + 1], accum_out=rs[0:NQ, i:i + 1]).then_inc(exp_done, 1)

                if attend:
                    act.wait_ge(kt_done, u + 1)
                    act.activation(kT_hi[:], ps[BKT][:, 0:NKE], ACT.Copy).then_inc(kT_hi_done, 1)
                if isinstance(s, int) and s == B - 1 and j == 0:
                    for c in range(C):
                        w_split(c, 1)
                if attend and not project:
                    exps(0)
                    exps(1)
                    exps(2)
                    p_split(0)
                    exps(3)
                    p_split(1)
                    p_split(2)
                    p_split(3)
                if attend and project:
                    if prev:
                        p_split(0)
                        p_split(1)
                    exps(0)
                    if prev:
                        p_split(2)
                if project:
                    act.wait_ge(k_proj_done, v + 1)
                    if j == 0 and later(s, 1):
                        act.wait_ge(kn_done, 4 * s)
                    act.activation(k_raw[:, 1 - par, j], ps[BK][:, 0:KW], ACT.Copy).then_inc(k_raw_done, 1)
                    if later(v, 1):
                        act.wait_ge(ssk_done, v)
                    act.activation(ksq[:], ps[BK][:, 0:KW], ACT.Square, scale=float(HD) ** -0.5).then_inc(ksq_done, 1)
                if attend and project:
                    exps(1)
                    if prev:
                        p_split(3)
                    exps(2)
                    exps(3)
                if prev:
                    act.wait_ge(pv_done, u)
                    if later(u, 3):
                        act.wait_ge(ao_stored[1 - j % 2], 16 * (2 * s + (-1, 0, 0, 1)[j]))
                    act.activation(ao[:, 1 - j % 2], ps[BPV][:, 0:QW], ACT.Copy).then_inc(ao_done, 1)
                if splits(s, j):
                    kv_split(s + 1 if j == 0 else s + 2, (j + 3) % 4)
                if attend:
                    act.wait_ge(v_raw_done, 4 * s + 4)
                    if prev:
                        act.wait_ge(pv_done, u)
                    act.activation(v_hi[:], v_raw[:, par, :, j * HD:(j + 1) * HD], ACT.Copy).then_inc(v_hi_done, 1)
                    if j + 1 < GH or projects(s):
                        q_split(u + 1)
                if attend and not project and 1 <= j < 3:
                    chunk(0, 0, 0, j - 1)
                if project:
                    act.wait_ge(v_proj_done, v + 1)
                    if j == 0 and later(s, 1):
                        act.wait_ge(v_lo_done, 4 * s)
                    act.activation(v_raw[:, 1 - par, j], ps[BV][:, 0:KW], ACT.Copy).then_inc(v_raw_done, 1)

            for j in range(KT):
                slot(-1, j, 1, 0, False, True)
            q_split(0)
            stages(act, lambda s, par, half: [slot(s, j, par, half, True, projects(s)) for j in range(GH)])
            last = 4 * STAGES - 1
            for t in range(KT):
                act.wait_ge(pt_done, 4 * last + t + 1)
                act.activation(pT_hi[0:ROWS[t], t], ps[BPT[t % 2]][0:ROWS[t], 0:QW], ACT.Copy).then_inc(pT_hi_done, 1)
            act.wait_ge(pv_done, last + 1)
            act.wait_ge(ao_stored[1], 16 * (2 * STAGES - 1))
            act.activation(ao[:, 1], ps[BPV][:, 0:QW], ACT.Copy).then_inc(ao_done, 1)

            def accumulators(th, nh):
                act.wait_ge(wo_used, 16 * th + 8 * nh + 8)
                for n in (2, 3):
                    act.activation(oT[th][:, 4 * nh + n], ps[n][:, 0:TW], ACT.Copy).then_inc(oT_act, 1)

            def turned_y(t):
                act.wait_ge(t2_done, t + 1)
                if t >= 2:
                    act.wait_ge(ae_done, t - 1)
                for n in range(2):
                    act.activation(yT[:, t % 2, 4 * n:4 * n + 4].rearrange("p c q -> p (c q)"), ps[experts_bank(t) + 2 + n][:, 0:4 * NQ],
                                   ACT.Copy).then_inc(yT_done, 1)

            def exps2(t):
                act.wait_ge(top_done, 2 * t + 2)
                if t >= 1:
                    act.wait_ge(gate_step, 5 * t)
                act.activation(ex[0:NQ], top[0:NQ, 0:2], ACT.Exp, bias=ntop[0:NQ]).then_inc(ex_done, 1)

            def turned_h(t):
                act.wait_ge(t3_done, t + 1)
                if t >= 1:
                    act.wait_ge(y2_done, t)
                act.activation(hwT[:], ps[experts_bank(t) + 1][:, 0:NQ], ACT.Copy).then_inc(hwT_done, 1)

            for nh in range(2):
                with act.Fori(1, G // 2) as gp:
                    chunk(0, nh, gp, 0)
                    chunk(0, nh, gp, 1)
                chunk(nh, 1 - nh, 0, 0)
                accumulators(0, nh)
                if nh == 0:
                    chunk(0, 1, 0, 1)
            for c in range(2 * G):
                t, n = c // 4, c + 1
                if c % 4 == 0 and t:
                    turned_h(t - 1)
                if n < 2 * G:
                    chunk_weights(1, n // G, n % G // 2, n % 2)
                if c % 4 == 3:
                    exps2(t)
                if n < 2 * G:
                    chunk_heads(n % 2)
                if c % 4 == 2:
                    turned_y(t)
                if c % G == G - 1:
                    accumulators(1, c // G)
            turned_h(TB - 1)
            for t in (TB, TB + 2):
                turned_y(t)
                turned_y(t + 1)
                exps2(t)
                turned_h(t)
                exps2(t + 1)
                turned_h(t + 1)

        @block.vector
        def _(dve):
            dve.wait_ge(consts_in, 32)
            dve.scalar_tensor_tensor(out=wqk[:], in0=qkw[:, 0:1], scalar=float(HD) ** -0.5, in1=qkw[:, 1:2],
                                     op0=ALU.mult, op1=ALU.mult).then_inc(wqk_done, 1)
            dve.wait_ge(tanh_done, 1)
            dve.tensor_scalar(cffn[:], gates_t[:, 1:2], SCALING, None, ALU.mult).then_inc(cffn_done, 1)

            def wq_split(k, h):
                dve.wait_ge(wq_hi_done, h + 1)
                dve.tensor_tensor(wq_lo[:, k], wq_raw[:, k], wq_hi[:, k], ALU.subtract).then_inc(wq_lo_done, 1)

            def stats(b):
                dve.wait_ge(x_in[b], 16)
                for n in range(2):
                    dve.bn_stats(bn6[0:NQ, b % 2, n], xa[0:NQ, b, n * 512:(n + 1) * 512]).then_inc(stats_done, 1)
                dve.wait_ge(stats_done, 2 * b + 2)
                dve.bn_aggr(mv[0:NQ, b], bn6[0:NQ, b % 2]).then_inc(aggr_done, 1)

            for t in range(KT):
                dve.memset(kv_hi[:, t, :, ROWS[t]:P].bitcast(U32), 0)
                ins = dve.memset(kv_lo[:, t, :, ROWS[t]:P].bitcast(U32), 0)
            ins.then_inc(pad_done, 1)

            def latent_split(b):
                dve.wait_ge(xt_hi_done, b + 1)
                dve.tensor_tensor(xT_lo[:, :, b * NQ:(b + 1) * NQ], xT_raw[:, b], xT_hi[:, :, b * NQ:(b + 1) * NQ],
                                  ALU.subtract).then_inc(xt_lo_done, 1)

            stats(0)
            for b in range(B):
                if b + 1 < B:
                    stats(b + 1)
                dve.wait_ge(aggr_done, b + 1)
                dve.wait_ge(rstd_done, b + 1)
                dve.tensor_scalar(xa[0:NQ, b], xa[0:NQ, b], mv[0:NQ, b, 0:1], rstd[0:NQ, b, 1:2],
                                  ALU.subtract, ALU.mult).then_inc(xn_done, 1)
                if b == 1:
                    wq_split(0, 0)
                    wq_split(1, 1)
                if b >= 1:
                    latent_split(b - 1)
            latent_split(B - 1)

            def w_split(c, half):
                dve.wait_ge(w_hi_done, C * half + c + 1)
                src = wstage(c) if half == 0 else w_raw[:, c % 2]
                dve.tensor_tensor(w_lo[:, c], src, w_hi[:, c], ALU.subtract).then_inc(w_lo_done, 1)

            def mean_squares(h, i):
                dve.wait_ge(ss_done, 2 * h + 2)
                if later(h, 4):
                    dve.wait_ge(rqt_done, h - 3)
                dve.tensor_scalar(ms[0:NQ, i % R], ps[4 + i % 2][0:NQ, 0:B], 1.0 / HD, RMS_EPS,
                                  ALU.mult, ALU.add).then_inc(ms_done, 1)

            def keep_rms(h, i):
                dve.wait_ge(rqt_done, h + 1)
                dst = rq[0:NQ, h] if isinstance(h, int) else rq[0:NQ, bass.ds(h, 1)].rearrange("p o b -> p (o b)")
                dve.tensor_scalar(dst, rqt[0:NQ, i % R], 1.0, None, ALU.mult).then_inc(rq_done, 1)

            def queries(g):
                for i in range(R):
                    h = 4 * g + i
                    for th in range(TH):
                        dve.wait_ge(sq_done, 2 * h + th + 1)
                        if not later(h, 1) and th == 0:
                            dve.wait_ge(wqk_done, 1)
                        if i == 0 and th == 0 and later(g, 1):
                            dve.wait_ge(qo_stored, 16 * g)
                        dve.tensor_scalar(qo[:, TB * th:TB * th + TB, i],
                                          ps[2 * (i % 2) + th][:, 0:TW].rearrange("p (b q) -> p b q", b=TB),
                                          wqk[:], None, ALU.mult).then_inc(qo_done, 1)
                        if th == 0 and later(h, 1):
                            mean_squares(h - 1, i + 3)
                        if th == 1 and later(h, 2):
                            keep_rms(h - 2, i + 2)
                    if not isinstance(g, int) or h + 2 < H:
                        wq_split(i % 2, h + 2)
                    if isinstance(g, int) and g == 0:
                        w_split(2 * i, 0)
                        w_split(2 * i + 1, 0)

            queries(0)
            with dve.Fori(1, G - 1) as g:
                queries(g)
            queries(G - 1)
            mean_squares(H - 1, R - 1)
            keep_rms(H - 2, R - 2)

            def kv_split(w, t):
                dve.wait_ge(kv_hi_done, w + 1)
                dve.tensor_tensor(kv_lo[:, t, :, 0:ROWS[t]], raw_tile(t), kv_hi[:, t, :, 0:ROWS[t]],
                                  ALU.subtract).then_inc(kv_lo_done, 1)

            for t in range(3):
                kv_split(t, t)
            keep_rms(H - 1, R - 1)

            def normalise_keys(s, j, par):
                u = 4 * s + j
                dve.wait_ge(rk_done, 4 * s + 4)
                dve.wait_ge(k_raw_done, 4 * s + 4)
                if later(u, 1):
                    dve.wait_ge(kt_done, u)
                dve.tensor_tensor(k_n[:], k_raw[:, par, :, j * HD:(j + 1) * HD],
                                  rk[:, par, :, j:j + 1].to_broadcast([P, KT, HD]), ALU.mult).then_inc(kn_done, 1)

            def q_split(u):
                dve.wait_ge(q_hi_done, u + 1)
                dve.tensor_tensor(q_lo[:], q_raw[:], q_hi[:], ALU.subtract).then_inc(q_lo_done, 1)

            def query_scales(s, j, half):
                u = 4 * s + j
                if later(u, 1):
                    dve.wait_ge(exp_done, 4 * u)
                elif isinstance(u, int):
                    dve.wait_ge(rq_done, H)
                h0 = R * (half * GH + j)
                if isinstance(s, int):
                    src = rq[0:NQ, h0:h0 + R, s % B]
                else:
                    src = rq[0:NQ, h0:h0 + R, bass.ds(s - B * half, 1)].rearrange("p h o -> p (h o)")
                dve.tensor_scalar(rqs[0:NQ], src, 1.0, None, ALU.mult).then_inc(rqs_done, 1)
                dve.tensor_scalar(nrq[0:NQ], src, -1.0, None, ALU.mult).then_inc(nrq_done, 1)

            def chunk_weights(th, nh, gp, k):
                m = 16 * th + 8 * nh + 2 * gp + k
                dve.wait_ge(wo_hi_done, 2 * m + 1)
                dve.tensor_tensor(wo_lo[:, k], wo_raw[:, k], wo_hi[:, k], ALU.subtract).then_inc(wo_lo_done, 1)

            def chunk_heads(th, nh, gp, k):
                m = 16 * th + 8 * nh + 2 * gp + k
                dve.wait_ge(wo_hi_done, 2 * m + 2)
                dve.tensor_tensor(at_lo[:, k], at_raw[:, k], at_hi[:, k], ALU.subtract).then_inc(wo_lo_done, 1)

            def chunk(th, nh, gp, k):
                chunk_weights(th, nh, gp, k)
                chunk_heads(th, nh, gp, k)

            def slot(s, j, par, half, attend, project):
                u, v, w = 4 * s + j, 4 * s + 4 + j, 4 * s + 7 + j
                prev = attend and later(u, 1)

                def p_split(t):
                    dve.wait_ge(pT_hi_done, 4 * (u - 1) + t + 1)
                    dve.tensor_tensor(pT_lo[0:ROWS[t], t], ps[BPT[t % 2]][0:ROWS[t], 0:QW], pT_hi[0:ROWS[t], t],
                                      ALU.subtract).then_inc(pT_lo_done, 1)

                def maxima(i):
                    a = 4 * u + i
                    dve.wait_ge(s_done, a + 1)
                    dve.tensor_reduce(mx[0:NQ, i:i + 1], ps[sbank(i, not project)][0:NQ, 0:NK], AX.X, ALU.max).then_inc(mx_done, 1)
                    if i == 0:
                        dve.wait_ge(nrq_done, u + 1)
                        dve.wait_ge(rqs_done, u + 1)
                    dve.wait_ge(mx_done, a + 1)
                    dve.tensor_tensor(nm[0:NQ, i:i + 1], mx[0:NQ, i:i + 1], nrq[0:NQ, i:i + 1], ALU.mult).then_inc(nm_done, 1)

                def scale(i):
                    a = 4 * u + i
                    dve.wait_ge(exp_done, a + 1)
                    dve.reciprocal(rr[0:NQ, i:i + 1], rs[0:NQ, i:i + 1]).then_inc(rr_done, 1)
                    dve.wait_ge(rr_done, a + 1)
                    dve.tensor_scalar(pr[0:NQ, j % 2, i], pr[0:NQ, j % 2, i], rr[0:NQ, i:i + 1], None,
                                      ALU.mult).then_inc(p_done, 1)

                if attend:
                    query_scales(s, j, half)
                    dve.wait_ge(kT_hi_done, u + 1)
                    dve.tensor_tensor(kT_lo[:], ps[BKT][:, 0:NKE], kT_hi[:], ALU.subtract).then_inc(kT_lo_done, 1)
                if isinstance(s, int) and s == B - 1 and j == 0:
                    for c in range(C):
                        w_split(c, 1)
                if attend and not project:
                    for i in range(R):
                        maxima(i)
                    if j + 1 < GH:
                        normalise_keys(s, j + 1, par)
                    for t in range(KT):
                        p_split(t)
                    for i in range(R):
                        scale(i)
                if attend and project:
                    if prev:
                        p_split(0)
                    if j + 1 < GH:
                        normalise_keys(s, j + 1, par)
                    if prev:
                        p_split(1)
                    maxima(0)
                    if prev:
                        p_split(2)
                    maxima(1)
                    scale(0)
                    if prev:
                        p_split(3)
                if project:
                    dve.wait_ge(ksq_done, v + 1)
                    if later(v, 4):
                        dve.wait_ge(msk_done, v - 3)
                    dve.tensor_reduce(ssk[:, j], ksq[:].rearrange("p (g d) -> p g d", g=GH), AX.X, ALU.add).then_inc(ssk_done, 1)
                if attend and project:
                    maxima(2)
                    scale(1)
                    maxima(3)
                    if j + 1 == GH:
                        normalise_keys(s + 1, 0, 1 - par)
                    scale(2)
                    scale(3)
                if splits(s, j):
                    kv_split(w, (j + 3) % 4)
                if attend:
                    dve.wait_ge(v_hi_done, u + 1)
                    dve.tensor_tensor(v_lo[:], v_raw[:, par, :, j * HD:(j + 1) * HD], v_hi[:], ALU.subtract).then_inc(v_lo_done, 1)
                    if j + 1 < GH or projects(s):
                        q_split(u + 1)
                if attend and not project and 1 <= j < 3:
                    chunk(0, 0, 0, j - 1)

            for j in range(KT):
                slot(-1, j, 1, 0, False, True)
            q_split(0)
            normalise_keys(0, 0, 0)
            stages(dve, lambda s, par, half: [slot(s, j, par, half, True, projects(s)) for j in range(GH)])
            last = 4 * STAGES - 1
            for t in range(KT):
                dve.wait_ge(pT_hi_done, 4 * last + t + 1)
                dve.tensor_tensor(pT_lo[0:ROWS[t], t], ps[BPT[t % 2]][0:ROWS[t], 0:QW], pT_hi[0:ROWS[t], t],
                                  ALU.subtract).then_inc(pT_lo_done, 1)

            def accumulators(th, nh):
                dve.wait_ge(wo_used, 16 * th + 8 * nh + 8)
                for n in (0, 1):
                    dve.tensor_copy(oT[th][:, 4 * nh + n], ps[n][:, 0:TW]).then_inc(oT_dve, 1)

            def residual(t):
                dve.wait_ge(t1_done, t + 1)
                dve.wait_ge(xr_in[t % 2], 16 * (t // 2 + 1))
                for n in range(2):
                    dve.scalar_tensor_tensor(out=x1[0:NQ, t % 3, n * 512:(n + 1) * 512], in0=ps[experts_bank(t) + n][0:NQ, :],
                                             scalar=gates_t[0:NQ, 0:1], in1=xr[0:NQ, t % 2, n * 512:(n + 1) * 512],
                                             op0=ALU.mult, op1=ALU.add).then_inc(x1_done, 1)
                for n in range(2):
                    dve.wait_ge(x1_done, 2 * t + n + 1)
                    dve.bn_stats(bn6[0:NQ, t % 2, n], x1[0:NQ, t % 3, n * 512:(n + 1) * 512]).then_inc(st2_done, 1)
                dve.wait_ge(st2_done, 2 * t + 2)
                dve.bn_aggr(mv[0:NQ, t], bn6[0:NQ, t % 2]).then_inc(ag2_done, 1)

            def norm(t):
                dve.wait_ge(rs2_done, t + 1)
                dve.wait_ge(ag2_done, t + 1)
                if t >= 2:
                    dve.wait_ge(t2_done, t - 1)
                dve.tensor_scalar(y[0:NQ, t % 2], x1[0:NQ, t % 3], mv[0:NQ, t, 0:1], mv2[0:NQ, t, 1:2],
                                  ALU.subtract, ALU.mult).then_inc(y_done, 1)

            def route_top(t):
                dve.wait_ge(ae_done, t + 1)
                dve.tensor_tensor(lg[0:NQ], ps[experts_bank(t)][0:NQ, ER:AE], rowc[0:NQ, 2:2 + E], ALU.add).then_inc(lg_done, 1)
                dve.wait_ge(lg_done, t + 1)
                dve.max(top[0:NQ], lg[0:NQ]).then_inc(top_done, 1)
                dve.wait_ge(top_done, 2 * t + 1)
                dve.max_index(topi[0:NQ], top[0:NQ], lg[0:NQ]).then_inc(topi_done, 1)
                dve.tensor_scalar(ntop[0:NQ], top[0:NQ, 0:1], -1.0, None, ALU.mult).then_inc(top_done, 1)
                dve.wait_ge(topi_done, t + 1)
                dve.tensor_copy(topf[0:NQ], topi[0:NQ, 0:2]).then_inc(topf_done, 1)

            def route_gates(t):
                dve.wait_ge(ex_done, t + 1)
                dve.tensor_reduce(exs[0:NQ], ex[0:NQ], AX.X, ALU.add).then_inc(gate_step, 1)
                dve.wait_ge(gate_step, 5 * t + 1)
                dve.reciprocal(exr[0:NQ], exs[0:NQ]).then_inc(gate_step, 1)
                dve.wait_ge(gate_step, 5 * t + 2)
                dve.tensor_scalar(gt[0:NQ], ex[0:NQ], exr[0:NQ], None, ALU.mult).then_inc(gate_step, 1)
                dve.wait_ge(gate_step, 5 * t + 3)
                dve.wait_ge(topf_done, t + 1)
                dve.tensor_scalar(wa[0:NQ], rowc[0:NQ, 2 + E:2 + 2 * E], topf[0:NQ, 0:1], gt[0:NQ, 0:1],
                                  ALU.is_equal, ALU.mult).then_inc(gate_step, 1)
                dve.tensor_scalar(wb[0:NQ], rowc[0:NQ, 2 + E:2 + 2 * E], topf[0:NQ, 1:2], gt[0:NQ, 1:2],
                                  ALU.is_equal, ALU.mult).then_inc(gate_step, 1)
                dve.wait_ge(gate_step, 5 * t + 5)
                dve.tensor_tensor(we[0:NQ], wa[0:NQ], wb[0:NQ], ALU.add).then_inc(wsum_done, 1)
                dve.wait_ge(wsum_done, t + 1)
                if t >= 1:
                    dve.wait_ge(t3_done, t)
                dve.tensor_tensor(hw[0:NQ].rearrange("p (e r) -> p e r", e=E),
                                  ps[experts_bank(t)][0:NQ, 0:ER].rearrange("p (e r) -> p e r", e=E),
                                  we[0:NQ].rearrange("p (e o) -> p e o", o=1).to_broadcast([NQ, E, ER // E]),
                                  ALU.mult).then_inc(hw_done, 1)

            def final(t):
                dve.wait_ge(y2_done, t + 1)
                if t == 0:
                    dve.wait_ge(cffn_done, 1)
                if t >= 2:
                    dve.wait_ge(x2_stored[t % 2], 16 * (t // 2))
                for n in range(2):
                    dve.scalar_tensor_tensor(out=x2[0:NQ, t % 2, n * 512:(n + 1) * 512], in0=ps[experts_bank(t) + 2 + n][0:NQ, :],
                                             scalar=cffn[0:NQ], in1=x1[0:NQ, t % 3, n * 512:(n + 1) * 512],
                                             op0=ALU.mult, op1=ALU.add).then_inc(x2_done, 1)

            for nh in range(2):
                with dve.Fori(1, G // 2) as gp:
                    chunk(0, nh, gp, 0)
                    chunk(0, nh, gp, 1)
                chunk(nh, 1 - nh, 0, 0)
                accumulators(0, nh)
                if nh == 0:
                    chunk(0, 1, 0, 1)
            for c in range(2 * G):
                t, n = c // 4, c + 1
                where = (1, n // G, n % G // 2, n % 2)
                if c % 4 == 1:
                    residual(t)
                if c % 4 == 3:
                    route_top(t)
                if n < 2 * G:
                    chunk_weights(*where)
                if c % 4 == 1:
                    norm(t)
                if c % 4 == 3:
                    route_gates(t)
                if n < 2 * G:
                    chunk_heads(*where)
                if c % 4 == 0 and t:
                    final(t - 1)
                if c % G == G - 1:
                    accumulators(1, c // G)
            final(TB - 1)
            for t in (TB, TB + 2):
                if t == TB:
                    residual(t)
                    residual(t + 1)
                norm(t)
                norm(t + 1)
                route_top(t)
                route_gates(t)
                route_top(t + 1)
                route_gates(t + 1)
                final(t)
                if t == TB:
                    residual(t + 2)
                final(t + 1)
                if t == TB:
                    residual(t + 3)


def kernel(x, ctx_4096, g_xattn, g_ffn, L0_xattn_Wq, L0_xattn_Wk, L0_xattn_Wv, L0_xattn_Wo,
           L0_xattn_q_norm_w, L0_xattn_k_norm_w, L0_ffn_router_w, L0_ffn_router_b, L0_ffn_A, L0_ffn_Bm):
    import concourse.bacc as bacc
    from concourse.bass_utils import run_bass_kernel_spmd

    a = np.asarray
    ctxT = a(ctx_4096).transpose(0, 2, 1).reshape(B, C, P, NC).transpose(0, 2, 1, 3)
    arrays = {
        "x": a(x),
        "ctxT": np.concatenate([ctxT[..., OFF[t]:OFF[t] + ROWS[t]].reshape(B, P, C * ROWS[t]) for t in range(KT - 1)],
                               axis=-1),
        "Wq": a(L0_xattn_Wq).reshape(C, P, H, HD).transpose(2, 1, 0, 3),
        "Wkv": np.concatenate([a(w).reshape(C, P, HALVES, KW).transpose(2, 1, 0, 3)
                               for w in (L0_xattn_Wk, L0_xattn_Wv)], axis=-1),
        "Wo": a(L0_xattn_Wo).reshape(G, R, HD, 2, 512).transpose(3, 0, 2, 1, 4),
        "AR": np.concatenate([a(L0_ffn_A).reshape(ER, D), a(L0_ffn_router_w)], axis=0)
                .T.reshape(C, P, AE).transpose(1, 0, 2),
        "BmT": a(L0_ffn_Bm).transpose(0, 2, 1).reshape(ER, D),
        "vecs": np.stack([a(L0_xattn_q_norm_w), a(L0_xattn_k_norm_w)], axis=1),
        "rows": np.broadcast_to(np.concatenate([a(g_xattn), a(g_ffn), a(L0_ffn_router_b),
                                                np.arange(E, dtype=np.float32)]), (P, 2 + 2 * E)),
    }
    arrays = {k: np.ascontiguousarray(v) for k, v in arrays.items()}
    nc = bacc.Bacc("TRN2", target_bir_lowering=False, num_devices=1)
    args = [nc.dram_tensor(k, v.shape, mybir.dt.from_np(v.dtype), kind="ExternalInput").ap() for k, v in arrays.items()]
    out = nc.dram_tensor("out", (B, NQ, D), F32, kind="ExternalOutput").ap()
    build(nc, *args, out)
    return run_bass_kernel_spmd(nc, [arrays], core_ids=[0]).results[0]["out"]
```

```python
from contextlib import ExitStack

import numpy as np

import concourse.bass as bass
from concourse import mybir

F32 = mybir.dt.float32
F32R = mybir.dt.float32r
U32 = mybir.dt.uint32
ACT = mybir.ActivationFunctionType
ALU = mybir.AluOpType
AX = mybir.AxisListType

P = 128
B = 8
NQ = 100
NC = 361
NK = NC + NQ
NKE = NK + NK % 2
D = 1024
C = D // P
HD = 128
H = 32
G = 8
R = H // G
HALVES = 2
GH = G // HALVES
KT = 4
ROWS = [121, 120, 120, NQ]
OFF = [0, 121, 241, NC]
RMAX = max(ROWS)
QW = R * NQ
KW = GH * HD
STAGES = HALVES * B
TH = 2
TB = B // TH
TW = TB * NQ
E = 8
ER = 128
AE = ER + E
RMS_EPS = 1e-6
LN_EPS = 1e-5
SCALING = 8.0 / 16


def build(nc, x, ctxT, Wq, Wkv, Wo, AR, BmT, vecs, rows, out):
    with ExitStack() as ctx:
        def sem(name):
            return ctx.enter_context(nc.semaphore(name))

        def sb(stack, name, shape, dt=F32):
            return stack.enter_context(nc.sbuf_tensor(name, shape, dt))

        xnT_d = nc.dram_tensor("xnT_d", [B, P, C, NQ], F32).ap()
        q_d = nc.dram_tensor("q_d", [G, P, B, QW], F32).ap()
        at_d = nc.dram_tensor("at_d", [STAGES, GH, P, QW], F32).ap()

        ident = sb(ctx, "ident", [P, P])
        mhalf = sb(ctx, "mhalf", [P, B * R])
        qkw = sb(ctx, "qkw", [P, 2])
        wqk = sb(ctx, "wqk", [P, 1])
        rowc = sb(ctx, "rowc", [P, 2 + 2 * E])
        gates_t = sb(ctx, "gates_t", [P, 2])
        cffn = sb(ctx, "cffn", [P, 1])
        rq = sb(ctx, "rq", [P, G, B * R])
        bn6 = sb(ctx, "bn6", [P, 2, 2, 6])
        mv = sb(ctx, "mv", [P, B, 2])
        mv2 = sb(ctx, "mv2", [P, B, 2])
        rstd = sb(ctx, "rstd", [P, B, 2])
        ms = sb(ctx, "ms", [P, B * R])
        rqt = sb(ctx, "rqt", [P, B * R])
        epst = sb(ctx, "epst", [P, GH])
        ssk = sb(ctx, "ssk", [P, KT, GH])
        msk = sb(ctx, "msk", [P, KT, GH])
        rk = sb(ctx, "rk", [P, 2, KT, GH])
        mx = sb(ctx, "mx", [P, R])
        nm = sb(ctx, "nm", [P, R])
        rqs = sb(ctx, "rqs", [P, R])
        nrq = sb(ctx, "nrq", [P, R])
        rs = sb(ctx, "rs", [P, R])
        rr = sb(ctx, "rr", [P, R])

        with ExitStack() as a1:
            xa = sb(a1, "xa", [P, B, D])
            xT_raw = sb(a1, "xT_raw", [P, B, C, NQ])
        bst = ExitStack()
        w_hi = sb(bst, "w_hi", [P, C, 2 * KW], F32R)
        w_lo = sb(bst, "w_lo", [P, C, 2 * KW], F32R)
        kv_raw = sb(bst, "kv_raw", [P, KT, C * RMAX])
        kv_hi = sb(bst, "kv_hi", [P, KT, C, P], F32R)
        kv_lo = sb(bst, "kv_lo", [P, KT, C, P], F32R)
        with ExitStack() as a2:
            xT_hi = sb(a2, "xT_hi", [P, C, B * NQ], F32R)
            xT_lo = sb(a2, "xT_lo", [P, C, B * NQ], F32R)
            wq_raw = sb(a2, "wq_raw", [P, 2, C, HD])
            wq_hi = sb(a2, "wq_hi", [P, 2, C, HD], F32R)
            wq_lo = sb(a2, "wq_lo", [P, 2, C, HD], F32R)
            qo = sb(a2, "qo", [P, B, R, NQ])
            sq = sb(a2, "sq", [P, TW])
            sq_hi = sb(a2, "sq_hi", [P, TW], F32R)
            sq_lo = sb(a2, "sq_lo", [P, TH, TW], F32R)
            ssT = kv_raw[:, KT - 1, 0:TH * TW]
            pick = sb(a2, "pick", [P, R - 1 + P], F32R)
        with ExitStack() as b2:
            k_raw = sb(b2, "k_raw", [P, 2, KT, KW])
            v_raw = sb(b2, "v_raw", [P, 2, KT, KW])
            ksq = sb(b2, "ksq", [P, KW])
            w_raw = sb(b2, "w_raw", [P, 4, KW])
            q_raw = sb(b2, "q_raw", [P, QW])
            q_hi = sb(b2, "q_hi", [P, QW], F32R)
            q_lo = sb(b2, "q_lo", [P, QW], F32R)
            k_n = sb(b2, "k_n", [P, KT, HD])
            kT_hi = sb(b2, "kT_hi", [P, NKE], F32R)
            kT_lo = sb(b2, "kT_lo", [P, NKE], F32R)
            v_hi = sb(b2, "v_hi", [P, KT, HD], F32R)
            v_lo = sb(b2, "v_lo", [P, KT, HD], F32R)
            pr = sb(b2, "pr", [P, 2, R, NK])
            pT_hi = sb(b2, "pT_hi", [P, KT, QW], F32R)
            pT_lo = sb(b2, "pT_lo", [P, KT, QW], F32R)
            ao = sb(b2, "ao", [P, 2, QW])
        with ExitStack() as c2:
            oT0 = sb(c2, "oT0", [P, C, TW])
            ar = sb(c2, "ar", [P, C, AE])
            bm = sb(c2, "bm", [P, D])
            xr = sb(c2, "xr", [P, 2, D])
            x1 = sb(c2, "x1", [P, 3, D])
            y = sb(c2, "y", [P, 2, D])
            yT = sb(c2, "yT", [P, 2, C, NQ])
            lg = sb(c2, "lg", [P, E])
            top = sb(c2, "top", [P, E])
            topi = sb(c2, "topi", [P, E], U32)
            topf = sb(c2, "topf", [P, 2])
            ntop = sb(c2, "ntop", [P, 1])
            ex = sb(c2, "ex", [P, 2])
            exs = sb(c2, "exs", [P, 1])
            exr = sb(c2, "exr", [P, 1])
            gt = sb(c2, "gt", [P, 2])
            wa = sb(c2, "wa", [P, E])
            wb = sb(c2, "wb", [P, E])
            we = sb(c2, "we", [P, E])
            hw = sb(c2, "hw", [P, ER])
            hwT = sb(c2, "hwT", [P, NQ])
            x2 = sb(c2, "x2", [P, 2, D])
        bst.close()
        c1 = ctx.enter_context(ExitStack())
        wo_hi = sb(c1, "wo_hi", [P, 2, R, 512], F32R)
        wo_lo = sb(c1, "wo_lo", [P, 2, R, 512], F32R)
        at_hi = sb(c1, "at_hi", [P, 2, TB, QW], F32R)
        at_lo = sb(c1, "at_lo", [P, 2, TB, QW], F32R)
        at_raw1 = sb(c1, "at_raw1", [P, TB, QW])
        gap = 2 * C * 2 * KW - 4 * R * 512 - 5 * TB * QW
        sb(c1, "gap", [P, gap])
        wo_raw0 = sb(c1, "wo_raw0", [P, R, 512])
        at_raw0 = sb(c1, "at_raw0", [P, TB, QW])
        wo_raw1 = sb(c1, "wo_raw1", [P, R, 512])
        wo_raw, at_raw = (wo_raw0, wo_raw1), (at_raw0, at_raw1)
        oT1 = sb(c1, "oT1", [P, C, TW])
        oT = (oT0, oT1)

        ps = [ctx.enter_context(nc.psum_tensor(f"bank{i}", [P, 512], F32)) for i in range(8)]
        BK, BV, BS, BPT, BPV, BKT = 0, 1, (2, 3), (4, 5), 6, 7

        def sbank(i, last):
            return (BPT[0], BKT)[i % 2] if last else BS[i % 2]

        def ptbank(t, last):
            return BPT[1] if last else BPT[t % 2]

        consts_in = sem("consts_in")
        pool_consts = sem("pool_consts")
        wqk_done = sem("wqk_done")
        tanh_done = sem("tanh_done")
        cffn_done = sem("cffn_done")
        x_in = [sem(f"x_in{b}") for b in range(B)]
        stats_done = sem("stats_done")
        aggr_done = sem("aggr_done")
        var_done = sem("var_done")
        rstd_done = sem("rstd_done")
        xn_done = sem("xn_done")
        xt_done = sem("xt_done")
        xt_raw_done = sem("xt_raw_done")
        xt_hi_done = sem("xt_hi_done")
        xt_lo_done = sem("xt_lo_done")
        xnT_stored = sem("xnT_stored")
        wq_in = [sem("wq_in0"), sem("wq_in1")]
        wq_hi_done = sem("wq_hi_done")
        wq_lo_done = sem("wq_lo_done")
        q_done = sem("q_done")
        sq_done = sem("sq_done")
        qo_done = sem("qo_done")
        qo_stored = sem("qo_stored")
        sq_hi_done = sem("sq_hi_done")
        sq_lo_done = sem("sq_lo_done")
        pick_zero = sem("pick_zero")
        pick_done = sem("pick_done")
        ss_done = sem("ss_done")
        ssT_done = sem("ssT_done")
        sst_turned = sem("sst_turned")
        ms_done = sem("ms_done")
        rqt_done = sem("rqt_done")
        rq_done = sem("rq_done")
        pad_done = sem("pad_done")
        w_in = [sem("w_in0"), sem("w_in1")]
        w2_in = [sem(f"w2_in{i}") for i in range(4)]
        w_hi_done = sem("w_hi_done")
        w_lo_done = sem("w_lo_done")
        kv_in = [sem(f"kv_in{t}") for t in range(KT)]
        kv_hi_done = sem("kv_hi_done")
        kv_lo_done = sem("kv_lo_done")
        k_proj_done = sem("k_proj_done")
        v_proj_done = sem("v_proj_done")
        k_raw_done = sem("k_raw_done")
        ksq_done = sem("ksq_done")
        v_raw_done = sem("v_raw_done")
        ssk_done = sem("ssk_done")
        msk_done = sem("msk_done")
        rk_done = sem("rk_done")
        kn_done = sem("kn_done")
        kt_done = sem("kt_done")
        kT_hi_done = sem("kT_hi_done")
        kT_lo_done = sem("kT_lo_done")
        q_in = sem("q_in")
        q_hi_done = sem("q_hi_done")
        q_lo_done = sem("q_lo_done")
        v_hi_done = sem("v_hi_done")
        v_lo_done = sem("v_lo_done")
        s_done = sem("s_done")
        rqs_done = sem("rqs_done")
        nrq_done = sem("nrq_done")
        mx_done = sem("mx_done")
        nm_done = sem("nm_done")
        exp_done = sem("exp_done")
        rr_done = sem("rr_done")
        p_done = sem("p_done")
        pt_done = sem("pt_done")
        pT_hi_done = sem("pT_hi_done")
        pT_lo_done = sem("pT_lo_done")
        pv_done = sem("pv_done")
        ao_done = sem("ao_done")
        ao_stored = [sem("ao_stored0"), sem("ao_stored1")]
        wo_in = [sem("wo_in0"), sem("wo_in1")]
        wo_hi_done = sem("wo_hi_done")
        wo_lo_done = sem("wo_lo_done")
        wo_used = sem("wo_used")
        oT_act = sem("oT_act")
        oT_dve = sem("oT_dve")
        ffn_in = sem("ffn_in")
        xr_in = [sem("xr_in0"), sem("xr_in1")]
        t1_done = sem("t1_done")
        x1_done = sem("x1_done")
        st2_done = sem("st2_done")
        ag2_done = sem("ag2_done")
        va2_done = sem("va2_done")
        rs2_done = sem("rs2_done")
        y_done = sem("y_done")
        t2_done = sem("t2_done")
        yT_done = sem("yT_done")
        ae_done = sem("ae_done")
        lg_done = sem("lg_done")
        top_done = sem("top_done")
        topi_done = sem("topi_done")
        topf_done = sem("topf_done")
        ex_done = sem("ex_done")
        gate_step = sem("gate_step")
        wsum_done = sem("wsum_done")
        hw_done = sem("hw_done")
        t3_done = sem("t3_done")
        hwT_done = sem("hwT_done")
        y2_done = sem("y2_done")
        x2_done = sem("x2_done")
        x2_stored = [sem("x2_stored0"), sem("x2_stored1")]

        block = ctx.enter_context(nc.Block())

        def later(n, k):
            return not isinstance(n, int) or n >= k

        def stages(eng, stage):
            stage(0, 0, 0)
            with eng.Fori(1, 6, 2) as s:
                stage(s, 1, 0)
                stage(s + 1, 0, 0)
            stage(7, 1, 0)
            with eng.Fori(8, 13, 2) as s:
                stage(s, 0, 1)
                stage(s + 1, 1, 1)
            stage(14, 0, 1)
            stage(15, 1, 1)

        def projects(s):
            return not isinstance(s, int) or s + 1 < STAGES

        def out_bank(t):
            return 0 if t in (TB + 1, TB + 3) else 4

        def experts_bank(t):
            return (2, 6, 4, 0)[t - TB] if t >= TB else 6

        def splits(s, j):
            return not isinstance(s, int) or 4 * s + j + 7 < 4 * STAGES

        def wstage(c):
            flat = kv_raw[:].rearrange("p t k -> p (t k)")
            return flat[:, (c % 2) * 2 * KW:(c % 2 + 1) * 2 * KW]

        def raw_tile(t):
            return kv_raw[:, t, 0:C * ROWS[t]].rearrange("p (c k) -> p c k", c=C)

        @block.sync
        def _(sp):
            for b in range(B):
                sp.dma_start(xa[0:NQ, b, :], x[b]).then_inc(x_in[b], 16)
                if b == 0:
                    sp.dma_start(qkw[:], vecs).then_inc(consts_in, 16)
                    sp.dma_start(rowc[:], rows).then_inc(consts_in, 16)
                if b in (3, 4):
                    sp.dma_start(wq_raw[:, b - 3], Wq[b - 3]).then_inc(wq_in[b - 3], 16)
            for b in range(B):
                sp.wait_ge(xt_raw_done, b + 1)
                sp.dma_start(xnT_d[b], xT_raw[:, b]).then_inc(xnT_stored, 16)

            def queries(g):
                for i in range(R):
                    h = 4 * g + i
                    if isinstance(h, int) and h < H - 2 or not isinstance(h, int):
                        sp.wait_ge(wq_lo_done, h + 1)
                        sp.dma_start(wq_raw[:, i % 2], Wq[h + 2] if isinstance(h, int) else
                                     Wq[bass.ds(h + 2, 1)].rearrange("o p c n -> p (o c) n")).then_inc(wq_in[i % 2], 16)
                    if isinstance(g, int) and g == 0:
                        for c in (2 * i, 2 * i + 1):
                            if c >= 2:
                                sp.wait_ge(w_lo_done, c - 1)
                            sp.dma_start(wstage(c), Wkv[0, :, c]).then_inc(w_in[c % 2], 16)
                sp.wait_ge(qo_done, 8 * g + 8)
                if isinstance(g, int):
                    sp.dma_start(q_d[g], qo[:].rearrange("p b i q -> p b (i q)")).then_inc(qo_stored, 16)
                else:
                    sp.dma_start(q_d[bass.ds(g, 1)].rearrange("o p b q -> p (o b) q"),
                                 qo[:].rearrange("p b i q -> p b (i q)")).then_inc(qo_stored, 16)

            queries(0)

            def load_kv(n, t):
                if later(n, 1):
                    sp.wait_ge(kv_lo_done, 4 * (n - 1) + t + 1)
                dst = kv_raw[:, t, 0:C * ROWS[t]]
                if t < KT - 1:
                    cols = slice(C * OFF[t], C * (OFF[t] + ROWS[t]))
                    src = ctxT[n % B, :, cols] if isinstance(n, int) else \
                        ctxT[bass.ds(n % B, 1), :, cols].rearrange("o p k -> p (o k)")
                else:
                    src = xnT_d[n % B].rearrange("p c k -> p (c k)") if isinstance(n, int) else \
                        xnT_d[bass.ds(n % B, 1)].rearrange("o p c k -> p (o c k)")
                sp.dma_start(dst, src).then_inc(kv_in[t], 16)

            sp.wait_ge(w_lo_done, C)
            sp.wait_ge(xnT_stored, 16 * B)
            for t in range(KT - 1):
                load_kv(0, t)
            with sp.Fori(1, G - 1) as g:
                queries(g)
            queries(G - 1)
            sp.wait_ge(sst_turned, G)
            load_kv(0, KT - 1)

            def load_q(s, j, half):
                u = 4 * s + j
                if later(u, 1):
                    sp.wait_ge(q_lo_done, u)
                else:
                    sp.wait_ge(qo_stored, 16 * G)
                if isinstance(s, int):
                    src = q_d[half * GH + j, :, s % B]
                else:
                    src = q_d[half * GH + j, :, bass.ds(s - B * half, 1)].rearrange("p o q -> p (o q)")
                sp.dma_start(q_raw[:], src).then_inc(q_in, 16)

            def store_attn(s, j):
                u = 4 * s + j
                sp.wait_ge(ao_done, u + 1)
                dst = at_d[s, j] if isinstance(s, int) else at_d[bass.ds(s, 1), j].rearrange("o p q -> p (o q)")
                sp.dma_start(dst, ao[:, j % 2]).then_inc(ao_stored[j % 2], 16)

            def load_w2(n):
                sp.dma_start(w_raw[:, n % 4], Wkv[1, :, n % C, n // C * KW:(n // C + 1) * KW]).then_inc(w2_in[n % 4], 16)

            load_q(0, 0, 0)
            for t in range(KT):
                load_kv(1, t)
            for n in range(4):
                load_w2(n)

            at_g = at_d.rearrange("(h b) g p q -> h b g p q", h=HALVES)

            def chunk(th, nh, gp, k):
                m = 16 * th + 8 * nh + 2 * gp + k
                if later(m, 2):
                    sp.wait_ge(wo_lo_done, 2 * m - 2)
                if isinstance(gp, int):
                    g = 2 * gp + k
                    wsrc = Wo[nh, g]
                    asrc = at_g[g // GH, TB * th:TB * th + TB, g % GH].rearrange("b p q -> p b q")
                else:
                    wsrc = Wo[nh, bass.ds(2 * gp + k, 1)].rearrange("o p i n -> p (o i) n")
                    asrc = at_g[bass.ds(gp // 2, 1), TB * th:TB * th + TB, bass.ds(gp % 2 * 2 + k, 1)]\
                        .rearrange("h b o p q -> p (h b o) q")
                sp.dma_start(wo_raw[k][:], wsrc).then_inc(wo_in[k], 16)
                sp.dma_start(at_raw[k][:], asrc).then_inc(wo_in[k], 16)

            def stage(s, par, half):
                for j in range(GH):
                    if j == 0 and isinstance(s, int) and s == B - 1:
                        for n in range(4, 2 * C):
                            sp.wait_ge(w_lo_done, C + n - 3)
                            load_w2(n)
                    if splits(s, 1):
                        load_kv(s + 2, j)
                    if isinstance(s, int) and s == STAGES - 2 and j == 1:
                        sp.wait_ge(kv_lo_done, 4 * STAGES)
                        sp.wait_ge(ao_stored[0], 32 * (B + TB))
                        sp.wait_ge(ao_stored[1], 32 * (B + TB))
                        chunk(0, 0, 0, 0)
                    if j + 1 < GH:
                        load_q(s, j + 1, half)
                        if not projects(s):
                            if j == 0:
                                sp.wait_ge(v_proj_done, 4 * STAGES)
                            chunk(0, 0, j, 1)
                            chunk(0, 0, j + 1, 0)
                    elif not projects(s):
                        chunk(0, 0, j, 1)
                        chunk(0, 1, 0, 0)
                    elif projects(s):
                        last_of_half = isinstance(s, int) and s == B - 1
                        load_q(s + 1, 0, 1 if last_of_half else half)
                    if j >= 1:
                        store_attn(s, j - 1)
                    elif later(s, 1):
                        store_attn(s - 1, GH - 1)

            stages(sp, stage)
            chunk(0, 1, 0, 1)
            chunk(0, 1, 1, 0)
            chunk(0, 1, 1, 1)
            sp.wait_ge(ao_done, 4 * STAGES)
            sp.dma_start(at_d[STAGES - 1, GH - 1], ao[:, 1]).then_inc(ao_stored[1], 16)

            def load_x(t):
                sp.dma_start(xr[0:NQ, t % 2], x[t]).then_inc(xr_in[t % 2], 16)

            def store(t):
                sp.wait_ge(x2_done, 2 * t + 2)
                sp.dma_start(out[t], x2[0:NQ, t % 2]).then_inc(x2_stored[t % 2], 16)

            sp.wait_ge(ao_stored[0], 16 * 2 * STAGES)
            sp.wait_ge(ao_stored[1], 16 * 2 * STAGES)
            sp.dma_start(ar[:], AR).then_inc(ffn_in, 16)
            sp.dma_start(bm[:], BmT).then_inc(ffn_in, 16)
            load_x(0)
            load_x(1)
            with sp.Fori(2, G // 2) as gp:
                chunk(0, 1, gp, 0)
                chunk(0, 1, gp, 1)
            for c in range(2 * G):
                t = c // 4
                chunk(1, c // G, c % G // 2, c % 2)
                if c % 4 == 0 and t >= 1:
                    sp.wait_ge(x1_done, 2 * t)
                    load_x(t + 1)
                if c % 4 == 3 and t >= 1:
                    store(t - 1)
            for t in range(TB - 1, B):
                if t + 2 < B:
                    sp.wait_ge(x1_done, 2 * t + 2)
                    load_x(t + 2)
                if t >= TB:
                    store(t - 1)
            store(B - 1)
            sp.wait_ge(x2_stored[0], 16 * B // 2)
            sp.wait_ge(x2_stored[1], 16 * B // 2)

        @block.gpsimd
        def _(pool):
            pool.memset(ident[:], 0.0).then_inc(pool_consts, 1)
            pool.memset(mhalf[:], -0.5).then_inc(pool_consts, 1)
            pool.memset(epst[:], RMS_EPS).then_inc(pool_consts, 1)
            pool.wait_ge(pool_consts, 3)
            pool.affine_select(out=ident[:], in_=ident[:], compare_op=ALU.not_equal, fill=1.0, base=0,
                               pattern=[[-1, P]], channel_multiplier=1).then_inc(pool_consts, 1)
            for b in range(B):
                pool.wait_ge(aggr_done, b + 1)
                pool.tensor_scalar(rstd[0:NQ, b, 0:1], mv[0:NQ, b, 1:2], 1.0, LN_EPS, ALU.mult, ALU.add).then_inc(var_done, 1)
                pool.wait_ge(var_done, b + 1)
                pool.tensor_tensor(rstd[0:NQ, b, 1:2], rstd[0:NQ, b, 0:1], mhalf[0:NQ, 0:1], ALU.pow).then_inc(rstd_done, 1)

            def group_rms(g):
                pool.wait_ge(ms_done, 2 * g + 2)
                if later(g, 1):
                    pool.wait_ge(rq_done, g)
                pool.tensor_tensor(rqt[0:NQ], ms[0:NQ], mhalf[0:NQ], ALU.pow).then_inc(rqt_done, 1)

            group_rms(0)
            with pool.Fori(1, G) as g:
                group_rms(g)

            def key_rms(n, par):
                for t in range(KT):
                    v = 4 * n + t
                    pool.wait_ge(ssk_done, v + 1)
                    pool.tensor_tensor(msk[:, t, :], ssk[:, t, :], epst[:], ALU.add).then_inc(msk_done, 1)
                    if t == 0 and later(n, 2):
                        pool.wait_ge(kn_done, 4 * (n - 1))
                    pool.wait_ge(msk_done, v + 1)
                    pool.tensor_tensor(rk[:, par, t, :], msk[:, t, :], mhalf[:, 0:GH], ALU.pow).then_inc(rk_done, 1)

            key_rms(0, 0)
            key_rms(1, 1)
            with pool.Fori(2, STAGES - 1, 2) as n:
                key_rms(n, 0)
                key_rms(n + 1, 1)
            for t in range(B):
                pool.wait_ge(ag2_done, t + 1)
                pool.tensor_scalar(mv2[0:NQ, t, 0:1], mv[0:NQ, t, 1:2], 1.0, LN_EPS, ALU.mult, ALU.add).then_inc(va2_done, 1)
                pool.wait_ge(va2_done, t + 1)
                pool.tensor_tensor(mv2[0:NQ, t, 1:2], mv2[0:NQ, t, 0:1], mhalf[0:NQ, 0:1], ALU.pow).then_inc(rs2_done, 1)

        @block.tensor
        def _(pe):
            def three(o, lh, ll, rh, rl, start, stop):
                pe.matmul(o, lh, rh, start=start, stop=False)
                pe.matmul(o, lh, rl, start=False, stop=False)
                return pe.matmul(o, ll, rh, start=False, stop=stop)

            def first_queries(cs):
                if cs[0] == 0:
                    pe.wait_ge(wq_lo_done, 1)
                    pe.wait_ge(xt_lo_done, TB)
                for c in cs:
                    mm = three(ps[0][:, 0:TW], wq_hi[:, 0, c], wq_lo[:, 0, c], xT_hi[:, c, 0:TW], xT_lo[:, c, 0:TW],
                               c == 0, c == C - 1)
                if cs[-1] == C - 1:
                    mm.then_inc(q_done, 1)

            pe.wait_ge(pool_consts, 4)
            for b in range(B):
                pe.wait_ge(xn_done, b + 1)
                if b >= 2:
                    pe.wait_ge(xt_raw_done, b - 1)
                for c in range(C):
                    bank = ps[4 + 2 * (b % 2) + c // 4]
                    mm = pe.transpose(bank[:, (c % 4) * NQ:(c % 4 + 1) * NQ], xa[0:NQ, b, c * P:(c + 1) * P],
                                      ident[0:NQ, 0:NQ])
                mm.then_inc(xt_done, 1)
                if b >= TB:
                    first_queries((2 * (b - TB), 2 * (b - TB) + 1))

            def squares(h, th, i, g):
                pe.wait_ge(sq_lo_done, 2 * h + th + 1)
                if not later(h, 1) and th == 0:
                    pe.wait_ge(pick_done, 1)
                if i == 0 and later(g, 1):
                    pe.wait_ge(ssT_done, 2 * g)
                o, row = ps[4 + th][:, 0:TW], pick[:, R - 1 - i:R - 1 - i + P]
                pe.matmul(o, row, sq_hi[:], start=i == 0, stop=False)
                pe.matmul(o, row, sq_lo[:, th], start=False, stop=i == R - 1).then_inc(ss_done, 1)

            def turn_sums(n):
                pe.wait_ge(ssT_done, 2 * n)
                for b in range(B):
                    mm = pe.transpose(ps[6 + b // 4][0:NQ, (b % 4) * P:(b % 4 + 1) * P], ssT[:, b * NQ:(b + 1) * NQ], ident[:])
                mm.then_inc(sst_turned, 1)

            def queries(g):
                for i in range(R):
                    h = 4 * g + i
                    pe.wait_ge(wq_lo_done, h + 1)
                    for th in range(TH):
                        if isinstance(g, int) and g == 0 and i == 0:
                            if th == 0:
                                continue
                            pe.wait_ge(xt_lo_done, B)
                        if later(h, 2):
                            pe.wait_ge(qo_done, 2 * (h - 2) + th + 1)
                        o = ps[2 * (i % 2) + th][:, 0:TW]
                        for c in range(C):
                            mm = three(o, wq_hi[:, i % 2, c], wq_lo[:, i % 2, c],
                                       xT_hi[:, c, th * TW:(th + 1) * TW], xT_lo[:, c, th * TW:(th + 1) * TW],
                                       c == 0, c == C - 1)
                        mm.then_inc(q_done, 1)
                        if th == 0 and later(h, 1):
                            squares(h - 1, 1, (i - 1) % R, g)
                        if th == 1:
                            squares(h, 0, i, g)
                            if i == 1 and later(g, 1):
                                turn_sums(g)

            queries(0)
            with pe.Fori(1, G) as g:
                queries(g)

            def chunk_head(th, nh, gp, k, i, first=False, last=False):
                m = 16 * th + 8 * nh + 2 * gp + k
                if i == 0:
                    pe.wait_ge(wo_lo_done, 2 * m + 2)
                for n in range(4):
                    mm = three(ps[n][:, 0:TW].rearrange("p (b q) -> p b q", b=TB),
                               wo_hi[:, k, i, n * P:(n + 1) * P], wo_lo[:, k, i, n * P:(n + 1) * P],
                               at_hi[:, k, :, i * NQ:(i + 1) * NQ], at_lo[:, k, :, i * NQ:(i + 1) * NQ],
                               first and i == 0, last and i == R - 1)
                if i == R - 1:
                    mm.then_inc(wo_used, 1)

            def chunk(th, nh, gp, k, first=False, last=False, between=None):
                for i in range(R):
                    chunk_head(th, nh, gp, k, i, first, last)
                    if between and i == R // 2 - 1:
                        between()

            def proj_chunk(s, j, half, n):
                v = 4 * s + 4 + j
                isv, cc = n // 4, 2 * (n % 4)
                if n == 0:
                    pe.wait_ge(kv_lo_done, v + 1)
                    if later(v, 1):
                        pe.wait_ge(ksq_done, v)
                if n == 4 and later(v, 1):
                    pe.wait_ge(v_raw_done, v)
                for c in (cc, cc + 1):
                    if j == 0 and (half or not isv):
                        pe.wait_ge(w_lo_done, C * (half + isv) + c + 1)
                    mm = three(ps[BV if isv else BK][:, 0:KW], kv_hi[:, j, c], kv_lo[:, j, c],
                               w_hi[:, c, isv * KW:(isv + 1) * KW], w_lo[:, c, isv * KW:(isv + 1) * KW],
                               c == 0, c == C - 1)
                if n == 3:
                    mm.then_inc(k_proj_done, 1)
                if n == 7:
                    mm.then_inc(v_proj_done, 1)

            def turn_keys(u):
                pe.wait_ge(kn_done, u + 1)
                if later(u, 1):
                    pe.wait_ge(kT_lo_done, u)
                if isinstance(u, int) and u > 4 * (STAGES - 1):
                    pe.wait_ge(exp_done, 4 * u)
                for t in range(KT):
                    r = ROWS[t] + (NKE - NK if t == KT - 1 else 0)
                    mm = pe.transpose(ps[BKT][:, OFF[t]:OFF[t] + r], k_n[0:r, t, :], ident[0:r, 0:r])
                mm.then_inc(kt_done, 1)

            def scores(u, i, last=False):
                if i == 0:
                    pe.wait_ge(kT_lo_done, u + 1)
                    pe.wait_ge(q_lo_done, u + 1)
                a = 4 * u + i
                if later(a, 2):
                    pe.wait_ge(exp_done, a - 1)
                three(ps[sbank(i, last)][0:NQ, 0:NKE], q_hi[:, i * NQ:(i + 1) * NQ], q_lo[:, i * NQ:(i + 1) * NQ],
                      kT_hi[:], kT_lo[:], True, True).then_inc(s_done, 1)

            def turn_probs(u, par, t, last=False):
                if t == 0:
                    pe.wait_ge(p_done, 4 * u + 4)
                a = 4 * u + t
                if last:
                    pe.wait_ge(pT_lo_done, a)
                elif later(a, 2):
                    pe.wait_ge(pT_lo_done, a - 1)
                for i in range(R):
                    mm = pe.transpose(ps[ptbank(t, last)][0:ROWS[t], i * NQ:(i + 1) * NQ],
                                      pr[0:NQ, par, i, OFF[t]:OFF[t] + ROWS[t]], ident[0:NQ, 0:NQ])
                mm.then_inc(pt_done, 1)

            def values(u, t):
                pe.wait_ge(pT_lo_done, 4 * u + t + 1)
                if t == 0:
                    pe.wait_ge(v_lo_done, u + 1)
                    if later(u, 1):
                        pe.wait_ge(ao_done, u)
                r = ROWS[t]
                mm = three(ps[BPV][:, 0:QW], v_hi[0:r, t], v_lo[0:r, t], pT_hi[0:r, t], pT_lo[0:r, t],
                           t == 0, t == KT - 1)
                if t == KT - 1:
                    mm.then_inc(pv_done, 1)

            def slot(s, j, half, attend, project):
                u = 4 * s + j
                prev = attend and later(u, 1)
                par = (j + 1) % 2
                nhalf = 1 if isinstance(s, int) and s == B - 1 else half

                def c_(n):
                    if project:
                        proj_chunk(s, j, nhalf, n)
                if attend and not project and j == 0:
                    turn_keys(u)
                    turn_probs(u - 1, par, 0, True)
                    scores(u, 0, True)
                    values(u - 1, 0)
                    scores(u, 1, True)
                    pe.wait_ge(v_raw_done, 4 * STAGES)
                    pe.wait_ge(ksq_done, 4 * STAGES)
                    pe.wait_ge(exp_done, 4 * u)
                    for i in range(R):
                        chunk_head(0, 0, 0, 0, i, first=True)
                        if i < 3:
                            turn_probs(u - 1, par, i + 1, True)
                        if i < 2:
                            scores(u, i + 2, True)
                            values(u - 1, i + 1)
                    values(u - 1, 3)
                    return
                if attend and not project:
                    def x_(n):
                        chunk_head(0, 0, j - 1 + n // 4, 1 - n // 4, n % 4)
                    turn_keys(u)
                    turn_probs(u - 1, par, 0, True)
                    x_(0)
                    scores(u, 0, True)
                    values(u - 1, 0)
                    x_(1)
                    scores(u, 1, True)
                    turn_probs(u - 1, par, 1, True)
                    x_(2)
                    scores(u, 2, True)
                    values(u - 1, 1)
                    turn_probs(u - 1, par, 2, True)
                    x_(3)
                    scores(u, 3, True)
                    values(u - 1, 2)
                    turn_probs(u - 1, par, 3, True)
                    x_(4)
                    values(u - 1, 3)
                    x_(5)
                    x_(6)
                    x_(7)
                    return
                new_weights = isinstance(s, int) and s == B - 1 and j == 0
                if not new_weights:
                    c_(0)
                if attend:
                    turn_keys(u)
                if prev:
                    turn_probs(u - 1, par, 0)
                if new_weights:
                    turn_probs(u - 1, par, 1)
                    c_(0)
                c_(1)
                if prev and not new_weights:
                    turn_probs(u - 1, par, 1)
                c_(2)
                if attend:
                    scores(u, 0)
                if prev:
                    values(u - 1, 0)
                    turn_probs(u - 1, par, 2)
                c_(3)
                if attend:
                    scores(u, 1)
                if prev:
                    values(u - 1, 1)
                    turn_probs(u - 1, par, 3)
                c_(4)
                if attend:
                    scores(u, 2)
                if prev:
                    values(u - 1, 2)
                c_(5)
                if attend:
                    scores(u, 3)
                if prev:
                    values(u - 1, 3)
                c_(6)
                c_(7)

            pe.wait_ge(qo_done, 2 * H - 2)
            for j in range(KT):
                slot(-1, j, 0, False, True)
                if j == 0:
                    squares(H - 1, 1, R - 1, G - 1)
                    turn_sums(G)
            pe.wait_ge(qo_done, 2 * H)
            pe.wait_ge(rq_done, G)
            stages(pe, lambda s, par, half: [slot(s, j, half, True, projects(s)) for j in range(GH)])
            last = 4 * STAGES - 1
            for t in range(KT):
                turn_probs(last, 1, t, True)
                chunk_head(0, 0, 3, 1, t, last=True)
                values(last, t)

            def accumulators_free(th, nh):
                m = 2 * (2 * th + nh)
                pe.wait_ge(oT_dve, m)
                pe.wait_ge(oT_act, m)

            def turn_out(t):
                o = out_bank(t)
                if t == 0:
                    accumulators_free(1, 0)
                if 1 <= t <= TB:
                    pe.wait_ge(x1_done, 2 * t)
                if t > TB + 1:
                    pe.wait_ge(x1_done, 2 * t - 2)
                for c in range(C):
                    if t == TB and c % 4 == 0:
                        accumulators_free(1 + c // 4, 1 - c // 4)
                    mm = pe.transpose(ps[o + c // 4][0:NQ, (c % 4) * P:(c % 4 + 1) * P],
                                      oT[t // TB][:, c, (t % TB) * NQ:(t % TB + 1) * NQ], ident[:])
                mm.then_inc(t1_done, 1)

            def turn_y(t):
                e = experts_bank(t)
                pe.wait_ge(y_done, t + 1)
                if 1 <= t < TB:
                    pe.wait_ge(x2_done, 2 * t)
                if t == TB + 1:
                    pe.wait_ge(x2_done, 2 * TB)
                if t > TB + 1:
                    pe.wait_ge(x1_done, 2 * t + 2)
                for c in range(C):
                    mm = pe.transpose(ps[e + c // 4][:, (c % 4) * NQ:(c % 4 + 1) * NQ],
                                      y[0:NQ, t % 2, c * P:(c + 1) * P], ident[0:NQ, 0:NQ])
                mm.then_inc(t2_done, 1)

            def low_rank(t):
                pe.wait_ge(yT_done, 2 * t + 2)
                if t == 0:
                    pe.wait_ge(ffn_in, 32)
                for c in range(C):
                    mm = pe.matmul(ps[experts_bank(t)][0:NQ, 0:AE], yT[:, t % 2, c], ar[:, c],
                                   start=(c == 0), stop=(c == C - 1))
                mm.then_inc(ae_done, 1)

            def turn_h(t):
                pe.wait_ge(hw_done, t + 1)
                pe.transpose(ps[experts_bank(t) + 1][:, 0:NQ], hw[0:NQ], ident[0:NQ, 0:NQ]).then_inc(t3_done, 1)

            def up(t):
                pe.wait_ge(hwT_done, t + 1)
                e = experts_bank(t)
                pe.matmul(ps[e][0:NQ, :], hwT[:], bm[:, 0:512], start=True, stop=True)
                pe.matmul(ps[e + 1][0:NQ, :], hwT[:], bm[:, 512:1024], start=True, stop=True).then_inc(y2_done, 1)

            accumulators_free(0, 1)
            chunk(0, 1, 0, 0, first=True)
            chunk(0, 1, 0, 1)
            with pe.Fori(1, G // 2 - 1) as gp:
                chunk(0, 1, gp, 0)
                chunk(0, 1, gp, 1)
            chunk(0, 1, G // 2 - 1, 0)
            chunk(0, 1, G // 2 - 1, 1, last=True)
            for c in range(2 * G):
                t = c // 4
                if c % G == 0:
                    accumulators_free(1, c // G)
                chunk(1, c // G, c % G // 2, c % 2, first=c % G == 0, last=c % G == G - 1,
                      between=(lambda: up(t - 1)) if c % 4 == 0 and t else None)
                (turn_out, turn_y, low_rank, turn_h)[c % 4](t)
            up(TB - 1)
            a, b, c, d = range(TB, B)
            for step, t in ((turn_out, a), (turn_out, b), (turn_y, a), (low_rank, a), (turn_out, c), (turn_y, b),
                            (low_rank, b), (turn_h, a), (up, a), (turn_out, d), (turn_h, b), (up, b), (turn_y, c),
                            (low_rank, c), (turn_y, d), (low_rank, d), (turn_h, c), (up, c), (turn_h, d), (up, d)):
                step(t)

        @block.scalar
        def _(act):
            act.wait_ge(consts_in, 32)
            act.activation(gates_t[:], rowc[:, 0:2], ACT.Tanh).then_inc(tanh_done, 1)

            def wq_split(g, i):
                k, h = i % 2, 4 * g + i
                act.wait_ge(wq_in[k], 16 * (2 * g + i // 2 + 1))
                if later(h, 2):
                    act.wait_ge(q_done, 2 * (h - 2) + 2)
                act.activation(wq_hi[:, k], wq_raw[:, k], ACT.Copy).then_inc(wq_hi_done, 1)

            for b in range(B):
                if b in (3, 4):
                    wq_split(0, b - 3)
                act.wait_ge(xt_done, b + 1)
                for n in range(2):
                    ins = act.activation(xT_raw[:, b, 4 * n:4 * n + 4].rearrange("p c q -> p (c q)"),
                                         ps[4 + 2 * (b % 2) + n][:, 0:4 * NQ], ACT.Copy)
                ins.then_inc(xt_raw_done, 1)
                act.wait_ge(xt_raw_done, b + 1)
                act.activation(xT_hi[:, :, b * NQ:(b + 1) * NQ], xT_raw[:, b], ACT.Copy).then_inc(xt_hi_done, 1)

            def w_split(c):
                act.wait_ge(w_in[c % 2], 16 * (c // 2 + 1))
                if c == 0:
                    act.wait_ge(xt_lo_done, B)
                    act.wait_ge(xnT_stored, 16 * B)
                act.activation(w_hi[:, c], wstage(c), ACT.Copy).then_inc(w_hi_done, 1)

            def w2_split(n):
                act.wait_ge(w2_in[n % 4], 16 * (n // 4 + 1))
                if n == 0:
                    act.wait_ge(k_proj_done, 4 * B)
                if n == C:
                    act.wait_ge(v_proj_done, 4 * B)
                act.activation(w_hi[:, n % C, n // C * KW:(n // C + 1) * KW], w_raw[:, n % 4], ACT.Copy).then_inc(w_hi_done, 1)

            def queries(g):
                for i in range(R):
                    h = 4 * g + i
                    for th in range(TH):
                        act.wait_ge(q_done, 2 * h + th + 1)
                        if later(h, 1) or th == 1:
                            act.wait_ge(sq_lo_done, 2 * h + th)
                        act.activation(sq[:], ps[2 * (i % 2) + th][:, 0:TW], ACT.Square).then_inc(sq_done, 1)
                        act.wait_ge(sq_done, 2 * h + th + 1)
                        if later(h, 1) or th == 1:
                            act.wait_ge(ss_done, 2 * h + th)
                        act.activation(sq_hi[:], sq[:], ACT.Copy).then_inc(sq_hi_done, 1)
                    if not isinstance(g, int) or h + 2 < H:
                        wq_split(g, i + 2)
                    if isinstance(g, int) and g == 0:
                        w_split(2 * i)
                        w_split(2 * i + 1)

            def kv_split(n, t):
                w = 4 * n + t
                act.wait_ge(kv_in[t], 16 * (n + 1))
                if later(w, 4):
                    act.wait_ge(v_proj_done, w - 3)
                act.activation(kv_hi[:, t, :, 0:ROWS[t]], raw_tile(t), ACT.Copy).then_inc(kv_hi_done, 1)

            queries(0)
            with act.Fori(1, G - 1) as g:
                queries(g)
            act.wait_ge(pad_done, 1)
            kv_split(0, 0)
            queries(G - 1)
            kv_split(0, 1)
            kv_split(0, 2)

            def q_split(u):
                act.wait_ge(q_in, 16 * (u + 1))
                if later(u, 1):
                    act.wait_ge(s_done, 4 * u)
                act.activation(q_hi[:], q_raw[:], ACT.Copy).then_inc(q_hi_done, 1)

            def chunk_weights(th, nh, gp, k):
                m = 16 * th + 8 * nh + 2 * gp + k
                act.wait_ge(wo_in[k], 32 * (8 * th + 4 * nh + gp + 1))
                if later(m, 2):
                    act.wait_ge(wo_used, m - 1)
                act.activation(wo_hi[:, k], wo_raw[k][:], ACT.Copy).then_inc(wo_hi_done, 1)

            def chunk_heads(k):
                act.activation(at_hi[:, k], at_raw[k][:], ACT.Copy).then_inc(wo_hi_done, 1)

            def chunk(th, nh, gp, k):
                chunk_weights(th, nh, gp, k)
                chunk_heads(k)

            def slot(s, j, par, half, attend, project):
                u, v = 4 * s + j, 4 * s + 4 + j
                prev = attend and later(u, 1)

                def p_split(t):
                    act.wait_ge(pt_done, 4 * (u - 1) + t + 1)
                    act.activation(pT_hi[0:ROWS[t], t], ps[ptbank(t, not project)][0:ROWS[t], 0:QW], ACT.Copy).then_inc(pT_hi_done, 1)

                def exps(i):
                    a = 4 * u + i
                    act.wait_ge(nm_done, a + 1)
                    if i == 0 and later(u, 2):
                        act.wait_ge(pt_done, 4 * (u - 1))
                    act.activation(pr[0:NQ, j % 2, i], ps[sbank(i, not project)][0:NQ, 0:NK], ACT.Exp, bias=nm[0:NQ, i:i + 1],
                                   scale=rqs[0:NQ, i:i + 1], accum_out=rs[0:NQ, i:i + 1]).then_inc(exp_done, 1)

                new_weights = isinstance(s, int) and s == B - 1 and j == 0
                if new_weights:
                    for n in range(4):
                        w2_split(n)
                if attend:
                    act.wait_ge(kt_done, u + 1)
                    act.activation(kT_hi[:], ps[BKT][:, 0:NKE], ACT.Copy).then_inc(kT_hi_done, 1)
                if new_weights:
                    for n in range(4, C):
                        w2_split(n)
                if attend and not project:
                    p_split(0)
                    if j == 0:
                        act.wait_ge(v_proj_done, 4 * STAGES)
                    chunk(0, 0, j, 0)
                    exps(0)
                    exps(1)
                    p_split(1)
                    exps(2)
                    p_split(2)
                    exps(3)
                    p_split(3)
                    chunk(0, 0, j, 1)
                if attend and project:
                    if prev:
                        p_split(0)
                        p_split(1)
                    if new_weights:
                        for n in range(C, C + 4):
                            w2_split(n)
                    exps(0)
                    if prev:
                        p_split(2)
                    if new_weights:
                        for n in range(C + 4, 2 * C):
                            w2_split(n)
                if project:
                    act.wait_ge(k_proj_done, v + 1)
                    if j == 0 and later(s, 1):
                        act.wait_ge(kn_done, 4 * s)
                    act.activation(k_raw[:, 1 - par, j], ps[BK][:, 0:KW], ACT.Copy).then_inc(k_raw_done, 1)
                    if later(v, 1):
                        act.wait_ge(ssk_done, v)
                    act.activation(ksq[:], ps[BK][:, 0:KW], ACT.Square, scale=float(HD) ** -0.5).then_inc(ksq_done, 1)
                if attend and project:
                    exps(1)
                    if prev:
                        p_split(3)
                    exps(2)
                    exps(3)
                if prev:
                    act.wait_ge(pv_done, u)
                    if later(u, 3):
                        act.wait_ge(ao_stored[1 - j % 2], 16 * (2 * s + (-1, 0, 0, 1)[j]))
                    act.activation(ao[:, 1 - j % 2], ps[BPV][:, 0:QW], ACT.Copy).then_inc(ao_done, 1)
                if splits(s, j):
                    kv_split(s + 1 if j == 0 else s + 2, (j + 3) % 4)
                if attend:
                    act.wait_ge(v_raw_done, 4 * s + 4)
                    if prev:
                        act.wait_ge(pv_done, u)
                    act.activation(v_hi[:], v_raw[:, par, :, j * HD:(j + 1) * HD], ACT.Copy).then_inc(v_hi_done, 1)
                    if j + 1 < GH or projects(s):
                        q_split(u + 1)
                if project:
                    act.wait_ge(v_proj_done, v + 1)
                    if j == 0 and later(s, 1):
                        act.wait_ge(v_lo_done, 4 * s)
                    act.activation(v_raw[:, 1 - par, j], ps[BV][:, 0:KW], ACT.Copy).then_inc(v_raw_done, 1)

            for j in range(KT):
                slot(-1, j, 1, 0, False, True)
            q_split(0)
            stages(act, lambda s, par, half: [slot(s, j, par, half, True, projects(s)) for j in range(GH)])
            last = 4 * STAGES - 1
            for t in range(KT):
                act.wait_ge(pt_done, 4 * last + t + 1)
                act.activation(pT_hi[0:ROWS[t], t], ps[ptbank(t, True)][0:ROWS[t], 0:QW], ACT.Copy).then_inc(pT_hi_done, 1)
                if t == 0:
                    chunk_weights(0, 1, 0, 0)
                if t == 1:
                    chunk_heads(0)

            def accumulators(th, nh):
                act.wait_ge(wo_used, 16 * th + 8 * nh + 8)
                for n in (2, 3):
                    act.activation(oT[th][:, 4 * nh + n], ps[n][:, 0:TW], ACT.Copy).then_inc(oT_act, 1)

            def turned_y(t):
                act.wait_ge(t2_done, t + 1)
                if t >= 2:
                    act.wait_ge(ae_done, t - 1)
                for n in range(2):
                    act.activation(yT[:, t % 2, 4 * n:4 * n + 4].rearrange("p c q -> p (c q)"), ps[experts_bank(t) + n][:, 0:4 * NQ],
                                   ACT.Copy).then_inc(yT_done, 1)

            def exps2(t):
                act.wait_ge(top_done, 2 * t + 2)
                if t >= 1:
                    act.wait_ge(gate_step, 5 * t)
                act.activation(ex[0:NQ], top[0:NQ, 0:2], ACT.Exp, bias=ntop[0:NQ]).then_inc(ex_done, 1)

            def turned_h(t):
                act.wait_ge(t3_done, t + 1)
                if t >= 1:
                    act.wait_ge(y2_done, t)
                act.activation(hwT[:], ps[experts_bank(t) + 1][:, 0:NQ], ACT.Copy).then_inc(hwT_done, 1)

            accumulators(0, 0)
            act.wait_ge(pv_done, last + 1)
            act.wait_ge(ao_stored[1], 16 * (2 * STAGES - 1))
            act.activation(ao[:, 1], ps[BPV][:, 0:QW], ACT.Copy).then_inc(ao_done, 1)
            chunk(0, 1, 0, 1)
            with act.Fori(1, G // 2) as gp:
                chunk(0, 1, gp, 0)
                chunk(0, 1, gp, 1)
            chunk(1, 0, 0, 0)
            accumulators(0, 1)
            for c in range(2 * G):
                t, n = c // 4, c + 1
                if c % 4 == 0 and t:
                    turned_h(t - 1)
                if n < 2 * G:
                    chunk_weights(1, n // G, n % G // 2, n % 2)
                if c % 4 == 3:
                    exps2(t)
                if n < 2 * G:
                    chunk_heads(n % 2)
                if c % 4 == 2:
                    turned_y(t)
                if c % G == G - 1:
                    accumulators(1, c // G)
            turned_h(TB - 1)
            a, b, c, d = range(TB, B)
            for step, t in ((turned_y, a), (exps2, a), (turned_y, b), (turned_h, a), (exps2, b), (turned_h, b),
                            (turned_y, c), (exps2, c), (turned_y, d), (turned_h, c), (exps2, d), (turned_h, d)):
                step(t)

        @block.vector
        def _(dve):
            dve.wait_ge(consts_in, 32)
            dve.scalar_tensor_tensor(out=wqk[:], in0=qkw[:, 0:1], scalar=float(HD) ** -0.5, in1=qkw[:, 1:2],
                                     op0=ALU.mult, op1=ALU.mult).then_inc(wqk_done, 1)
            dve.wait_ge(tanh_done, 1)
            dve.tensor_scalar(cffn[:], gates_t[:, 1:2], SCALING, None, ALU.mult).then_inc(cffn_done, 1)

            def wq_split(k, h):
                dve.wait_ge(wq_hi_done, h + 1)
                dve.tensor_tensor(wq_lo[:, k], wq_raw[:, k], wq_hi[:, k], ALU.subtract).then_inc(wq_lo_done, 1)

            def stats(b):
                dve.wait_ge(x_in[b], 16)
                for n in range(2):
                    dve.bn_stats(bn6[0:NQ, b % 2, n], xa[0:NQ, b, n * 512:(n + 1) * 512]).then_inc(stats_done, 1)
                dve.wait_ge(stats_done, 2 * b + 2)
                dve.bn_aggr(mv[0:NQ, b], bn6[0:NQ, b % 2]).then_inc(aggr_done, 1)

            dve.memset(pick[:].bitcast(U32), 0).then_inc(pick_zero, 1)
            dve.wait_ge(pick_zero, 1)
            dve.memset(pick[:, R - 1:R].bitcast(U32), 0x3F800000).then_inc(pick_done, 1)

            for t in range(KT):
                dve.memset(kv_hi[:, t, :, ROWS[t]:P].bitcast(U32), 0)
                ins = dve.memset(kv_lo[:, t, :, ROWS[t]:P].bitcast(U32), 0)
            ins.then_inc(pad_done, 1)

            def latent_split(b):
                dve.wait_ge(xt_hi_done, b + 1)
                dve.tensor_tensor(xT_lo[:, :, b * NQ:(b + 1) * NQ], xT_raw[:, b], xT_hi[:, :, b * NQ:(b + 1) * NQ],
                                  ALU.subtract).then_inc(xt_lo_done, 1)

            stats(0)
            for b in range(B):
                if b + 1 < B:
                    stats(b + 1)
                dve.wait_ge(aggr_done, b + 1)
                dve.wait_ge(rstd_done, b + 1)
                dve.tensor_scalar(xa[0:NQ, b], xa[0:NQ, b], mv[0:NQ, b, 0:1], rstd[0:NQ, b, 1:2],
                                  ALU.subtract, ALU.mult).then_inc(xn_done, 1)
                if b in (4, 5):
                    wq_split(b - 4, b - 4)
                if b >= 1:
                    latent_split(b - 1)
            latent_split(B - 1)

            def w_split(c):
                dve.wait_ge(w_hi_done, c + 1)
                dve.tensor_tensor(w_lo[:, c], wstage(c), w_hi[:, c], ALU.subtract).then_inc(w_lo_done, 1)

            def w2_split(n):
                dve.wait_ge(w_hi_done, C + n + 1)
                cols = slice(n // C * KW, (n // C + 1) * KW)
                dve.tensor_tensor(w_lo[:, n % C, cols], w_raw[:, n % 4], w_hi[:, n % C, cols], ALU.subtract).then_inc(w_lo_done, 1)

            def copy_sums(n):
                dve.wait_ge(ss_done, 2 * R * n)
                for th in range(TH):
                    dve.tensor_scalar(ssT[:, th * TW:(th + 1) * TW], ps[4 + th][:, 0:TW], 1.0, None,
                                      ALU.mult).then_inc(ssT_done, 1)

            def mean_squares(n):
                dve.wait_ge(sst_turned, n)
                for th in range(TH):
                    dve.tensor_scalar(ms[0:NQ, TB * R * th:TB * R * (th + 1)].rearrange("p (b i) -> p b i", b=TB),
                                      ps[6 + th][0:NQ, :].rearrange("p (b i) -> p b i", b=TB)[:, :, 0:R],
                                      1.0 / HD, RMS_EPS, ALU.mult, ALU.add).then_inc(ms_done, 1)

            def keep_rms(n):
                dve.wait_ge(rqt_done, n)
                dst = rq[0:NQ, n - 1] if isinstance(n, int) else rq[0:NQ, bass.ds(n - 1, 1)].rearrange("p o b -> p (o b)")
                dve.tensor_scalar(dst, rqt[0:NQ], 1.0, None, ALU.mult).then_inc(rq_done, 1)

            def queries(g):
                for i in range(R):
                    h = 4 * g + i
                    for th in range(TH):
                        dve.wait_ge(sq_hi_done, 2 * h + th + 1)
                        dve.tensor_tensor(sq_lo[:, th], sq[:], sq_hi[:], ALU.subtract).then_inc(sq_lo_done, 1)
                        if not later(h, 1) and th == 0:
                            dve.wait_ge(wqk_done, 1)
                        if i == 0 and th == 0 and later(g, 1):
                            copy_sums(g)
                            dve.wait_ge(qo_stored, 16 * g)
                        dve.tensor_scalar(qo[:, TB * th:TB * th + TB, i],
                                          ps[2 * (i % 2) + th][:, 0:TW].rearrange("p (b q) -> p b q", b=TB),
                                          wqk[:], None, ALU.mult).then_inc(qo_done, 1)
                        if i == 2 and th == 0 and later(g, 1):
                            mean_squares(g)
                        if i == 3 and th == 1 and later(g, 1):
                            keep_rms(g)
                    if not isinstance(g, int) or h + 2 < H:
                        wq_split(i % 2, h + 2)
                    if isinstance(g, int) and g == 0:
                        w_split(2 * i)
                        w_split(2 * i + 1)

            def kv_split(w, t):
                dve.wait_ge(kv_hi_done, w + 1)
                dve.tensor_tensor(kv_lo[:, t, :, 0:ROWS[t]], raw_tile(t), kv_hi[:, t, :, 0:ROWS[t]],
                                  ALU.subtract).then_inc(kv_lo_done, 1)

            queries(0)
            with dve.Fori(1, G - 1) as g:
                queries(g)
            kv_split(0, 0)
            queries(G - 1)
            kv_split(1, 1)
            kv_split(2, 2)
            copy_sums(G)

            def normalise_keys(s, j, par):
                u = 4 * s + j
                dve.wait_ge(rk_done, 4 * s + 4)
                dve.wait_ge(k_raw_done, 4 * s + 4)
                if later(u, 1):
                    dve.wait_ge(kt_done, u)
                dve.tensor_tensor(k_n[:], k_raw[:, par, :, j * HD:(j + 1) * HD],
                                  rk[:, par, :, j:j + 1].to_broadcast([P, KT, HD]), ALU.mult).then_inc(kn_done, 1)

            def q_split(u):
                dve.wait_ge(q_hi_done, u + 1)
                dve.tensor_tensor(q_lo[:], q_raw[:], q_hi[:], ALU.subtract).then_inc(q_lo_done, 1)

            def query_scales(s, j, half):
                u = 4 * s + j
                if later(u, 1):
                    dve.wait_ge(exp_done, 4 * u)
                elif isinstance(u, int):
                    dve.wait_ge(rq_done, G)
                if isinstance(s, int):
                    src = rq[0:NQ, half * GH + j, R * (s % B):R * (s % B) + R]
                else:
                    src = rq[0:NQ, half * GH + j, bass.ds(R * (s - B * half), R)]
                dve.tensor_scalar(rqs[0:NQ], src, 1.0, None, ALU.mult).then_inc(rqs_done, 1)
                dve.tensor_scalar(nrq[0:NQ], src, -1.0, None, ALU.mult).then_inc(nrq_done, 1)

            def chunk_weights(th, nh, gp, k):
                m = 16 * th + 8 * nh + 2 * gp + k
                dve.wait_ge(wo_hi_done, 2 * m + 1)
                dve.tensor_tensor(wo_lo[:, k], wo_raw[k][:], wo_hi[:, k], ALU.subtract).then_inc(wo_lo_done, 1)

            def chunk_heads(th, nh, gp, k):
                m = 16 * th + 8 * nh + 2 * gp + k
                dve.wait_ge(wo_hi_done, 2 * m + 2)
                dve.tensor_tensor(at_lo[:, k], at_raw[k][:], at_hi[:, k], ALU.subtract).then_inc(wo_lo_done, 1)

            def chunk(th, nh, gp, k):
                chunk_weights(th, nh, gp, k)
                chunk_heads(th, nh, gp, k)

            def slot(s, j, par, half, attend, project):
                u, v, w = 4 * s + j, 4 * s + 4 + j, 4 * s + 7 + j
                prev = attend and later(u, 1)

                def p_split(t):
                    dve.wait_ge(pT_hi_done, 4 * (u - 1) + t + 1)
                    dve.tensor_tensor(pT_lo[0:ROWS[t], t], ps[ptbank(t, not project)][0:ROWS[t], 0:QW],
                                      pT_hi[0:ROWS[t], t], ALU.subtract).then_inc(pT_lo_done, 1)

                def maxima(i):
                    a = 4 * u + i
                    dve.wait_ge(s_done, a + 1)
                    dve.tensor_reduce(mx[0:NQ, i:i + 1], ps[sbank(i, not project)][0:NQ, 0:NK], AX.X, ALU.max).then_inc(mx_done, 1)
                    if i == 0:
                        dve.wait_ge(nrq_done, u + 1)
                        dve.wait_ge(rqs_done, u + 1)
                    dve.wait_ge(mx_done, a + 1)
                    dve.tensor_tensor(nm[0:NQ, i:i + 1], mx[0:NQ, i:i + 1], nrq[0:NQ, i:i + 1], ALU.mult).then_inc(nm_done, 1)

                def scale(i):
                    a = 4 * u + i
                    dve.wait_ge(exp_done, a + 1)
                    dve.reciprocal(rr[0:NQ, i:i + 1], rs[0:NQ, i:i + 1]).then_inc(rr_done, 1)
                    dve.wait_ge(rr_done, a + 1)
                    dve.tensor_scalar(pr[0:NQ, j % 2, i], pr[0:NQ, j % 2, i], rr[0:NQ, i:i + 1], None,
                                      ALU.mult).then_inc(p_done, 1)

                new_weights = isinstance(s, int) and s == B - 1 and j == 0
                if new_weights:
                    for n in range(4):
                        w2_split(n)
                if attend:
                    query_scales(s, j, half)
                    dve.wait_ge(kT_hi_done, u + 1)
                    dve.tensor_tensor(kT_lo[:], ps[BKT][:, 0:NKE], kT_hi[:], ALU.subtract).then_inc(kT_lo_done, 1)
                if new_weights:
                    for n in range(4, C):
                        w2_split(n)
                if attend and not project:
                    p_split(0)
                    chunk(0, 0, j, 0)
                    maxima(0)
                    if j + 1 < GH:
                        normalise_keys(s, j + 1, par)
                    maxima(1)
                    p_split(1)
                    scale(0)
                    maxima(2)
                    p_split(2)
                    scale(1)
                    maxima(3)
                    p_split(3)
                    scale(2)
                    scale(3)
                    chunk(0, 0, j, 1)
                if attend and project:
                    if prev:
                        p_split(0)
                    if j + 1 < GH:
                        normalise_keys(s, j + 1, par)
                    if prev:
                        p_split(1)
                    if new_weights:
                        for n in range(C, C + 4):
                            w2_split(n)
                    maxima(0)
                    if prev:
                        p_split(2)
                    if new_weights:
                        for n in range(C + 4, 2 * C):
                            w2_split(n)
                    maxima(1)
                    scale(0)
                    if prev:
                        p_split(3)
                if project:
                    dve.wait_ge(ksq_done, v + 1)
                    if later(v, 4):
                        dve.wait_ge(msk_done, v - 3)
                    dve.tensor_reduce(ssk[:, j], ksq[:].rearrange("p (g d) -> p g d", g=GH), AX.X, ALU.add).then_inc(ssk_done, 1)
                if attend and project:
                    maxima(2)
                    scale(1)
                    maxima(3)
                    if j + 1 == GH:
                        normalise_keys(s + 1, 0, 1 - par)
                    scale(2)
                    scale(3)
                if splits(s, j):
                    kv_split(w, (j + 3) % 4)
                if attend:
                    dve.wait_ge(v_hi_done, u + 1)
                    dve.tensor_tensor(v_lo[:], v_raw[:, par, :, j * HD:(j + 1) * HD], v_hi[:], ALU.subtract).then_inc(v_lo_done, 1)
                    if j + 1 < GH or projects(s):
                        q_split(u + 1)

            for j in range(KT):
                slot(-1, j, 1, 0, False, True)
                if j == 0:
                    mean_squares(G)
                if j == 2:
                    keep_rms(G)
            q_split(0)
            normalise_keys(0, 0, 0)
            stages(dve, lambda s, par, half: [slot(s, j, par, half, True, projects(s)) for j in range(GH)])
            last = 4 * STAGES - 1
            for t in range(KT):
                dve.wait_ge(pT_hi_done, 4 * last + t + 1)
                dve.tensor_tensor(pT_lo[0:ROWS[t], t], ps[ptbank(t, True)][0:ROWS[t], 0:QW], pT_hi[0:ROWS[t], t],
                                  ALU.subtract).then_inc(pT_lo_done, 1)
                if t == 0:
                    chunk_weights(0, 1, 0, 0)
                if t == 1:
                    chunk_heads(0, 1, 0, 0)

            def accumulators(th, nh):
                dve.wait_ge(wo_used, 16 * th + 8 * nh + 8)
                for n in (0, 1):
                    dve.tensor_copy(oT[th][:, 4 * nh + n], ps[n][:, 0:TW]).then_inc(oT_dve, 1)

            def residual(t):
                dve.wait_ge(t1_done, t + 1)
                dve.wait_ge(xr_in[t % 2], 16 * (t // 2 + 1))
                if t >= 3:
                    dve.wait_ge(x2_done, 2 * (t - 3) + 2)
                for n in range(2):
                    dve.scalar_tensor_tensor(out=x1[0:NQ, t % 3, n * 512:(n + 1) * 512], in0=ps[out_bank(t) + n][0:NQ, :],
                                             scalar=gates_t[0:NQ, 0:1], in1=xr[0:NQ, t % 2, n * 512:(n + 1) * 512],
                                             op0=ALU.mult, op1=ALU.add).then_inc(x1_done, 1)
                for n in range(2):
                    dve.wait_ge(x1_done, 2 * t + n + 1)
                    dve.bn_stats(bn6[0:NQ, t % 2, n], x1[0:NQ, t % 3, n * 512:(n + 1) * 512]).then_inc(st2_done, 1)
                dve.wait_ge(st2_done, 2 * t + 2)
                dve.bn_aggr(mv[0:NQ, t], bn6[0:NQ, t % 2]).then_inc(ag2_done, 1)

            def norm(t):
                dve.wait_ge(rs2_done, t + 1)
                dve.wait_ge(ag2_done, t + 1)
                if t >= 2:
                    dve.wait_ge(t2_done, t - 1)
                dve.tensor_scalar(y[0:NQ, t % 2], x1[0:NQ, t % 3], mv[0:NQ, t, 0:1], mv2[0:NQ, t, 1:2],
                                  ALU.subtract, ALU.mult).then_inc(y_done, 1)

            def route_top(t):
                dve.wait_ge(ae_done, t + 1)
                dve.tensor_tensor(lg[0:NQ], ps[experts_bank(t)][0:NQ, ER:AE], rowc[0:NQ, 2:2 + E], ALU.add).then_inc(lg_done, 1)
                dve.wait_ge(lg_done, t + 1)
                dve.max(top[0:NQ], lg[0:NQ]).then_inc(top_done, 1)
                dve.wait_ge(top_done, 2 * t + 1)
                dve.max_index(topi[0:NQ], top[0:NQ], lg[0:NQ]).then_inc(topi_done, 1)
                dve.tensor_scalar(ntop[0:NQ], top[0:NQ, 0:1], -1.0, None, ALU.mult).then_inc(top_done, 1)
                dve.wait_ge(topi_done, t + 1)
                dve.tensor_copy(topf[0:NQ], topi[0:NQ, 0:2]).then_inc(topf_done, 1)

            def route_gates(t):
                dve.wait_ge(ex_done, t + 1)
                dve.tensor_reduce(exs[0:NQ], ex[0:NQ], AX.X, ALU.add).then_inc(gate_step, 1)
                dve.wait_ge(gate_step, 5 * t + 1)
                dve.reciprocal(exr[0:NQ], exs[0:NQ]).then_inc(gate_step, 1)
                dve.wait_ge(gate_step, 5 * t + 2)
                dve.tensor_scalar(gt[0:NQ], ex[0:NQ], exr[0:NQ], None, ALU.mult).then_inc(gate_step, 1)
                dve.wait_ge(gate_step, 5 * t + 3)
                dve.wait_ge(topf_done, t + 1)
                dve.tensor_scalar(wa[0:NQ], rowc[0:NQ, 2 + E:2 + 2 * E], topf[0:NQ, 0:1], gt[0:NQ, 0:1],
                                  ALU.is_equal, ALU.mult).then_inc(gate_step, 1)
                dve.tensor_scalar(wb[0:NQ], rowc[0:NQ, 2 + E:2 + 2 * E], topf[0:NQ, 1:2], gt[0:NQ, 1:2],
                                  ALU.is_equal, ALU.mult).then_inc(gate_step, 1)
                dve.wait_ge(gate_step, 5 * t + 5)
                dve.tensor_tensor(we[0:NQ], wa[0:NQ], wb[0:NQ], ALU.add).then_inc(wsum_done, 1)
                dve.wait_ge(wsum_done, t + 1)
                if t >= 1:
                    dve.wait_ge(t3_done, t)
                dve.tensor_tensor(hw[0:NQ].rearrange("p (e r) -> p e r", e=E),
                                  ps[experts_bank(t)][0:NQ, 0:ER].rearrange("p (e r) -> p e r", e=E),
                                  we[0:NQ].rearrange("p (e o) -> p e o", o=1).to_broadcast([NQ, E, ER // E]),
                                  ALU.mult).then_inc(hw_done, 1)

            def final(t):
                dve.wait_ge(y2_done, t + 1)
                if t == 0:
                    dve.wait_ge(cffn_done, 1)
                if t >= 2:
                    dve.wait_ge(x2_stored[t % 2], 16 * (t // 2))
                for n in range(2):
                    dve.scalar_tensor_tensor(out=x2[0:NQ, t % 2, n * 512:(n + 1) * 512], in0=ps[experts_bank(t) + n][0:NQ, :],
                                             scalar=cffn[0:NQ], in1=x1[0:NQ, t % 3, n * 512:(n + 1) * 512],
                                             op0=ALU.mult, op1=ALU.add).then_inc(x2_done, 1)

            accumulators(0, 0)
            chunk(0, 1, 0, 1)
            with dve.Fori(1, G // 2) as gp:
                chunk(0, 1, gp, 0)
                chunk(0, 1, gp, 1)
            chunk(1, 0, 0, 0)
            accumulators(0, 1)
            for c in range(2 * G):
                t, n = c // 4, c + 1
                where = (1, n // G, n % G // 2, n % 2)
                if c % 4 == 1:
                    residual(t)
                if c % 4 == 3:
                    route_top(t)
                if n < 2 * G:
                    chunk_weights(*where)
                if c % 4 == 1:
                    norm(t)
                if c % 4 == 3:
                    route_gates(t)
                if n < 2 * G:
                    chunk_heads(*where)
                if c % 4 == 0 and t:
                    final(t - 1)
                if c % G == G - 1:
                    accumulators(1, c // G)
            def route(t):
                route_top(t)
                route_gates(t)

            a, b, c, d = range(TB, B)
            for step, t in ((residual, a), (final, a - 1), (norm, a), (residual, b), (route_top, a), (norm, b),
                            (route_gates, a), (residual, c), (route, b), (norm, c), (final, a), (residual, d),
                            (final, b), (norm, d), (route, c), (route, d), (final, c), (final, d)):
                step(t)


def kernel(x, ctx_4096, g_xattn, g_ffn, L0_xattn_Wq, L0_xattn_Wk, L0_xattn_Wv, L0_xattn_Wo,
           L0_xattn_q_norm_w, L0_xattn_k_norm_w, L0_ffn_router_w, L0_ffn_router_b, L0_ffn_A, L0_ffn_Bm):
    import concourse.bacc as bacc
    from concourse.bass_utils import run_bass_kernel_spmd

    a = np.asarray
    ctxT = a(ctx_4096).transpose(0, 2, 1).reshape(B, C, P, NC).transpose(0, 2, 1, 3)
    arrays = {
        "x": a(x),
        "ctxT": np.concatenate([ctxT[..., OFF[t]:OFF[t] + ROWS[t]].reshape(B, P, C * ROWS[t]) for t in range(KT - 1)],
                               axis=-1),
        "Wq": a(L0_xattn_Wq).reshape(C, P, H, HD).transpose(2, 1, 0, 3),
        "Wkv": np.concatenate([a(w).reshape(C, P, HALVES, KW).transpose(2, 1, 0, 3)
                               for w in (L0_xattn_Wk, L0_xattn_Wv)], axis=-1),
        "Wo": a(L0_xattn_Wo).reshape(G, R, HD, 2, 512).transpose(3, 0, 2, 1, 4),
        "AR": np.concatenate([a(L0_ffn_A).reshape(ER, D), a(L0_ffn_router_w)], axis=0)
                .T.reshape(C, P, AE).transpose(1, 0, 2),
        "BmT": a(L0_ffn_Bm).transpose(0, 2, 1).reshape(ER, D),
        "vecs": np.stack([a(L0_xattn_q_norm_w), a(L0_xattn_k_norm_w)], axis=1),
        "rows": np.broadcast_to(np.concatenate([a(g_xattn), a(g_ffn), a(L0_ffn_router_b),
                                                np.arange(E, dtype=np.float32)]), (P, 2 + 2 * E)),
    }
    arrays = {k: np.ascontiguousarray(v) for k, v in arrays.items()}
    nc = bacc.Bacc("TRN2", target_bir_lowering=False, num_devices=1)
    args = [nc.dram_tensor(k, v.shape, mybir.dt.from_np(v.dtype), kind="ExternalInput").ap() for k, v in arrays.items()]
    out = nc.dram_tensor("out", (B, NQ, D), F32, kind="ExternalOutput").ap()
    build(nc, *args, out)
    return run_bass_kernel_spmd(nc, [arrays], core_ids=[0]).results[0]["out"]
```
